# Optimizing a Trainium2 kernel written in Bass

```python
import numpy as np
import jax
import jax.numpy as jnp

def _softmax(x, axis=-1):
    return jax.nn.softmax(x, axis=axis)

def _gelu(x):
    return jax.nn.gelu(x, approximate=True)

def _silu(x):
    return jax.nn.silu(x)

def _sigmoid(x):
    return jax.nn.sigmoid(x)

def _layernorm(x, axis=-1, eps=1e-05):
    m = jnp.mean(x, axis=axis, keepdims=True)
    v = jnp.var(x, axis=axis, keepdims=True)
    return (x - m) / jnp.sqrt(v + eps)

def _scatter_add(tgt, idx, src, axis=0):
    return tgt.at[idx].add(src)

def _segment_sum(src, seg, n):
    return jax.ops.segment_sum(src, seg, n)
kernel_name = 'mk_perceiver_d4_seqx_r4_8d9d63'

def setup_inputs(seed: int=0):
    np.random.seed(seed)
    _w = jnp.asarray

    def _rec_inputs():
        import jax
        import jax.numpy as jnp
        _rk = jax.random.key(seed)
        x = -0.0002928 + 1 * jax.random.normal(jax.random.fold_in(_rk, 1), (16, 64, 256), jnp.float32)
        _lenS = 64 - jax.random.randint(jax.random.fold_in(_rk, 7), (16,), 0, max(1, 64 // 4) + 1, jnp.int32)
        _lenS2 = 1601 - jax.random.randint(jax.random.fold_in(_rk, 8), (16,), 0, max(1, 1601 // 4) + 1, jnp.int32)
        _ctx_1024P = jax.random.normal(jax.random.fold_in(_rk, 11), (16, 16, 256), jnp.float32)
        _ctx_1024c = jax.random.dirichlet(jax.random.fold_in(_rk, 511), 0.3 * jnp.ones((16,), jnp.float32), (16, 1601))
        _ctx_1024t = jnp.einsum('bsk,bkd->bsd', _ctx_1024c, _ctx_1024P)
        _ctx_1024t = _ctx_1024t * jax.lax.rsqrt(jnp.mean(jnp.square(_ctx_1024t)) + 1e-12) * 0.953939
        ctx_1024 = -0.000191848 + 0.999787 * (_ctx_1024t + 0.3 * jax.random.normal(jax.random.fold_in(_rk, 611), (16, 1601, 256), jnp.float32))
        _validS = jnp.arange(64)[None, :] < _lenS[:, None]
        _validS2 = jnp.arange(1601)[None, :] < _lenS2[:, None]
        _causal = jnp.tril(jnp.ones((64, 64), dtype=bool))
        mask_Bx1x1xS2_fk0 = jnp.where(jnp.broadcast_to(_validS2[:, None, None, :], (16, 1, 1, 1601)), 0.0, 1.0).astype(jnp.float32)
        mask_BxS2_ik0 = jnp.where(jnp.broadcast_to(_validS2[:, :], (16, 1601)), 0, 1).astype(jnp.int32)
        return (x, ctx_1024, mask_Bx1x1xS2_fk0, mask_BxS2_ik0)
    x, ctx_1024, mask_Bx1x1xS2_fk0, mask_BxS2_ik0 = _rec_inputs()

    def _L0_xattn_setup():
        import jax, jax.numpy as jnp
        import numpy as np
        D_MODEL = 256
        NUM_HEADS = 16
        DEPTH = D_MODEL // NUM_HEADS
        key = jax.random.key(seed)
        ks = jax.random.split(key, 10)
        B, T, C = (2, 512, 768)
        s = 1.0 / np.sqrt(D_MODEL)
        inp = {'x': jax.random.normal(ks[0], (B, T, D_MODEL), dtype=jnp.float32), 'context': jax.random.normal(ks[1], (B, C, D_MODEL), dtype=jnp.float32), 'Wq': jax.random.normal(ks[2], (D_MODEL, D_MODEL), dtype=jnp.float32) * s, 'bq': jnp.zeros((D_MODEL,), dtype=jnp.float32), 'Wk': jax.random.normal(ks[3], (D_MODEL, D_MODEL), dtype=jnp.float32) * s, 'bk': jnp.zeros((D_MODEL,), dtype=jnp.float32), 'Wv': jax.random.normal(ks[4], (D_MODEL, D_MODEL), dtype=jnp.float32) * s, 'bv': jnp.zeros((D_MODEL,), dtype=jnp.float32), 'Wo': jax.random.normal(ks[5], (D_MODEL, D_MODEL), dtype=jnp.float32) * s, 'bo': jnp.zeros((D_MODEL,), dtype=jnp.float32)}
        return inp
    _L0_xattn_all = _L0_xattn_setup()
    _L0_xattn_in = {k: v for k, v in _L0_xattn_all.items() if k in ('Wq', 'bq', 'Wk', 'bk', 'Wv', 'bv', 'Wo', 'bo')}
    del _L0_xattn_all

    def _L0_attn_setup():
        import jax, jax.numpy as jnp
        import numpy as np
        import math
        DIM = 256
        NUM_HEADS = 16
        HEAD_DIM = DIM // NUM_HEADS
        MAX_BIAS = 8.0
        SCALE = HEAD_DIM ** (-0.5)

        def _alibi_slopes(n):

            def pow2(n):
                start = 2.0 ** (-2.0 ** (-(math.log2(n) - 3)))
                return [start * start ** i for i in range(n)]
            if math.log2(n).is_integer():
                return pow2(n)
            c = 2 ** math.floor(math.log2(n))
            return pow2(c) + _alibi_slopes(2 * c)[0::2][:n - c]

        def _rotate_half(t):
            t1, t2 = jnp.split(t, 2, axis=-1)
            return jnp.concatenate([-t2, t1], axis=-1)
        key = jax.random.key(seed)
        k1, k2, k3, k4 = jax.random.split(key, 4)
        B, N, C = (2, 512, DIM)
        x = jax.random.normal(k1, (B, N, C), dtype=jnp.float32)
        qkv_w = jax.random.normal(k2, (3 * C, C), dtype=jnp.float32) * C ** (-0.5)
        proj_w = jax.random.normal(k3, (C, C), dtype=jnp.float32) * C ** (-0.5)
        proj_b = jax.random.normal(k4, (C,), dtype=jnp.float32) * 0.01
        slopes = jnp.asarray(np.array(_alibi_slopes(NUM_HEADS), dtype=np.float32))
        return {'x': x, 'qkv_w': qkv_w, 'proj_w': proj_w, 'proj_b': proj_b, 'slopes': slopes}
    _L0_attn_all = _L0_attn_setup()
    _L0_attn_in = {k: v for k, v in _L0_attn_all.items() if k in ('qkv_w', 'proj_w', 'proj_b', 'slopes')}
    del _L0_attn_all

    def _L0_ffn_setup():
        import jax, jax.numpy as jnp
        import numpy as np
        H = 256
        I = 176
        E = 64
        TOP_K = 8
        NG = 8
        TOPK_GROUP = 4
        N_SHARED = 2
        ROUTED_SCALE = 2.5
        S_I = I * N_SHARED

        def _route(x, gate_w, gate_bias):
            T = x.shape[0]
            logits = x @ gate_w.T
            scores = jax.nn.sigmoid(logits)
            scores_for_choice = scores + gate_bias[None, :]
            grp = scores_for_choice.reshape(T, NG, E // NG)
            group_scores = jnp.sum(jax.lax.top_k(grp, 2)[0], axis=-1)
            _, gidx = jax.lax.top_k(group_scores, TOPK_GROUP)
            gmask = jnp.zeros((T, NG), dtype=scores.dtype).at[jnp.arange(T)[:, None], gidx].set(1.0)
            emask = jnp.repeat(gmask, E // NG, axis=1)
            masked = jnp.where(emask > 0, scores_for_choice, 0.0)
            _, topk_idx = jax.lax.top_k(masked, TOP_K)
            topk_w = jnp.take_along_axis(scores, topk_idx, axis=1)
            topk_w = topk_w / (jnp.sum(topk_w, axis=-1, keepdims=True) + 1e-20)
            topk_w = topk_w * ROUTED_SCALE
            rw = jnp.zeros((T, E), dtype=scores.dtype).at[jnp.arange(T)[:, None], topk_idx].add(topk_w)
            return rw

        def _mlp(x, gw, uw, dw):
            return jax.nn.silu(x @ gw.T) * (x @ uw.T) @ dw.T
        key = jax.random.key(seed)
        ks = jax.random.split(key, 10)
        sc = 0.02
        return {'hidden_states': jax.random.normal(ks[0], (1, 256, H), dtype=jnp.float32), 'gate_w': sc * jax.random.normal(ks[1], (E, H), dtype=jnp.float32), 'gate_bias': sc * jax.random.normal(ks[2], (E,), dtype=jnp.float32), 'Wg': sc * jax.random.normal(ks[3], (E, I, H), dtype=jnp.float32), 'Wu': sc * jax.random.normal(ks[4], (E, I, H), dtype=jnp.float32), 'Wd': sc * jax.random.normal(ks[5], (E, H, I), dtype=jnp.float32), 'Sg': sc * jax.random.normal(ks[6], (S_I, H), dtype=jnp.float32), 'Su': sc * jax.random.normal(ks[7], (S_I, H), dtype=jnp.float32), 'Sd': sc * jax.random.normal(ks[8], (H, S_I), dtype=jnp.float32)}
    _L0_ffn_all = _L0_ffn_setup()
    _L0_ffn_in = {k: v for k, v in _L0_ffn_all.items() if k in ('gate_w', 'gate_bias', 'Wg', 'Wu', 'Wd', 'Sg', 'Su', 'Sd')}
    del _L0_ffn_all

    def _L1_xattn_setup():
        import jax, jax.numpy as jnp
        import numpy as np
        B, S, D, H = (2, 512, 256, 16)
        DH = D // H

        def _split_heads(x):
            b, s, _ = x.shape
            return x.reshape(b, s, H, DH).transpose(0, 2, 1, 3)
        key = jax.random.key(seed)
        ks = jax.random.split(key, 8)
        scale = 0.02
        return {'query': jax.random.normal(ks[0], (B, S, D), jnp.float32), 'key': jax.random.normal(ks[1], (B, S, D), jnp.float32), 'value': jax.random.normal(ks[2], (B, S, D), jnp.float32), 'mask': jax.random.randint(ks[3], (B, 1, 1, S), 0, 2).astype(jnp.float32), 'Wq': jax.random.normal(ks[4], (D, D), jnp.float32) * scale, 'bq': jnp.zeros((D,), jnp.float32), 'Wk': jax.random.normal(ks[5], (D, D), jnp.float32) * scale, 'bk': jnp.zeros((D,), jnp.float32), 'Wv': jax.random.normal(ks[6], (D, D), jnp.float32) * scale, 'bv': jnp.zeros((D,), jnp.float32), 'Wo': jax.random.normal(ks[7], (D, D), jnp.float32) * scale, 'bo': jnp.zeros((D,), jnp.float32)}
    _L1_xattn_all = _L1_xattn_setup()
    _L1_xattn_in = {k: v for k, v in _L1_xattn_all.items() if k in ('Wq', 'bq', 'Wk', 'bk', 'Wv', 'bv', 'Wo', 'bo')}
    del _L1_xattn_all

    def _L1_attn_setup():
        import jax, jax.numpy as jnp
        import numpy as np
        B, T, D_MODEL = (2, 512, 256)
        N_HEADS, HEAD_DIM = (16, 64)
        ROPE_BASE = 10000.0

        def rotate_half(x):
            half = x.shape[-1] // 2
            x1, x2 = (x[..., :half], x[..., half:])
            return jnp.concatenate([-x2, x1], axis=-1)
        key = jax.random.key(seed)
        ks = jax.random.split(key, 5)
        scale = 0.02
        return {'x': jax.random.normal(ks[0], (B, T, D_MODEL), dtype=jnp.float32), 'Wq': jax.random.normal(ks[1], (D_MODEL, N_HEADS * HEAD_DIM), dtype=jnp.float32) * scale, 'Wk': jax.random.normal(ks[2], (D_MODEL, N_HEADS * HEAD_DIM), dtype=jnp.float32) * scale, 'Wv': jax.random.normal(ks[3], (D_MODEL, N_HEADS * HEAD_DIM), dtype=jnp.float32) * scale, 'Wo': jax.random.normal(ks[4], (N_HEADS * HEAD_DIM, D_MODEL), dtype=jnp.float32) * scale}
    _L1_attn_all = _L1_attn_setup()
    _L1_attn_in = {k: v for k, v in _L1_attn_all.items() if k in ('Wq', 'Wk', 'Wv', 'Wo')}
    del _L1_attn_all

    def _L1_ffn_setup():
        import jax, jax.numpy as jnp
        import numpy as np

        def _bitlinear(x, w_latent):
            scale = jax.lax.stop_gradient(jnp.clip(jnp.mean(jnp.abs(w_latent), axis=1, keepdims=True), 1e-05, None))
            tern = jnp.clip(jnp.round(w_latent / scale), -1.0, 1.0)
            w = w_latent + jax.lax.stop_gradient(tern - w_latent)
            return x @ (w * scale).T
        key = jax.random.key(seed)
        ks = jax.random.split(key, 6)
        dim, hidden, rank = (256, 1024, 16)
        B, S = (4, 1024)
        x = jax.random.normal(ks[0], (B, S, dim), dtype=jnp.float32)
        w_fc = 0.02 * jax.random.normal(ks[1], (hidden, dim), dtype=jnp.float32)
        w_proj = 0.02 * jax.random.normal(ks[2], (dim, hidden), dtype=jnp.float32)
        u = 0.02 * jax.random.normal(ks[3], (hidden, rank), dtype=jnp.float32)
        v = 0.02 * jax.random.normal(ks[4], (rank, dim), dtype=jnp.float32)
        fast_b = jax.random.normal(ks[5], (rank, rank), dtype=jnp.float32)
        gate = jnp.float32(0.05)
        return {'x': x, 'fast_b': fast_b, 'w_fc': w_fc, 'w_proj': w_proj, 'u': u, 'v': v, 'gate': gate}
    _L1_ffn_all = _L1_ffn_setup()
    _L1_ffn_in = {k: v for k, v in _L1_ffn_all.items() if k in ('fast_b', 'w_fc', 'w_proj', 'u', 'v', 'gate')}
    del _L1_ffn_all

    def _L2_xattn_setup():
        import jax, jax.numpy as jnp
        import numpy as np
        D_MODEL = 256
        N_HEADS = 16
        D_HEAD = D_MODEL // N_HEADS
        key = jax.random.key(seed)
        ks = jax.random.split(key, 11)
        B, T = (2, 512)
        s = 1.0 / np.sqrt(D_MODEL)
        return {'query': jax.random.normal(ks[0], (B, T, D_MODEL), dtype=jnp.float32), 'key': jax.random.normal(ks[1], (B, T, D_MODEL), dtype=jnp.float32), 'value': jax.random.normal(ks[2], (B, T, D_MODEL), dtype=jnp.float32), 'Wq': jax.random.normal(ks[3], (D_MODEL, D_MODEL), dtype=jnp.float32) * s, 'bq': jnp.zeros((D_MODEL,), dtype=jnp.float32), 'Wk': jax.random.normal(ks[4], (D_MODEL, D_MODEL), dtype=jnp.float32) * s, 'bk': jnp.zeros((D_MODEL,), dtype=jnp.float32), 'Wv': jax.random.normal(ks[5], (D_MODEL, D_MODEL), dtype=jnp.float32) * s, 'bv': jnp.zeros((D_MODEL,), dtype=jnp.float32), 'Wh': jax.random.normal(ks[6], (D_MODEL, D_MODEL), dtype=jnp.float32) * s, 'bh': jnp.zeros((D_MODEL,), dtype=jnp.float32)}
    _L2_xattn_all = _L2_xattn_setup()
    _L2_xattn_in = {k: v for k, v in _L2_xattn_all.items() if k in ('Wq', 'bq', 'Wk', 'bk', 'Wv', 'bv', 'Wh', 'bh')}
    del _L2_xattn_all

    def _L2_attn_setup():
        import jax, jax.numpy as jnp
        import numpy as np
        E = 2

        def _linear_scan(u, a):

            def comb(x, y):
                a1, b1 = x
                a2, b2 = y
                return (a2 * a1, a2 * b1 + b2)
            _, h = jax.lax.associative_scan(comb, (a, u), axis=0)
            return h
        key = jax.random.key(seed)
        ks = jax.random.split(key, 8)
        n, b, d = (512, 4, 256)
        s = 1.0 / np.sqrt(d)
        return {'x': jax.random.normal(ks[0], (n, b, d), jnp.float32), 'lower_bound': jax.random.uniform(ks[1], (d,), jnp.float32), 'W_in': jax.random.normal(ks[2], (d, 3 * d), jnp.float32) * s, 'b_in': jnp.zeros((3 * d,), jnp.float32), 'W_out': jax.random.normal(ks[3], (d, d), jnp.float32) * s, 'b_out': jnp.zeros((d,), jnp.float32), 'gamma': jnp.ones((d,), jnp.float32), 'beta': jnp.zeros((d,), jnp.float32)}
    _L2_attn_all = _L2_attn_setup()
    _L2_attn_in = {k: v for k, v in _L2_attn_all.items() if k in ('lower_bound', 'W_in', 'b_in', 'W_out', 'b_out', 'gamma', 'beta')}
    del _L2_attn_all

    def _L2_ffn_setup():
        import jax, jax.numpy as jnp
        import numpy as np
        B, S, D, E, F = (2, 512, 256, 14, 512)
        key = jax.random.key(seed)
        k = jax.random.split(key, 4)
        h = jax.random.normal(k[0], (B, S, D), dtype=jnp.float32)
        router_w = jax.random.normal(k[1], (D, E), dtype=jnp.float32) * 0.02
        w1 = jax.random.uniform(k[2], (E, D, F), dtype=jnp.float32, minval=-1.0, maxval=1.0) * float(np.sqrt(6.0 / D))
        w2 = jax.random.uniform(k[3], (E, F, D), dtype=jnp.float32, minval=-1.0, maxval=1.0) * float(np.sqrt(6.0 / F))
        b1 = jnp.zeros((E, F), dtype=jnp.float32)
        b2 = jnp.zeros((E, D), dtype=jnp.float32)
        return {'h': h, 'router_w': router_w, 'w1': w1, 'b1': b1, 'w2': w2, 'b2': b2}
    _L2_ffn_all = _L2_ffn_setup()
    _L2_ffn_in = {k: v for k, v in _L2_ffn_all.items() if k in ('router_w', 'w1', 'b1', 'w2', 'b2')}
    del _L2_ffn_all

    def _L3_xattn_setup():
        import jax, jax.numpy as jnp
        import numpy as np
        E = 256
        H = 16
        D = E // H
        key = jax.random.key(seed)
        ks = jax.random.split(key, 8)
        B, Lq, Lkv = (2, 512, 512)
        scale = 1.0 / np.sqrt(E)
        return {'query': jax.random.normal(ks[0], (B, Lq, E), dtype=jnp.float32), 'key_value': jax.random.normal(ks[1], (B, Lkv, E), dtype=jnp.float32), 'mask': jax.random.randint(ks[2], (B, Lkv), 0, 2, dtype=jnp.int32), 'Wq': jax.random.normal(ks[3], (E, E), dtype=jnp.float32) * scale, 'bq': jnp.zeros((E,), dtype=jnp.float32), 'Wk': jax.random.normal(ks[4], (E, E), dtype=jnp.float32) * scale, 'bk': jnp.zeros((E,), dtype=jnp.float32), 'Wv': jax.random.normal(ks[5], (E, E), dtype=jnp.float32) * scale, 'bv': jnp.zeros((E,), dtype=jnp.float32), 'Wo': jax.random.normal(ks[6], (E, E), dtype=jnp.float32) * scale, 'bo': jnp.zeros((E,), dtype=jnp.float32)}
    _L3_xattn_all = _L3_xattn_setup()
    _L3_xattn_in = {k: v for k, v in _L3_xattn_all.items() if k in ('Wq', 'bq', 'Wk', 'bk', 'Wv', 'bv', 'Wo', 'bo')}
    del _L3_xattn_all

    def _L3_attn_setup():
        import jax, jax.numpy as jnp
        import numpy as np
        key = jax.random.key(seed)
        ks = jax.random.split(key, 7)
        B, P, D = (4, 512, 256)
        s = 1.0 / np.sqrt(D)
        return {'x': jax.random.normal(ks[0], (B, P, D), dtype=jnp.float32), 'Wq': jax.random.normal(ks[1], (D, D), dtype=jnp.float32) * s, 'bq': jnp.zeros((D,), dtype=jnp.float32), 'Wk': jax.random.normal(ks[2], (D, D), dtype=jnp.float32) * s, 'bk': jnp.zeros((D,), dtype=jnp.float32), 'Wv': jax.random.normal(ks[3], (D, D), dtype=jnp.float32) * s, 'bv': jnp.zeros((D,), dtype=jnp.float32)}
    _L3_attn_all = _L3_attn_setup()
    _L3_attn_in = {k: v for k, v in _L3_attn_all.items() if k in ('Wq', 'bq', 'Wk', 'bk', 'Wv', 'bv')}
    del _L3_attn_all

    def _L3_ffn_setup():
        import jax, jax.numpy as jnp
        import numpy as np
        LORA_DIM = 16
        LORA_TOKEN_INDEX = 1
        B, S, D, H = (4, 512, 256, 1024)
        key = jax.random.key(seed)
        ks = jax.random.split(key, 6)
        x = jax.random.normal(ks[0], (B, S, D), dtype=jnp.float32)
        W1 = jax.random.normal(ks[1], (H, D), dtype=jnp.float32) * 0.02
        b1 = jnp.zeros((H,), dtype=jnp.float32)
        W2 = jax.random.normal(ks[2], (D, H), dtype=jnp.float32) * 0.02
        b2 = jnp.zeros((D,), dtype=jnp.float32)
        scale = jnp.asarray(0.001, dtype=jnp.float32)
        return {'x': x, 'W1': W1, 'b1': b1, 'W2': W2, 'b2': b2, 'scale': scale}
    _L3_ffn_all = _L3_ffn_setup()
    _L3_ffn_in = {k: v for k, v in _L3_ffn_all.items() if k in ('W1', 'b1', 'W2', 'b2', 'scale')}
    del _L3_ffn_all
    return {'x': x, 'ctx_1024': ctx_1024, 'mask_Bx1x1xS2_fk0': mask_Bx1x1xS2_fk0, 'mask_BxS2_ik0': mask_BxS2_ik0, 'L0_xattn_Wq': _L0_xattn_in['Wq'], 'L0_xattn_bq': _L0_xattn_in['bq'], 'L0_xattn_Wk': _L0_xattn_in['Wk'], 'L0_xattn_bk': _L0_xattn_in['bk'], 'L0_xattn_Wv': _L0_xattn_in['Wv'], 'L0_xattn_bv': _L0_xattn_in['bv'], 'L0_xattn_Wo': _L0_xattn_in['Wo'], 'L0_xattn_bo': _L0_xattn_in['bo'], 'L0_attn_qkv_w': _L0_attn_in['qkv_w'], 'L0_attn_proj_w': _L0_attn_in['proj_w'], 'L0_attn_proj_b': _L0_attn_in['proj_b'], 'L0_attn_slopes': _L0_attn_in['slopes'], 'L0_ffn_gate_w': _L0_ffn_in['gate_w'], 'L0_ffn_gate_bias': _L0_ffn_in['gate_bias'], 'L0_ffn_Wg': _L0_ffn_in['Wg'], 'L0_ffn_Wu': _L0_ffn_in['Wu'], 'L0_ffn_Wd': _L0_ffn_in['Wd'], 'L0_ffn_Sg': _L0_ffn_in['Sg'], 'L0_ffn_Su': _L0_ffn_in['Su'], 'L0_ffn_Sd': _L0_ffn_in['Sd'], 'L1_xattn_Wq': _L1_xattn_in['Wq'], 'L1_xattn_bq': _L1_xattn_in['bq'], 'L1_xattn_Wk': _L1_xattn_in['Wk'], 'L1_xattn_bk': _L1_xattn_in['bk'], 'L1_xattn_Wv': _L1_xattn_in['Wv'], 'L1_xattn_bv': _L1_xattn_in['bv'], 'L1_xattn_Wo': _L1_xattn_in['Wo'], 'L1_xattn_bo': _L1_xattn_in['bo'], 'L1_attn_Wq': _L1_attn_in['Wq'], 'L1_attn_Wk': _L1_attn_in['Wk'], 'L1_attn_Wv': _L1_attn_in['Wv'], 'L1_attn_Wo': _L1_attn_in['Wo'], 'L1_ffn_fast_b': _L1_ffn_in['fast_b'], 'L1_ffn_w_fc': _L1_ffn_in['w_fc'], 'L1_ffn_w_proj': _L1_ffn_in['w_proj'], 'L1_ffn_u': _L1_ffn_in['u'], 'L1_ffn_v': _L1_ffn_in['v'], 'L1_ffn_gate': _L1_ffn_in['gate'], 'L2_xattn_Wq': _L2_xattn_in['Wq'], 'L2_xattn_bq': _L2_xattn_in['bq'], 'L2_xattn_Wk': _L2_xattn_in['Wk'], 'L2_xattn_bk': _L2_xattn_in['bk'], 'L2_xattn_Wv': _L2_xattn_in['Wv'], 'L2_xattn_bv': _L2_xattn_in['bv'], 'L2_xattn_Wh': _L2_xattn_in['Wh'], 'L2_xattn_bh': _L2_xattn_in['bh'], 'L2_attn_lower_bound': _L2_attn_in['lower_bound'], 'L2_attn_W_in': _L2_attn_in['W_in'], 'L2_attn_b_in': _L2_attn_in['b_in'], 'L2_attn_W_out': _L2_attn_in['W_out'], 'L2_attn_b_out': _L2_attn_in['b_out'], 'L2_attn_gamma': _L2_attn_in['gamma'], 'L2_attn_beta': _L2_attn_in['beta'], 'L2_ffn_router_w': _L2_ffn_in['router_w'], 'L2_ffn_w1': _L2_ffn_in['w1'], 'L2_ffn_b1': _L2_ffn_in['b1'], 'L2_ffn_w2': _L2_ffn_in['w2'], 'L2_ffn_b2': _L2_ffn_in['b2'], 'L3_xattn_Wq': _L3_xattn_in['Wq'], 'L3_xattn_bq': _L3_xattn_in['bq'], 'L3_xattn_Wk': _L3_xattn_in['Wk'], 'L3_xattn_bk': _L3_xattn_in['bk'], 'L3_xattn_Wv': _L3_xattn_in['Wv'], 'L3_xattn_bv': _L3_xattn_in['bv'], 'L3_xattn_Wo': _L3_xattn_in['Wo'], 'L3_xattn_bo': _L3_xattn_in['bo'], 'L3_attn_Wq': _L3_attn_in['Wq'], 'L3_attn_bq': _L3_attn_in['bq'], 'L3_attn_Wk': _L3_attn_in['Wk'], 'L3_attn_bk': _L3_attn_in['bk'], 'L3_attn_Wv': _L3_attn_in['Wv'], 'L3_attn_bv': _L3_attn_in['bv'], 'L3_ffn_W1': _L3_ffn_in['W1'], 'L3_ffn_b1': _L3_ffn_in['b1'], 'L3_ffn_W2': _L3_ffn_in['W2'], 'L3_ffn_b2': _L3_ffn_in['b2'], 'L3_ffn_scale': _L3_ffn_in['scale']}

def reference(x, ctx_1024, mask_Bx1x1xS2_fk0, mask_BxS2_ik0, L0_xattn_Wq, L0_xattn_bq, L0_xattn_Wk, L0_xattn_bk, L0_xattn_Wv, L0_xattn_bv, L0_xattn_Wo, L0_xattn_bo, L0_attn_qkv_w, L0_attn_proj_w, L0_attn_proj_b, L0_attn_slopes, L0_ffn_gate_w, L0_ffn_gate_bias, L0_ffn_Wg, L0_ffn_Wu, L0_ffn_Wd, L0_ffn_Sg, L0_ffn_Su, L0_ffn_Sd, L1_xattn_Wq, L1_xattn_bq, L1_xattn_Wk, L1_xattn_bk, L1_xattn_Wv, L1_xattn_bv, L1_xattn_Wo, L1_xattn_bo, L1_attn_Wq, L1_attn_Wk, L1_attn_Wv, L1_attn_Wo, L1_ffn_fast_b, L1_ffn_w_fc, L1_ffn_w_proj, L1_ffn_u, L1_ffn_v, L1_ffn_gate, L2_xattn_Wq, L2_xattn_bq, L2_xattn_Wk, L2_xattn_bk, L2_xattn_Wv, L2_xattn_bv, L2_xattn_Wh, L2_xattn_bh, L2_attn_lower_bound, L2_attn_W_in, L2_attn_b_in, L2_attn_W_out, L2_attn_b_out, L2_attn_gamma, L2_attn_beta, L2_ffn_router_w, L2_ffn_w1, L2_ffn_b1, L2_ffn_w2, L2_ffn_b2, L3_xattn_Wq, L3_xattn_bq, L3_xattn_Wk, L3_xattn_bk, L3_xattn_Wv, L3_xattn_bv, L3_xattn_Wo, L3_xattn_bo, L3_attn_Wq, L3_attn_bq, L3_attn_Wk, L3_attn_bk, L3_attn_Wv, L3_attn_bv, L3_ffn_W1, L3_ffn_b1, L3_ffn_W2, L3_ffn_b2, L3_ffn_scale):
    import jax
    import jax.numpy as jnp

    def _L0_xattn_ref(x, context, Wq, bq, Wk, bk, Wv, bv, Wo, bo):
        import jax, jax.numpy as jnp
        import numpy as np
        D_MODEL = 256
        NUM_HEADS = 16
        DEPTH = D_MODEL // NUM_HEADS
        B, T, D = x.shape
        C = context.shape[1]
        H, d = (NUM_HEADS, DEPTH)
        q = x @ Wq.T + bq
        k = context @ Wk.T + bk
        v = context @ Wv.T + bv
        q = q.reshape(B, T, H, d).transpose(0, 2, 1, 3)
        k = k.reshape(B, C, H, d).transpose(0, 2, 1, 3)
        v = v.reshape(B, C, H, d).transpose(0, 2, 1, 3)
        scores = jnp.einsum('bhtd,bhcd->bhtc', q, k) / jnp.sqrt(jnp.asarray(d, x.dtype))
        attn = jax.nn.softmax(scores, axis=-1)
        out = jnp.einsum('bhtc,bhcd->bhtd', attn, v)
        out = out.transpose(0, 2, 1, 3).reshape(B, T, D)
        return out @ Wo.T + bo

    def _L0_attn_ref(x, qkv_w, proj_w, proj_b, slopes):
        import jax, jax.numpy as jnp
        import numpy as np
        import math
        DIM = 256
        NUM_HEADS = 16
        HEAD_DIM = DIM // NUM_HEADS
        MAX_BIAS = 8.0
        SCALE = HEAD_DIM ** (-0.5)

        def _alibi_slopes(n):

            def pow2(n):
                start = 2.0 ** (-2.0 ** (-(math.log2(n) - 3)))
                return [start * start ** i for i in range(n)]
            if math.log2(n).is_integer():
                return pow2(n)
            c = 2 ** math.floor(math.log2(n))
            return pow2(c) + _alibi_slopes(2 * c)[0::2][:n - c]

        def _rotate_half(t):
            t1, t2 = jnp.split(t, 2, axis=-1)
            return jnp.concatenate([-t2, t1], axis=-1)
        B, N, C = x.shape
        H, D = (NUM_HEADS, HEAD_DIM)
        qkv = (x @ qkv_w.T).reshape(B, N, 3, H, D).transpose(2, 0, 3, 1, 4)
        q, k, v = (qkv[0], qkv[1], qkv[2])
        inv_freq = 1.0 / 10000.0 ** (jnp.arange(0, D, 2, dtype=jnp.float32) / D)
        freqs = jnp.arange(N, dtype=jnp.float32)[:, None] * inv_freq[None, :]
        sin = jnp.tile(jnp.sin(freqs), (1, 2))
        cos = jnp.tile(jnp.cos(freqs), (1, 2))
        q = q * cos + _rotate_half(q) * sin
        k = k * cos + _rotate_half(k) * sin
        attn = jnp.einsum('bhqd,bhkd->bhqk', q, k) * SCALE
        pos = jnp.arange(N, dtype=jnp.float32)
        diff = pos[None, :] - pos[:, None]
        diff = jnp.where(diff > 0, 0.0, diff)
        alibi = diff[None, :, :] * slopes[:, None, None] * MAX_BIAS
        attn = attn + alibi[None]
        w = jax.nn.softmax(attn, axis=-1)
        out = jnp.einsum('bhqk,bhkd->bhqd', w, v)
        out = out.transpose(0, 2, 1, 3).reshape(B, N, C)
        return out @ proj_w.T + proj_b

    def _L0_ffn_ref(hidden_states, gate_w, gate_bias, Wg, Wu, Wd, Sg, Su, Sd):
        import jax, jax.numpy as jnp
        import numpy as np
        H = 256
        I = 176
        E = 64
        TOP_K = 8
        NG = 8
        TOPK_GROUP = 4
        N_SHARED = 2
        ROUTED_SCALE = 2.5
        S_I = I * N_SHARED

        def _route(x, gate_w, gate_bias):
            T = x.shape[0]
            logits = x @ gate_w.T
            scores = jax.nn.sigmoid(logits)
            scores_for_choice = scores + gate_bias[None, :]
            grp = scores_for_choice.reshape(T, NG, E // NG)
            group_scores = jnp.sum(jax.lax.top_k(grp, 2)[0], axis=-1)
            _, gidx = jax.lax.top_k(group_scores, TOPK_GROUP)
            gmask = jnp.zeros((T, NG), dtype=scores.dtype).at[jnp.arange(T)[:, None], gidx].set(1.0)
            emask = jnp.repeat(gmask, E // NG, axis=1)
            masked = jnp.where(emask > 0, scores_for_choice, 0.0)
            _, topk_idx = jax.lax.top_k(masked, TOP_K)
            topk_w = jnp.take_along_axis(scores, topk_idx, axis=1)
            topk_w = topk_w / (jnp.sum(topk_w, axis=-1, keepdims=True) + 1e-20)
            topk_w = topk_w * ROUTED_SCALE
            rw = jnp.zeros((T, E), dtype=scores.dtype).at[jnp.arange(T)[:, None], topk_idx].add(topk_w)
            return rw

        def _mlp(x, gw, uw, dw):
            return jax.nn.silu(x @ gw.T) * (x @ uw.T) @ dw.T
        B, S, _ = hidden_states.shape
        x = hidden_states.reshape(B * S, H)
        rw = _route(x, gate_w, gate_bias)
        expert_out = jax.vmap(lambda gw_, uw_, dw_: _mlp(x, gw_, uw_, dw_))(Wg, Wu, Wd)
        routed = jnp.einsum('eth,te->th', expert_out, rw)
        shared = _mlp(x, Sg, Su, Sd)
        out = (routed + shared).reshape(B, S, H)
        return out

    def _L1_xattn_ref(query, key, value, mask, Wq, bq, Wk, bk, Wv, bv, Wo, bo):
        import jax, jax.numpy as jnp
        import numpy as np
        B, S, D, H = (2, 512, 256, 16)
        DH = D // H

        def _split_heads(x):
            b, s, _ = x.shape
            return x.reshape(b, s, H, DH).transpose(0, 2, 1, 3)
        q = _split_heads(query @ Wq + bq)
        k = _split_heads(key @ Wk + bk)
        v = _split_heads(value @ Wv + bv)
        logits = jnp.einsum('bhqd,bhkd->bhqk', q, k) / jnp.sqrt(jnp.float32(DH))
        logits = logits + mask * -1000000000.0
        attn = jax.nn.softmax(logits, axis=-1)
        out = jnp.einsum('bhqk,bhkd->bhqd', attn, v)
        out = out.transpose(0, 2, 1, 3).reshape(query.shape[0], -1, D)
        return out @ Wo + bo

    def _L1_attn_ref(x, Wq, Wk, Wv, Wo):
        import jax, jax.numpy as jnp
        import numpy as np
        B, T, D_MODEL = (2, 512, 256)
        N_HEADS, HEAD_DIM = (16, 64)
        ROPE_BASE = 10000.0

        def rotate_half(x):
            half = x.shape[-1] // 2
            x1, x2 = (x[..., :half], x[..., half:])
            return jnp.concatenate([-x2, x1], axis=-1)
        Bx, Tx, C = x.shape
        H, D = (N_HEADS, HEAD_DIM)
        Q = (x @ Wq).reshape(Bx, Tx, H, D).transpose(0, 2, 1, 3)
        K = (x @ Wk).reshape(Bx, Tx, H, D).transpose(0, 2, 1, 3)
        V = (x @ Wv).reshape(Bx, Tx, H, D).transpose(0, 2, 1, 3)
        t = jnp.arange(Tx, dtype=jnp.float32)
        inv_freq = 1.0 / ROPE_BASE ** (jnp.arange(0, D, 2, dtype=jnp.float32) / D)
        f = t[:, None] * inv_freq[None, :]
        freqs = jnp.concatenate([f, f], axis=-1)
        cos, sin = (jnp.cos(freqs), jnp.sin(freqs))
        Q = Q * cos + rotate_half(Q) * sin
        K = K * cos + rotate_half(K) * sin
        scores = jnp.einsum('bhqd,bhkd->bhqk', Q, K) / jnp.sqrt(jnp.float32(D))
        w = Tx // 4
        idx = jnp.arange(Tx)
        allowed = jnp.abs(idx[:, None] - idx[None, :]) <= w
        scores = jnp.where(allowed[None, None], scores, -jnp.inf)
        attn = jax.nn.softmax(scores, axis=-1)
        out = jnp.einsum('bhqk,bhkd->bhqd', attn, V)
        out = out.transpose(0, 2, 1, 3).reshape(Bx, Tx, H * D)
        return out @ Wo

    def _L1_ffn_ref(x, fast_b, w_fc, w_proj, u, v, gate):
        import jax, jax.numpy as jnp
        import numpy as np

        def _bitlinear(x, w_latent):
            scale = jax.lax.stop_gradient(jnp.clip(jnp.mean(jnp.abs(w_latent), axis=1, keepdims=True), 1e-05, None))
            tern = jnp.clip(jnp.round(w_latent / scale), -1.0, 1.0)
            w = w_latent + jax.lax.stop_gradient(tern - w_latent)
            return x @ (w * scale).T
        h = _bitlinear(x, w_fc) + gate * (x @ v.T @ fast_b.T @ u.T)
        r = jnp.maximum(h, 0.0)
        return _bitlinear(r * r, w_proj)

    def _L2_xattn_ref(query, key, value, Wq, bq, Wk, bk, Wv, bv, Wh, bh):
        import jax, jax.numpy as jnp
        import numpy as np
        D_MODEL = 256
        N_HEADS = 16
        D_HEAD = D_MODEL // N_HEADS
        B, T_src, _ = query.shape
        T_dst = key.shape[1]
        Q = query @ Wq.T + bq
        K = key @ Wk.T + bk
        V = value @ Wv.T + bv
        Q = Q.reshape(B, T_src, N_HEADS, D_HEAD).transpose(0, 2, 1, 3)
        K = K.reshape(B, T_dst, N_HEADS, D_HEAD).transpose(0, 2, 1, 3)
        V = V.reshape(B, T_dst, N_HEADS, D_HEAD).transpose(0, 2, 1, 3)
        dot = jnp.einsum('bhsd,bhtd->bhst', Q, K) / np.sqrt(D_HEAD)
        scores = jax.nn.softmax(dot, axis=-1)
        out = jnp.einsum('bhst,bhtd->bhsd', scores, V)
        out = out.reshape(B, T_src, D_MODEL)
        return out @ Wh.T + bh

    def _L2_attn_ref(x, lower_bound, W_in, b_in, W_out, b_out, gamma, beta):
        import jax, jax.numpy as jnp
        import numpy as np
        E = 2

        def _linear_scan(u, a):

            def comb(x, y):
                a1, b1 = x
                a2, b2 = y
                return (a2 * a1, a2 * b1 + b2)
            _, h = jax.lax.associative_scan(comb, (a, u), axis=0)
            return h
        n, b, d = x.shape
        h = d // E
        feat = x @ W_in + b_in
        inp, og, fg = jnp.split(feat, 3, axis=-1)
        inp = jax.nn.silu(inp)
        og = jax.nn.sigmoid(og)
        fg = jax.nn.sigmoid(fg)
        inp = inp.reshape(n, b, h, E)
        og = og.reshape(n, b, h, E)
        fg = fg.reshape(n, b, h, E)
        lb = lower_bound.reshape(h, E)
        lam = lb + (1.0 - lb) * fg
        u = jnp.einsum('nbhd,nbhe->nbhde', 1.0 - lam, inp)
        a = jnp.broadcast_to(lam[..., None], u.shape)
        u = u.reshape(n, b, h * E * E)
        a = a.reshape(n, b, h * E * E)
        state_fwd = _linear_scan(u, a)
        state_rev = jnp.flip(_linear_scan(jnp.flip(u, 0), jnp.flip(a, 0)), 0)
        state = (state_fwd + state_rev).reshape(n, b, h, E, E)
        out = jnp.einsum('nbhde,nbhd->nbhe', state, og).reshape(n, b, d)
        mu = jnp.mean(out, axis=-1, keepdims=True)
        var = jnp.var(out, axis=-1, keepdims=True)
        out = (out - mu) * jax.lax.rsqrt(var + 1e-05) * gamma + beta
        return out @ W_out + b_out

    def _L2_ffn_ref(h, router_w, w1, b1, w2, b2):
        import jax, jax.numpy as jnp
        import numpy as np
        B, S, D, E, F = (2, 512, 256, 14, 512)
        Bb, Ss, Dd = h.shape
        x = h.reshape(-1, Dd)
        logits = x @ router_w
        assignments = jnp.argmax(logits, axis=-1)
        probs = jax.nn.softmax(logits, axis=-1)
        weights = jnp.take_along_axis(probs, assignments[:, None], axis=1)[:, 0]
        hid = jnp.einsum('nd,edf->nef', x, w1) + b1
        hid = jax.nn.gelu(hid, approximate=False)
        all_out = jnp.einsum('nef,efd->ned', hid, w2) + b2
        sel = jnp.take_along_axis(all_out, assignments[:, None, None], axis=1)[:, 0, :]
        moe_out = (sel * weights[:, None]).reshape(Bb, Ss, Dd)
        return moe_out

    def _L3_xattn_ref(query, key_value, mask, Wq, bq, Wk, bk, Wv, bv, Wo, bo):
        import jax, jax.numpy as jnp
        import numpy as np
        E = 256
        H = 16
        D = E // H
        B, Lq, _ = query.shape
        Lkv = key_value.shape[1]
        Q = (query @ Wq.T + bq).reshape(B, Lq, H, D)
        K = (key_value @ Wk.T + bk).reshape(B, Lkv, H, D)
        V = (key_value @ Wv.T + bv).reshape(B, Lkv, H, D)
        scores = jnp.einsum('bqhd,bkhd->bhqk', Q, K) / jnp.sqrt(jnp.float32(D))
        scores = jnp.where(mask[:, None, None, :] == 0, -jnp.inf, scores)
        probs = jax.nn.softmax(scores, axis=-1)
        context = jnp.einsum('bhqk,bkhd->bqhd', probs, V).reshape(B, Lq, E)
        return context @ Wo.T + bo

    def _L3_attn_ref(x, Wq, bq, Wk, bk, Wv, bv):
        import jax, jax.numpy as jnp
        import numpy as np
        b, p, d = x.shape
        q = jnp.einsum('bpd,ed->bpe', x, Wq) + bq
        k = jnp.einsum('bpd,ed->bpe', x, Wk) + bk
        v = jnp.einsum('bpd,ed->bpe', x, Wv) + bv
        attn = jnp.einsum('bqd,bkd->bqk', q, k)
        causal = jnp.triu(jnp.ones((p, p), dtype=bool), k=1)
        attn = jnp.where(causal, -jnp.inf, attn)
        attn = attn / jnp.sqrt(jnp.asarray(d, dtype=attn.dtype))
        scores = jax.nn.softmax(attn, axis=-1)
        return jnp.einsum('bqk,bkd->bqd', scores, v)

    def _L3_ffn_ref(x, W1, b1, W2, b2, scale):
        import jax, jax.numpy as jnp
        import numpy as np
        LORA_DIM = 16
        LORA_TOKEN_INDEX = 1
        B, S, D, H = (4, 512, 256, 1024)
        Bx, Sx, Dx = x.shape
        Hx = W1.shape[0]
        lt = jax.lax.dynamic_slice_in_dim(x, LORA_TOKEN_INDEX, LORA_DIM, axis=1)
        even = lt[:, ::2, :]
        odd = lt[:, 1::2, :]
        m1 = (even[:, :4, :, None] * odd[:, :4, None, :]).reshape(Bx, Hx, Dx)
        m2 = (even[:, 4:, :, None] * odd[:, 4:, None, :]).reshape(Bx, Dx, Hx)
        h = jnp.einsum('bsd,hd->bsh', x, W1) + scale * jnp.einsum('bsd,bhd->bsh', x, m1) + b1
        h = jax.nn.gelu(h, approximate=False)
        out = jnp.einsum('bsh,oh->bso', h, W2) + scale * jnp.einsum('bsh,boh->bso', h, m2) + b2
        return out
    x = x + _L0_xattn_ref(_layernorm(x, axis=-1), ctx_1024, L0_xattn_Wq, L0_xattn_bq, L0_xattn_Wk, L0_xattn_bk, L0_xattn_Wv, L0_xattn_bv, L0_xattn_Wo, L0_xattn_bo)
    x = x + _L0_attn_ref(_layernorm(x, axis=-1), L0_attn_qkv_w, L0_attn_proj_w, L0_attn_proj_b, L0_attn_slopes)
    x = x + _L0_ffn_ref(_layernorm(x, axis=-1), L0_ffn_gate_w, L0_ffn_gate_bias, L0_ffn_Wg, L0_ffn_Wu, L0_ffn_Wd, L0_ffn_Sg, L0_ffn_Su, L0_ffn_Sd)
    x = x + _L1_xattn_ref(_layernorm(x, axis=-1), ctx_1024, ctx_1024, mask_Bx1x1xS2_fk0, L1_xattn_Wq, L1_xattn_bq, L1_xattn_Wk, L1_xattn_bk, L1_xattn_Wv, L1_xattn_bv, L1_xattn_Wo, L1_xattn_bo)
    x = x + _L1_attn_ref(_layernorm(x, axis=-1), L1_attn_Wq, L1_attn_Wk, L1_attn_Wv, L1_attn_Wo)
    x = x + _L1_ffn_ref(_layernorm(x, axis=-1), L1_ffn_fast_b, L1_ffn_w_fc, L1_ffn_w_proj, L1_ffn_u, L1_ffn_v, L1_ffn_gate)
    x = x + _L2_xattn_ref(_layernorm(x, axis=-1), ctx_1024, ctx_1024, L2_xattn_Wq, L2_xattn_bq, L2_xattn_Wk, L2_xattn_bk, L2_xattn_Wv, L2_xattn_bv, L2_xattn_Wh, L2_xattn_bh)
    x = x + _L2_attn_ref(_layernorm(x, axis=-1), L2_attn_lower_bound, L2_attn_W_in, L2_attn_b_in, L2_attn_W_out, L2_attn_b_out, L2_attn_gamma, L2_attn_beta)
    x = x + _L2_ffn_ref(_layernorm(x, axis=-1), L2_ffn_router_w, L2_ffn_w1, L2_ffn_b1, L2_ffn_w2, L2_ffn_b2)
    x = x + _L3_xattn_ref(_layernorm(x, axis=-1), ctx_1024, mask_BxS2_ik0, L3_xattn_Wq, L3_xattn_bq, L3_xattn_Wk, L3_xattn_bk, L3_xattn_Wv, L3_xattn_bv, L3_xattn_Wo, L3_xattn_bo)
    x = x + _L3_attn_ref(_layernorm(x, axis=-1), L3_attn_Wq, L3_attn_bq, L3_attn_Wk, L3_attn_bk, L3_attn_Wv, L3_attn_bv)
    x = x + _L3_ffn_ref(_layernorm(x, axis=-1), L3_ffn_W1, L3_ffn_b1, L3_ffn_W2, L3_ffn_b2, L3_ffn_scale)
    return x

_drawn_inputs = setup_inputs


def setup_inputs(seed=0):
    import zlib

    import numpy as np

    out = dict(_drawn_inputs(seed))
    spreads = {'L0_xattn_bq': (0.0, 0.304),
     'L0_xattn_bk': (0.0, 2.0),
     'L0_xattn_bv': (0.0, 0.1),
     'L0_xattn_bo': (0.0, 0.1),
     'L1_xattn_bq': (0.0, 0.8),
     'L1_xattn_bk': (0.0, 2.0),
     'L1_xattn_bv': (0.0, 0.455),
     'L1_xattn_bo': (0.0, 0.1),
     'L2_xattn_bq': (0.0, 1.708),
     'L2_xattn_bk': (0.0, 2.0),
     'L2_xattn_bv': (0.0, 0.359),
     'L2_xattn_bh': (0.0, 0.381),
     'L2_attn_b_in': (0.0, 0.1),
     'L2_attn_b_out': (0.0, 0.385),
     'L2_attn_gamma': (1.0, 0.2),
     'L2_attn_beta': (0.0, 0.377),
     'L2_ffn_b1': (0.0, 2.0),
     'L2_ffn_b2': (0.0, 2.0),
     'L3_xattn_bq': (0.0, 1.793),
     'L3_xattn_bk': (0.0, 2.0),
     'L3_xattn_bv': (0.0, 0.439),
     'L3_xattn_bo': (0.0, 0.41),
     'L3_attn_bq': (0.0, 2.0),
     'L3_attn_bk': (0.0, 2.0),
     'L3_attn_bv': (0.0, 0.442),
     'L3_ffn_b1': (0.0, 0.491),
     'L3_ffn_b2': (0.0, 0.401)}
    factors = {'L0_attn_proj_b': 4.034,
     'L0_ffn_gate_w': 4.764,
     'L0_ffn_gate_bias': 6.689,
     'L0_ffn_Wg': 4.692,
     'L0_ffn_Wu': 4.263,
     'L0_ffn_Wd': 4.103,
     'L0_ffn_Sg': 3.329,
     'L0_ffn_Su': 3.107,
     'L0_ffn_Sd': 3.406,
     'L1_xattn_Wq': 8.0,
     'L1_xattn_Wk': 8.0,
     'L1_attn_Wq': 8.0,
     'L1_attn_Wk': 8.0,
     'L1_ffn_fast_b': 8.0,
     'L1_ffn_u': 8.0,
     'L1_ffn_v': 8.0}
    for name, (base, spread) in spreads.items():
        noise = np.random.default_rng([zlib.crc32(name.encode()), seed]).standard_normal(out[name].shape)
        drawn = base * np.exp(spread * noise) if base else spread * noise
        out[name] = jnp.asarray(drawn.astype(out[name].dtype))
    for name, factor in factors.items():
        out[name] = (out[name] * factor).astype(out[name].dtype)
    return out
```

```python
from contextlib import ExitStack, contextmanager

import numpy as np
import concourse.bass as bass
from concourse import mybir

F32 = mybir.dt.float32
I32 = mybir.dt.int32
ALU = mybir.AluOpType
ACT = mybir.ActivationFunctionType
AX = mybir.AxisListType

P = 128
B, S, D = 16, 64, 256
TOK = B * S
TILES = TOK // P
KC = D // P
HALF = 512
CTX = 1601
HEADS = 16
PAIRS = HEADS // 2
KEY_TILES = -(-CTX // P)
LAST_KEYS = CTX - (KEY_TILES - 1) * P
EPS = 1e-5
NEG = -1e30


@contextmanager
def stage(nc, names):
    sems = [nc.alloc_semaphore(f"{n}_{nc.next_id()}") for n in names.split()]
    with ExitStack() as mem:
        block = mem.enter_context(nc.Block())
        yield (block, *sems)
    nc.clear_and_free_semaphores(sems)
    nc.all_engine_barrier()


def spread(ap, shape):
    return ap.to_broadcast(list(shape))


class Net:

    def __init__(self, nc, dram, ctx):
        self.nc, self.dram = nc, dram
        self.ctx = ctx
        self.x = self.sb("x_tok", [P, TILES, D])
        self.xnT = self.sb("xnT", [P, KC, TOK])
        self.actT = self.sb("actT", [P, 8, TOK])
        self.ident = self.sb("ident", [P, P])
        self.stack2 = self.sb("stack2", [P, S])
        self.ones = self.sb("ones", [P, P])
        self.parity = self.sb("parity", [P, 4])
        self.eps = self.sb("eps", [P, 1])
        self.ps = [ctx.enter_context(nc.psum_tensor(f"bank{i}", [P, 1024], F32)) for i in range(4)]

    def sb(self, name, shape, dt=F32, ctx=None):
        return (ctx or self.ctx).enter_context(self.nc.sbuf_tensor(name, shape, dt))

    def bank(self, i):
        return self.ps[i // 2][:, (i % 2) * 512:(i % 2) * 512 + 512]


def load_all(net):
    nc, d = net.nc, net.dram
    with stage(nc, "loaded eps_set") as (block, loaded, eps_set):
        @block.sync
        def _(sp):
            sp.dma_start(net.x[:], d["x"].rearrange("(t p) n -> p t n", p=P)).then_inc(loaded, 16)
            sp.dma_start(net.ident[:], d["ident"]).then_inc(loaded, 16)
            sp.dma_start(net.stack2[:], d["stack2"]).then_inc(loaded, 16)
            sp.dma_start(net.parity[:], d["parity"]).then_inc(loaded, 16)
            sp.wait_ge(loaded, 64)

        @block.vector
        def _(dve):
            nc.vector.memset(net.eps[:], EPS).then_inc(eps_set, 1)
            nc.vector.memset(net.ones[:], 1.0).then_inc(eps_set, 1)
            dve.wait_ge(eps_set, 2)


def norm(net, tag, src, gamma=None, beta=None):
    nc, d = net.nc, net.dram
    with ExitStack() as mem, stage(nc, "chain stats_ready std_ready xn_ready turned taken cols") as (
            block, chain, stats_ready, std_ready, xn_ready, turned, taken, cols):
        stats = net.sb(tag + "_stats", [P, TILES, 6], ctx=mem)
        mv = net.sb(tag + "_mv", [P, TILES, 2], ctx=mem)
        std = net.sb(tag + "_std", [P, TILES], ctx=mem)
        rstd = net.sb(tag + "_rstd", [P, TILES], ctx=mem)
        xn = net.sb(tag + "_xn", [P, TILES, D], ctx=mem)
        gb = net.sb(tag + "_gb", [P, 2 * KC], ctx=mem)

        if gamma:
            @block.sync
            def _(sp):
                sp.dma_start(gb[:, 0:KC], d[gamma]).then_inc(cols, 16)
                sp.dma_start(gb[:, KC:2 * KC], d[beta]).then_inc(cols, 16)

        @block.vector
        def _(dve):
            for t in range(TILES):
                nc.vector.bn_stats(stats[:, t, :], src[:, t, :]).then_inc(chain, 1)
            for t in range(TILES):
                dve.wait_ge(chain, t + 1)
                nc.vector.bn_aggr(mv[:, t, :], stats[:, t, :]).then_inc(stats_ready, 1)
            dve.wait_ge(std_ready, 1)
            nc.vector.reciprocal(rstd[:], std[:]).then_inc(chain, 1)
            dve.wait_ge(chain, TILES + 1)
            for t in range(TILES):
                nc.vector.tensor_scalar(xn[:, t, :], src[:, t, :], mv[:, t, 0:1], rstd[:, t:t + 1],
                                        ALU.subtract, ALU.mult).then_inc(xn_ready, 1)

        @block.scalar
        def _(act):
            act.wait_ge(stats_ready, TILES)
            nc.scalar.activation(std[:], mv[:, :, 1], ACT.Sqrt, bias=net.eps[:, 0:1]).then_inc(std_ready, 1)
            if gamma:
                act.wait_ge(cols, 32)
            for t in range(TILES):
                act.wait_ge(turned, t + 1)
                for c in range(KC):
                    kw = dict(scale=gb[:, c:c + 1], bias=gb[:, KC + c:KC + c + 1]) if gamma else {}
                    fn = ACT.Identity if gamma else ACT.Copy
                    last = nc.scalar.activation(net.xnT[:, c, t * P:(t + 1) * P],
                                                net.bank(t % 8)[:, c * P:(c + 1) * P], fn, **kw)
                last.then_inc(taken, 1)

        @block.tensor
        def _(pe):
            for t in range(TILES):
                pe.wait_ge(xn_ready, t + 1)
                for c in range(KC):
                    last = nc.tensor.transpose(net.bank(t % 8)[:, c * P:(c + 1) * P],
                                               xn[:, t, c * P:(c + 1) * P], net.ident[:])
                last.then_inc(turned, 1)


def project(net, tag, w, bias, chunks=KC, extra=None, src=None, w_sb=None, out=None):
    nc, d = net.nc, net.dram
    src = src or net.actT
    with ExitStack() as mem, stage(nc, "w_in made added stored") as (block, w_in, made, added, stored):
        wsb = w_sb or net.sb(tag + "_w", [P, chunks, D], ctx=mem)
        brow = net.sb(tag + "_b", [1, D], ctx=mem)

        @block.sync
        def _(sp):
            if not w_sb:
                sp.dma_start(wsb[:], d[w].rearrange("(c p) n -> p c n", p=P)).then_inc(w_in, 16)
            if bias:
                sp.dma_start(brow[:], d[bias]).then_inc(w_in, 16)
            if out is not None:
                for t in range(TILES):
                    sp.wait_ge(added, t + 1)
                    sp.dma_start(out[t * P:(t + 1) * P, :], net.x[:, t, :]).then_inc(stored, 16)
                sp.wait_ge(stored, 16 * TILES)

        @block.tensor
        def _(pe):
            if bias or not w_sb:
                pe.wait_ge(w_in, 16 * (bool(bias) + (not w_sb)))
            for t in range(TILES):
                dst = net.bank(t % 8)[:, 0:D]
                if bias:
                    nc.tensor.matmul(dst, net.ones[0:1, :], brow[:], start=True, stop=False)
                for k, (a, b) in enumerate(extra(t) if extra else []):
                    nc.tensor.matmul(dst, a, b, start=(k == 0 and not bias), stop=False)
                for c in range(chunks):
                    last = nc.tensor.matmul(dst, src[:, c, t * P:(t + 1) * P], wsb[:, c, :],
                                            start=(c == 0 and not bias and not extra), stop=(c == chunks - 1))
                last.then_inc(made, 1)

        @block.vector
        def _(dve):
            for t in range(TILES):
                dve.wait_ge(made, t + 1)
                nc.vector.tensor_tensor(net.x[:, t, :], net.x[:, t, :], net.bank(t % 8)[:, 0:D],
                                        ALU.add).then_inc(added, 1)


def cross_attention(net, tag, wq, bq, wk, bk, wv, bv, mask=None, scratch=None):
    nc, d = net.nc, net.dram
    USES = 8 + 2 * PAIRS
    SPLIT = 1024
    PART = [(0, SPLIT), (SPLIT, CTX)]
    GROUPS = [(0, 4), (4, 8), (8, 12), (12, 13)]
    names = ("w_in bias_in ctx_in0 ctx_in1 mask_in0 mask_in1 mask_ready slot_full slot_free0 slot_free1 turn_full "
             "turn_free0 turn_free1 q_full q_ready negmax_ready exp_done pv_done o_ready summed bank_free chain "
             "stored0 stored1 zeroed")
    with ExitStack() as mem, stage(nc, names) as (
            block, w_in, bias_in, ctx_in0, ctx_in1, mask_in0, mask_in1, mask_ready, slot_full, slot_free0, slot_free1,
            turn_full, turn_free0, turn_free1, q_full, q_ready, negmax_ready, exp_done, pv_done, o_ready, summed,
            bank_free, chain, stored0, stored1, zeroed):
        ctx_in, mask_in, stored = (ctx_in0, ctx_in1), (mask_in0, mask_in1), (stored0, stored1)
        slot_free = (slot_free0, slot_free1)
        turn_free = (turn_free0, turn_free1)
        wts = net.sb(tag + "_w", [P, 3, KC, D], ctx=mem)
        cols = net.sb(tag + "_cols", [P, 2, KC], ctx=mem)
        bvb = net.sb(tag + "_bv", [P, D], ctx=mem)
        ctxT = net.sb(tag + "_ctx", [P, 2, KC, CTX], ctx=mem)
        kT = net.sb(tag + "_kT", [P, KC, CTX], ctx=mem)
        v = net.sb(tag + "_v", [P, KEY_TILES, D], ctx=mem)
        prob = net.sb(tag + "_p", [P, 2, CTX], ctx=mem)
        probT = net.sb(tag + "_pT", [P, 2, KEY_TILES, P], ctx=mem)
        qb = net.sb(tag + "_q", [P, 2, KC, 2, S], ctx=mem)
        mbias = net.sb(tag + "_m", [P, 2, CTX], ctx=mem) if mask else None
        scrap = net.sb(tag + "_scrap", [P, 2], ctx=mem)
        part_max = net.sb(tag + "_mx", [P, 2, 2], ctx=mem)
        negmax = net.sb(tag + "_nm", [P, 2], ctx=mem)
        sums = net.sb(tag + "_sum", [P, 2, PAIRS], ctx=mem)
        rsum = net.sb(tag + "_rs", [P, PAIRS], ctx=mem)
        o_bd = net.sb(tag + "_o", [P, 2, PAIRS, 2, 16], ctx=mem)
        slots = net.ps[0:2]
        turns = (net.bank(4), net.bank(5))
        outs = (net.bank(6), net.bank(7))

        def q_psum(u):
            return outs[u][:, 384:512].rearrange("p (c s) -> p c s", c=KC)

        @block.sync
        def _(sp):
            for n, w in enumerate((wq, wk, wv)):
                sp.dma_start(wts[:, n], d[w].rearrange("(c p) n -> p c n", p=P)).then_inc(w_in, 16)
            sp.dma_start(cols[:, 0], d[bq]).then_inc(bias_in, 16)
            sp.dma_start(cols[:, 1], d[bk]).then_inc(bias_in, 16)
            sp.dma_start(bvb[:], spread(d[bv], (P, D))).then_inc(bias_in, 16)

            def load(b, u):
                sp.dma_start(ctxT[:, u], d["ctxT"][bass.ds(b, 1)].rearrange("o c p n -> p (o c) n")).then_inc(ctx_in[u], 16)
                if mask:
                    sp.dma_start((mbias[:, u].bitcast(I32) if mask == "mask_int" else mbias[:, u]),
                                 spread(d[mask][bass.ds(b, 1)], (P, CTX))).then_inc(mask_in[u], 16)

            def store(b, u):
                sp.wait_ge(o_ready, 4 + 2 * b + 2)
                for e in range(2):
                    sp.dma_start(scratch[bass.ds(b, 1)].rearrange("o (h e) s f -> s (o e) h f", e=2)[:, e],
                                 o_bd[e * S:(e + 1) * S, u, :, e]).then_inc(stored[u], 16)
            load(0, 0)
            load(1, 1)
            with sp.Fori(0, B // 2 - 1) as i:
                for u in range(2):
                    b = 2 * i + u
                    sp.wait_ge(slot_full, b * USES + 8)
                    if mask:
                        sp.wait_ge(negmax_ready, b * PAIRS + PAIRS)
                    load(b + 2, u)
                    if scratch is not None:
                        store(b, u)
            if scratch is not None:
                for b in (B - 2, B - 1):
                    store(b, b % 2)
                for u in range(2):
                    sp.wait_ge(stored[u], 32 + 16 * B)

        @block.gpsimd
        def _(pool):
            nc.gpsimd.memset(o_bd[:], 0.0).then_inc(zeroed, 1)

        @block.tensor
        def _(pe):
            pe.wait_ge(w_in, 48)

            def start_use(b, use):
                pe.wait_ge(slot_free[use % 2], b * (USES // 2) + use // 2 + 1)
                return slots[use % 2]

            def project_q(b, u):
                if scratch is None:
                    pe.wait_ge(bank_free, b + 1)
                else:
                    pe.wait_ge(o_ready, 2 * b + 2)
                for c in range(KC):
                    for k in range(KC):
                        last = nc.tensor.matmul(q_psum(u)[:, c], wts[:, 0, k, c * P:(c + 1) * P],
                                                net.xnT[:, k, bass.ds(b * S, S)], start=(k == 0), stop=(k == KC - 1))
                last.then_inc(q_full, 1)

            def project_kv(i, b, u):
                pe.wait_ge(ctx_in[u], i * 16 + 16)
                for c in range(KC):
                    for h, (lo, hi) in enumerate(PART):
                        slot = start_use(b, 2 * c + h)
                        for a in range(lo, hi, HALF):
                            z = min(a + HALF, hi)
                            for k in range(KC):
                                last = nc.tensor.matmul(slot[:, a - lo:z - lo], wts[:, 1, k, c * P:(c + 1) * P],
                                                        ctxT[:, u, k, a:z], start=(k == 0), stop=(k == KC - 1))
                        last.then_inc(slot_full, 1)
                for g, (lo, hi) in enumerate(GROUPS):
                    slot = start_use(b, 4 + g)
                    for t in range(lo, hi):
                        n = P if t < KEY_TILES - 1 else LAST_KEYS
                        for k in range(KC):
                            last = nc.tensor.matmul(slot[0:n, (t - lo) * D:(t - lo + 1) * D],
                                                    ctxT[:, u, k, t * P:t * P + n], wts[:, 2, k, :],
                                                    start=(k == 0), stop=(k == KC - 1))
                    last.then_inc(slot_full, 1)

            def scores(b, u, hp):
                r, c = 32 * (hp % 4), hp // 4
                for h, (lo, hi) in enumerate(PART):
                    slot = start_use(b, 8 + 2 * hp + h)
                    for a in range(lo, hi, HALF):
                        z = min(a + HALF, hi)
                        last = nc.tensor.matmul(slot[:, a - lo:z - lo], qb[r:r + 32, u, c, :, :], kT[r:r + 32, c, a:z],
                                                start=True, stop=True)
                    last.then_inc(slot_full, 1)

            def turn(b, hp, groups):
                pe.wait_ge(exp_done, b * PAIRS + hp + 1)
                for g in groups:
                    lo, hi = GROUPS[g]
                    pe.wait_ge(turn_free[g % 2], b * 2 * PAIRS + 2 * hp + g // 2 + 1)
                    for t in range(lo, hi):
                        n = P if t < KEY_TILES - 1 else LAST_KEYS
                        last = nc.tensor.transpose(turns[g % 2][0:n, (t - lo) * P:(t - lo + 1) * P],
                                                   prob[:, hp % 2, t * P:t * P + n], net.ident[:])
                    last.then_inc(turn_full, 1)

            def attend(b, u, hp):
                for f in turn_free:
                    pe.wait_ge(f, b * 2 * PAIRS + 2 * hp + 3)
                for t in range(KEY_TILES):
                    n = P if t < KEY_TILES - 1 else LAST_KEYS
                    last = nc.tensor.matmul(outs[u][:, hp * 32:(hp + 1) * 32], probT[0:n, hp % 2, t, :],
                                            v[0:n, t, hp * 32:(hp + 1) * 32], start=(t == 0), stop=(t == KEY_TILES - 1))
                last.then_inc(pv_done, 1)

            with pe.Fori(0, B // 2) as i:
                for u in range(2):
                    b = 2 * i + u
                    project_q(b, u)
                    project_kv(i, b, u)
                    pe.wait_ge(q_ready, b * 4 + 4)
                    scores(b, u, 0)
                    for hp in range(PAIRS):
                        turn(b, hp, (0, 1))
                        if hp + 1 < PAIRS:
                            scores(b, u, hp + 1)
                        turn(b, hp, (2, 3))
                        if hp:
                            attend(b, u, hp - 1)
                    attend(b, u, PAIRS - 1)
                    if scratch is None:
                        pe.wait_ge(o_ready, 4 + 2 * b + 2)
                        for c in range(KC):
                            flat = o_bd[:, u].rearrange("p h e f -> p (h e f)")
                            last = nc.tensor.matmul(outs[u][:, 256 + c * S:256 + (c + 1) * S],
                                                    flat[:, c * P:(c + 1) * P], net.stack2[:], start=True, stop=True)
                        last.then_inc(summed, 1)

        @block.vector
        def _(dve):
            dve.sem_inc(slot_free0, 1)
            dve.sem_inc(slot_free1, 1)
            dve.sem_inc(turn_free0, 1)
            dve.sem_inc(turn_free1, 1)
            dve.sem_inc(turn_full, 8)
            dve.sem_inc(pv_done, 2)
            dve.sem_inc(bank_free, 2)
            dve.sem_inc(o_ready, 4)
            dve.sem_inc(stored0, 32)
            dve.sem_inc(stored1, 32)
            dve.wait_ge(bias_in, 48)
            dve.wait_ge(zeroed, 1)

            def take_scores(b, u, hp):
                s = hp % 2
                dve.wait_ge(turn_full, b * 4 * PAIRS + 4 * hp + 4)
                for h, (lo, hi) in enumerate(PART):
                    use = 8 + 2 * hp + h
                    dve.wait_ge(slot_full, b * USES + use + 1)
                    src, dst = slots[use % 2][:, 0:hi - lo], prob[:, s, lo:hi]
                    if mask:
                        nc.vector.memset(scrap[:, h:h + 1], 0.0)
                        ins = nc.vector.tensor_tensor_reduce(dst, src, mbias[:, u, lo:hi], 1.0, -3e38, ALU.add, ALU.max,
                                                             part_max[:, s, h:h + 1])
                    else:
                        ins = nc.vector.tensor_scalar(dst, src, 0.0, None, ALU.add, ALU.max,
                                                      accum_out=part_max[:, s, h:h + 1])
                    ins.then_inc(slot_free[use % 2], 1)
                dve.wait_ge(slot_free0, b * (USES // 2) + 4 + hp + 2)
                dve.wait_ge(slot_free1, b * (USES // 2) + 4 + hp + 2)
                nc.vector.tensor_reduce(negmax[:, s:s + 1], part_max[:, s, :], AX.X, ALU.max,
                                        negate=True).then_inc(negmax_ready, 1)

            def take_turn(b, hp):
                dve.wait_ge(pv_done, b * PAIRS + hp + 1)
                for g in (0, 1):
                    lo, hi = GROUPS[g]
                    dve.wait_ge(turn_full, 8 + b * 4 * PAIRS + 4 * hp + g + 1)
                    nc.vector.tensor_copy(probT[:, hp % 2, lo:hi, :].rearrange("p t n -> p (t n)"),
                                          turns[g % 2][:, 0:(hi - lo) * P]).then_inc(turn_free[g % 2], 1)

            with dve.Fori(0, B // 2) as i:
                for u in range(2):
                    b = 2 * i + u
                    dve.wait_ge(q_full, b + 1)
                    for c in range(KC):
                        for e in range(2):
                            nc.vector.tensor_scalar(qb[:, u, c, e, :], q_psum(u)[:, c], cols[:, 0, c:c + 1],
                                                    net.parity[:, e:e + 1], ALU.add, ALU.mult).then_inc(q_ready, 1)
                    for g, (lo, hi) in enumerate(GROUPS):
                        use, n = 4 + g, P if g < 3 else LAST_KEYS
                        dve.wait_ge(slot_full, b * USES + use + 1)
                        nc.vector.tensor_tensor(
                            v[0:n, lo:hi, :], slots[use % 2][0:n, 0:(hi - lo) * D].rearrange("p (t f) -> p t f", f=D),
                            spread(bvb[0:n, :].unsqueeze(1), (n, hi - lo, D)), ALU.add).then_inc(slot_free[use % 2], 1)
                    if mask == "mask_f32":
                        dve.wait_ge(mask_in[u], i * 16 + 16)
                        nc.vector.tensor_scalar(mbias[:, u], mbias[:, u], -1e9, None, ALU.mult).then_inc(mask_ready, 1)
                        dve.wait_ge(mask_ready, b + 1)
                    elif mask:
                        dve.wait_ge(mask_in[u], i * 16 + 16)
                        nc.vector.tensor_scalar(mbias[:, u], mbias[:, u].bitcast(I32), 0.0, -3e38,
                                                ALU.is_equal, ALU.mult).then_inc(mask_ready, 1)
                        dve.wait_ge(mask_ready, b + 1)
                    take_scores(b, u, 0)
                    for hp in range(PAIRS):
                        take_turn(b, hp)
                        if hp + 1 < PAIRS:
                            take_scores(b, u, hp + 1)
                    dve.wait_ge(exp_done, b * PAIRS + PAIRS)
                    nc.vector.reciprocal(rsum[:], sums[:, u, :]).then_inc(chain, 1)
                    dve.wait_ge(chain, b + 1)
                    dve.wait_ge(pv_done, 2 + b * PAIRS + PAIRS)
                    if scratch is not None:
                        dve.wait_ge(stored[u], 32 * i + 32)
                    o3 = outs[u][:, 0:256].rearrange("p (h e f) -> p h e f", h=PAIRS, e=2)
                    for e in range(2):
                        r = slice(e * S, (e + 1) * S)
                        ins = nc.vector.tensor_tensor(o_bd[r, u, :, e, :], o3[r, :, e, :],
                                                      spread(rsum[r, :].unsqueeze(2), (S, PAIRS, 16)), ALU.mult)
                        ins.then_inc(o_ready, 1)

        @block.scalar
        def _(act):
            act.wait_ge(bias_in, 48)

            def take_turn(b, hp):
                act.wait_ge(pv_done, b * PAIRS + hp + 1)
                for g in (2, 3):
                    lo, hi = GROUPS[g]
                    n = P if g < 3 else LAST_KEYS
                    act.wait_ge(turn_full, 8 + b * 4 * PAIRS + 4 * hp + g + 1)
                    nc.scalar.activation(probT[0:n, hp % 2, lo:hi, :].rearrange("p t n -> p (t n)"),
                                         turns[g % 2][0:n, 0:(hi - lo) * P], ACT.Copy).then_inc(turn_free[g % 2], 1)

            def exps(b, u, hp):
                s = hp % 2
                act.wait_ge(negmax_ready, b * PAIRS + hp + 1)
                nc.scalar.activation(prob[:, s, :], prob[:, s, :], ACT.Exp, bias=negmax[:, s:s + 1],
                                     accum_out=sums[:, u, hp:hp + 1]).then_inc(exp_done, 1)

            with act.Fori(0, B // 2) as i:
                for u in range(2):
                    b = 2 * i + u
                    for c in range(KC):
                        for h, (lo, hi) in enumerate(PART):
                            use = 2 * c + h
                            act.wait_ge(slot_full, b * USES + use + 1)
                            nc.scalar.activation(kT[:, c, lo:hi], slots[use % 2][:, 0:hi - lo], ACT.Identity,
                                                 bias=cols[:, 1, c:c + 1]).then_inc(slot_free[use % 2], 1)
                    exps(b, u, 0)
                    for hp in range(PAIRS):
                        take_turn(b, hp)
                        if hp + 1 < PAIRS:
                            exps(b, u, hp + 1)
                    if scratch is None:
                        act.wait_ge(summed, b + 1)
                        nc.scalar.activation(net.actT[:, 0:KC, bass.ds(b * S, S)],
                                             outs[u][:, 256:256 + KC * S].rearrange("p (c s) -> p c s", c=KC),
                                             ACT.Copy).then_inc(bank_free, 1)


def self_attention(net, tag, width, chunks, wts, extra_bias):
    nc, d = net.nc, net.dram
    N = chunks * S
    names = ("w_in tab_in xb_ready proj_full rot q_ready k_ready v_full v_ready s_full soft p_ready turned "
             "pt_ready o_full chain o_ready summed act_done zeroed bias_ready")
    with ExitStack() as mem, stage(nc, names) as (
            block, w_in, tab_in, xb_ready, proj_full, rot, q_ready, k_ready, v_full, v_ready, s_full, soft,
            p_ready, turned, pt_ready, o_full, chain, o_ready, summed, act_done, zeroed, bias_ready):
        F = chunks * P
        w = net.sb(tag + "_w", [P, 5, KC, F], ctx=mem)
        tabs = net.sb(tag + "_rope", [P, 2, S], ctx=mem)
        xb = net.sb(tag + "_xb", [P, 2, KC, 2, S], ctx=mem)
        rq = net.sb(tag + "_rq", [P, 4, chunks, S], ctx=mem)
        q2 = net.sb(tag + "_q2", [P, chunks, S], ctx=mem)
        qb = net.sb(tag + "_qb", [P, chunks, 2, S], ctx=mem)
        kT = net.sb(tag + "_kT", [P, chunks, S], ctx=mem)
        v2 = net.sb(tag + "_v", [P, F], ctx=mem)
        bias = net.sb(tag + "_bias", [P, PAIRS, S], ctx=mem)
        slopes = net.sb(tag + "_slopes", [P, PAIRS], ctx=mem)
        dist = net.sb(tag + "_dist", [P, S], ctx=mem)
        sc = net.sb(tag + "_s", [P, PAIRS, S], ctx=mem)
        mx = net.sb(tag + "_mx", [P, PAIRS], ctx=mem)
        sums = net.sb(tag + "_sum", [P, PAIRS], ctx=mem)
        rs = net.sb(tag + "_rs", [P, PAIRS], ctx=mem)
        pT = net.sb(tag + "_pT", [P, PAIRS // 2, P], ctx=mem)
        o_bd = net.sb(tag + "_o", [P, PAIRS, 2, width // 2], ctx=mem)
        rope_ps = [net.bank(i)[:, 0:N].rearrange("p (c s) -> p c s", s=S) for i in range(4)]
        v_ps = net.ps[2]
        s_ps, t_ps = net.bank(6), net.bank(7)
        o_ps, a_ps = net.ps[0], net.bank(2)

        @block.sync
        def _(sp):
            for n, name in enumerate(wts):
                sp.dma_start(w[:, n], d[name].rearrange("(c p) n -> p c n", p=P)).then_inc(w_in, 16)
            sp.dma_start(tabs[:], d[tag + "_rope"]).then_inc(tab_in, 16)
            sp.dma_start(dist[:], d[tag + "_dist"]).then_inc(tab_in, 16)
            if extra_bias == "alibi":
                for e in range(2):
                    sp.dma_start(slopes[e * S:(e + 1) * S, :], spread(d["slopes"][e:e + 1], (S, PAIRS))).then_inc(tab_in, 16)

        @block.gpsimd
        def _(pool):
            nc.gpsimd.memset(o_bd[:], 0.0).then_inc(zeroed, 1)
            with pool.Fori(0, B // 2) as i:
                for u in range(2):
                    b = 2 * i + u
                    pool.wait_ge(v_full, 1 + b)
                    for c in range(2):
                        nc.gpsimd.tensor_copy(xb[:, u, :, c, :], net.xnT[:, :, bass.ds(b * S, S)]).then_inc(xb_ready, 1)

        @block.tensor
        def _(pe):
            pe.wait_ge(w_in, 80)
            with pe.Fori(0, B // 2) as i:
                for u in range(2):
                    b = 2 * i + u
                    pe.wait_ge(xb_ready, 2 * b + 2)
                    pe.wait_ge(act_done, b + 1)
                    for n in range(4):
                        for c in range(chunks):
                            for k in range(KC):
                                last = nc.tensor.matmul(rope_ps[n][:, c], w[:, n, k, c * P:(c + 1) * P],
                                                        xb[:, u, k, 0, :], start=(k == 0), stop=(k == KC - 1))
                        last.then_inc(proj_full, 1)
                    for h in range(0, F, HALF):
                        z = min(h + HALF, F)
                        for k in range(KC):
                            last = nc.tensor.matmul(v_ps[:, h:z], xb[:, u, k], w[:, 4, k, h:z],
                                                    start=(k == 0), stop=(k == KC - 1))
                    last.then_inc(v_full, 1)
                    pe.wait_ge(q_ready, 2 * b + 2)
                    pe.wait_ge(k_ready, b + 1)
                    for hp in range(PAIRS):
                        c, r = hp * width // P, hp * width % P
                        dst = s_ps[:, hp * S:(hp + 1) * S] if width == P else net.bank(r // width)[:, c * S:(c + 1) * S]
                        last = nc.tensor.matmul(dst, qb[r:r + width, c], kT[r:r + width, c],
                                                start=True, stop=True)
                    last.then_inc(s_full, 1)
                    pe.wait_ge(p_ready, b + 1)
                    for j in range(PAIRS // 2):
                        last = nc.tensor.transpose(t_ps[:, j * P:(j + 1) * P],
                                                   sc[:, 2 * j:2 * j + 2].rearrange("p h s -> p (h s)"), net.ident[:])
                    last.then_inc(turned, 1)
                    pe.wait_ge(pt_ready, b + 1)
                    pe.wait_ge(v_ready, b + 1)
                    for hp in range(PAIRS):
                        r = S * (hp % 2)
                        at = (hp % 2) * 512 + (hp // 2) * width
                        last = nc.tensor.matmul(o_ps[:, at:at + width], pT[r:r + S, hp // 2],
                                                v2[r:r + S, hp * width:(hp + 1) * width], start=True, stop=True)
                    last.then_inc(o_full, 1)
                    pe.wait_ge(o_ready, 2 * b + 2)
                    flat = o_bd[:].rearrange("p h e f -> p (h e f)")
                    for c in range(chunks):
                        last = nc.tensor.matmul(a_ps[:, c * S:(c + 1) * S], flat[:, c * P:(c + 1) * P], net.stack2[:],
                                                start=True, stop=True)
                    last.then_inc(summed, 1)

        @block.vector
        def _(dve):
            dve.sem_inc(act_done, 1)
            dve.sem_inc(v_full, 2)
            dve.wait_ge(tab_in, 64 if extra_bias == "alibi" else 32)
            dve.wait_ge(zeroed, 1)
            for hp in range(PAIRS):
                if extra_bias == "alibi":
                    nc.vector.tensor_scalar(bias[:, hp], dist[:], slopes[:, hp:hp + 1], None, ALU.mult).then_inc(bias_ready, 1)
                else:
                    nc.vector.tensor_copy(bias[:, hp], dist[:]).then_inc(bias_ready, 1)
            with dve.Fori(0, B) as b:
                for n in range(4):
                    dve.wait_ge(proj_full, 4 * b + n + 1)
                    nc.vector.tensor_tensor(rq[:, n], rope_ps[n], spread(tabs[:, n % 2:n % 2 + 1], (P, chunks, S)),
                                            ALU.mult).then_inc(rot, 1)
                dve.wait_ge(rot, 5 * b + 4)
                nc.vector.tensor_tensor(q2[:], rq[:, 0], rq[:, 1], ALU.add).then_inc(rot, 1)
                nc.vector.tensor_tensor(kT[:], rq[:, 2], rq[:, 3], ALU.add).then_inc(k_ready, 1)
                dve.wait_ge(s_full, b + 1)
                dve.wait_ge(bias_ready, PAIRS)
                if width == P:
                    nc.vector.tensor_tensor(sc[:], s_ps.rearrange("p (h s) -> p h s", s=S), bias[:],
                                            ALU.add).then_inc(chain, 2)
                else:
                    for t in range(2):
                        s4 = net.ps[t][:].rearrange("p (j n) -> p j n", j=2)[:, :, 0:chunks * S]
                        sel = [z.rearrange("p (c t j) s -> p t j c s", c=chunks, t=2)[:, t] for z in (sc[:], bias[:])]
                        nc.vector.tensor_tensor(sel[0], s4.rearrange("p j (c s) -> p j c s", s=S), sel[1],
                                                ALU.add).then_inc(chain, 1)
                dve.wait_ge(chain, 5 * b + 2)
                nc.vector.tensor_reduce(mx[:], sc[:], AX.X, ALU.max).then_inc(chain, 1)
                dve.wait_ge(chain, 5 * b + 3)
                nc.vector.tensor_tensor(sc[:], sc[:], spread(mx[:].unsqueeze(2), (P, PAIRS, S)), ALU.subtract).then_inc(soft, 1)
                dve.wait_ge(p_ready, b + 1)
                nc.vector.tensor_reduce(sums[:], sc[:], AX.X, ALU.add).then_inc(chain, 1)
                dve.wait_ge(chain, 5 * b + 4)
                nc.vector.reciprocal(rs[:], sums[:]).then_inc(chain, 1)
                dve.wait_ge(turned, b + 1)
                nc.vector.tensor_copy(pT[:].rearrange("p j n -> p (j n)"), t_ps).then_inc(pt_ready, 1)
                dve.wait_ge(chain, 5 * b + 5)
                dve.wait_ge(o_full, b + 1)
                o5 = o_ps[:].rearrange("p (b n) -> p b n", b=2)[:, :, 0:4 * width]\
                    .rearrange("p b (j e f) -> p b j e f", j=4, e=2)
                bd = o_bd[:].rearrange("p (j b) e f -> p b j e f", b=2)
                r5 = rs[:].rearrange("p (j b) -> p b j", b=2)
                for e in range(2):
                    r = slice(e * S, (e + 1) * S)
                    nc.vector.tensor_tensor(bd[r, :, :, e, :], o5[r, :, :, e, :],
                                            spread(r5[r].unsqueeze(3), (S, 2, 4, width // 2)), ALU.mult).then_inc(o_ready, 1)

        @block.scalar
        def _(act):
            with act.Fori(0, B) as b:
                act.wait_ge(rot, 5 * b + 5)
                for e in range(2):
                    nc.scalar.activation(qb[:, :, e, :], q2[:], ACT.Copy,
                                         scale=net.parity[:, 2 * (width // P) + e:2 * (width // P) + e + 1]).then_inc(q_ready, 1)
                act.wait_ge(v_full, b + 3)
                nc.scalar.activation(v2[:], v_ps[:, 0:F], ACT.Copy).then_inc(v_ready, 1)
                act.wait_ge(soft, b + 1)
                nc.scalar.activation(sc[:], sc[:], ACT.Exp).then_inc(p_ready, 1)
                act.wait_ge(summed, b + 1)
                nc.scalar.activation(net.actT[:, 0:chunks, bass.ds(b * S, S)],
                                     a_ps[:, 0:N].rearrange("p (c s) -> p c s", s=S), ACT.Copy).then_inc(act_done, 1)


def causal_attention(net, tag):
    nc, d = net.nc, net.dram
    names = "w_in xb_ready qk_full qk_ready v_full v_ready s_full chain p_ready turned pt_ready o_full added"
    with ExitStack() as mem, stage(nc, names) as (
            block, w_in, xb_ready, qk_full, qk_ready, v_full, v_ready, s_full, chain, p_ready, turned, pt_ready,
            o_full, added):
        w = net.sb(tag + "_w", [P, 3, KC, D], ctx=mem)
        cols = net.sb(tag + "_cols", [P, 2, KC], ctx=mem)
        bvb = net.sb(tag + "_bv", [P, D], ctx=mem)
        mask = net.sb(tag + "_mask", [P, P], ctx=mem)
        xb = net.sb(tag + "_xb", [P, KC, P], ctx=mem)
        qk = net.sb(tag + "_qk", [P, 2, KC, P], ctx=mem)
        v = net.sb(tag + "_v", [P, D], ctx=mem)
        sc = net.sb(tag + "_s", [P, P], ctx=mem)
        negmax = net.sb(tag + "_nm", [P, 1], ctx=mem)
        total = net.sb(tag + "_sum", [P, 2], ctx=mem)
        pT = net.sb(tag + "_pT", [P, P], ctx=mem)

        @block.sync
        def _(sp):
            for n, name in enumerate(("L3_attn_Wq", "L3_attn_Wk", "L3_attn_Wv")):
                sp.dma_start(w[:, n], d[name].rearrange("(c p) n -> p c n", p=P)).then_inc(w_in, 16)
            sp.dma_start(cols[:, 0], d["L3_attn_bq"]).then_inc(w_in, 16)
            sp.dma_start(cols[:, 1], d["L3_attn_bk"]).then_inc(w_in, 16)
            sp.dma_start(bvb[:], spread(d["L3_attn_bv"], (P, D))).then_inc(w_in, 16)
            sp.dma_start(mask[:], d["causal"]).then_inc(w_in, 16)

        @block.gpsimd
        def _(pool):
            with pool.Fori(0, TILES) as t:
                pool.wait_ge(v_full, t + 1)
                nc.gpsimd.tensor_copy(xb[:], net.xnT[:, :, bass.ds(t * P, P)]).then_inc(xb_ready, 1)

        @block.tensor
        def _(pe):
            pe.wait_ge(w_in, 112)
            with pe.Fori(0, TILES) as t:
                pe.wait_ge(xb_ready, t + 1)
                pe.wait_ge(added, t + 1)
                for n in range(2):
                    for c in range(KC):
                        for k in range(KC):
                            last = nc.tensor.matmul(net.bank(n)[:, c * P:(c + 1) * P], w[:, n, k, c * P:(c + 1) * P],
                                                    xb[:, k], start=(k == 0), stop=(k == KC - 1))
                    last.then_inc(qk_full, 1)
                for k in range(KC):
                    last = nc.tensor.matmul(net.bank(2)[:, 0:D], xb[:, k], w[:, 2, k], start=(k == 0), stop=(k == KC - 1))
                last.then_inc(v_full, 1)
                pe.wait_ge(qk_ready, 4 * t + 4)
                for k in range(KC):
                    last = nc.tensor.matmul(net.bank(3)[:, 0:P], qk[:, 0, k], qk[:, 1, k], start=(k == 0), stop=(k == KC - 1))
                last.then_inc(s_full, 1)
                pe.wait_ge(p_ready, t + 1)
                nc.tensor.transpose(net.bank(4)[:, 0:P], sc[:], net.ident[:]).then_inc(turned, 1)
                pe.wait_ge(pt_ready, t + 1)
                pe.wait_ge(v_ready, t + 1)
                nc.tensor.matmul(net.bank(5)[:, 0:D], pT[:], v[:], start=True, stop=True).then_inc(o_full, 1)

        @block.vector
        def _(dve):
            dve.sem_inc(added, 1)
            dve.sem_inc(v_full, 1)
            dve.wait_ge(w_in, 112)
            with dve.Fori(0, TILES) as t:
                dve.wait_ge(v_full, t + 2)
                nc.vector.tensor_tensor(v[:], net.bank(2)[:, 0:D], bvb[:], ALU.add).then_inc(v_ready, 1)
                dve.wait_ge(s_full, t + 1)
                nc.vector.scalar_tensor_tensor(sc[:], net.bank(3)[:, 0:P], float(D) ** -0.5, mask[:], ALU.mult,
                                               ALU.add).then_inc(chain, 1)
                dve.wait_ge(chain, 3 * t + 1)
                nc.vector.tensor_reduce(negmax[:], sc[:], AX.X, ALU.max, negate=True).then_inc(chain, 1)
                dve.wait_ge(p_ready, t + 1)
                nc.vector.reciprocal(total[:, 1:2], total[:, 0:1]).then_inc(chain, 1)
                dve.wait_ge(turned, t + 1)
                nc.vector.tensor_copy(pT[:], net.bank(4)[:, 0:P]).then_inc(pt_ready, 1)
                dve.wait_ge(o_full, t + 1)
                dve.wait_ge(chain, 3 * t + 3)
                xt = net.x[:, bass.ds(t, 1), :].rearrange("p o n -> p (o n)")
                nc.vector.scalar_tensor_tensor(xt, net.bank(5)[:, 0:D], total[:, 1:2], xt, ALU.mult,
                                               ALU.add).then_inc(added, 1)

        @block.scalar
        def _(act):
            act.wait_ge(w_in, 112)
            with act.Fori(0, TILES) as t:
                for n in range(2):
                    act.wait_ge(qk_full, 2 * t + n + 1)
                    for c in range(KC):
                        nc.scalar.activation(qk[:, n, c], net.bank(n)[:, c * P:(c + 1) * P], ACT.Identity,
                                             bias=cols[:, n, c:c + 1]).then_inc(qk_ready, 1)
                act.wait_ge(chain, 3 * t + 2)
                nc.scalar.activation(sc[:], sc[:], ACT.Exp, bias=negmax[:, 0:1],
                                     accum_out=total[:, 0:1]).then_inc(p_ready, 1)


def rank_below(nc, dve, link, gt, eq, vals, tri, rank, n):
    shape = (P, TILES * n * n)
    for t in range(TILES):
        a = spread(vals[:, t, :].unsqueeze(1), (P, n, n))
        b = spread(vals[:, t, :].unsqueeze(2), (P, n, n))
        nc.vector.tensor_tensor(gt[:, t], a, b, ALU.is_gt)
        link(nc.vector.tensor_tensor(eq[:, t], a, b, ALU.is_equal))
    for t in range(TILES):
        link(nc.vector.tensor_tensor(eq[:, t], eq[:, t], tri, ALU.mult))
    link(nc.vector.tensor_tensor(gt.rearrange("p t i j -> p (t i j)"), gt.rearrange("p t i j -> p (t i j)"),
                                 eq.rearrange("p t i j -> p (t i j)"), ALU.add))
    link(nc.vector.tensor_reduce(rank, gt.rearrange("p t i j -> p (t i) j"), AX.X, ALU.add))


def route_groups(net, tag, rwT):
    nc, d = net.nc, net.dram
    E, G, K = 64, 8, 8
    with ExitStack() as mem, stage(nc, "w_in logits sig chain rw_ready turned ones_set") as (
            block, w_in, logits, sig, chain, rw_ready, turned, ones_set):
        w = net.sb(tag + "_gw", [P, KC, E], ctx=mem)
        gb = net.sb(tag + "_gb", [P, E], ctx=mem)
        tri = net.sb(tag + "_tri", [P, G, G], ctx=mem)
        score = net.sb(tag + "_score", [P, TILES, E], ctx=mem)
        choice = net.sb(tag + "_choice", [P, TILES, E], ctx=mem)
        top = net.sb(tag + "_top", [P, TILES, G, 8], ctx=mem)
        gs = net.sb(tag + "_gs", [P, TILES, G], ctx=mem)
        gt = net.sb(tag + "_gt", [P, TILES, G, G], ctx=mem)
        eq = net.sb(tag + "_eq", [P, TILES, G, G], ctx=mem)
        rank = net.sb(tag + "_rank", [P, TILES, G], ctx=mem)
        best = net.sb(tag + "_best", [P, TILES, K], ctx=mem)
        left = net.sb(tag + "_left", [P, TILES, E], ctx=mem)
        tot = net.sb(tag + "_tot", [P, TILES], ctx=mem)

        @block.sync
        def _(sp):
            sp.dma_start(w[:], d["gate_wT"].rearrange("(c p) n -> p c n", p=P)).then_inc(w_in, 16)
            sp.dma_start(gb[:], spread(d["gate_bias"], (P, E))).then_inc(w_in, 16)
            sp.dma_start(tri[:], spread(d["tri8"].unsqueeze(0), (P, G, G))).then_inc(w_in, 16)

        @block.tensor
        def _(pe):
            pe.wait_ge(w_in, 48)
            for t in range(TILES):
                for k in range(KC):
                    last = nc.tensor.matmul(net.bank(0)[:, t * E:(t + 1) * E], net.xnT[:, k, t * P:(t + 1) * P], w[:, k],
                                            start=(k == 0), stop=(k == KC - 1))
            last.then_inc(logits, 1)
            pe.wait_ge(rw_ready, 1)
            for t in range(TILES):
                last = nc.tensor.transpose(net.bank(1 + t // 4)[0:E, (t % 4) * P:(t % 4 + 1) * P], score[:, t],
                                           net.ident[:])
            last.then_inc(turned, 1)

        @block.scalar
        def _(act):
            act.wait_ge(logits, 1)
            nc.scalar.activation(score[:].rearrange("p t e -> p (t e)"), net.bank(0), ACT.Sigmoid).then_inc(sig, 1)

        @block.vector
        def _(dve):
            done = [0]

            def link(ins):
                done[0] += 1
                ins.then_inc(chain, 1)
                dve.wait_ge(chain, done[0])

            nc.vector.memset(rwT[E:E + 1, :], 1.0).then_inc(ones_set, 1)
            dve.wait_ge(w_in, 48)
            dve.wait_ge(sig, 1)
            link(nc.vector.tensor_tensor(choice[:], score[:], spread(gb[:].unsqueeze(1), (P, TILES, E)), ALU.add))
            for t in range(TILES):
                for g in range(G):
                    ins = nc.vector.max(top[:, t, g], choice[:, t, g * 8:(g + 1) * 8])
            link(ins)
            link(nc.vector.tensor_tensor(gs[:], top[:, :, :, 0], top[:, :, :, 1], ALU.add))
            rank_below(nc, dve, link, gt[:], eq[:], gs, tri[:], rank[:].rearrange("p t g -> p (t g)"), G)
            link(nc.vector.tensor_scalar(gs[:], rank[:], 4.0, None, ALU.is_lt))
            link(nc.vector.tensor_tensor(choice[:].rearrange("p t (g e) -> p (t g) e", g=G),
                                         choice[:].rearrange("p t (g e) -> p (t g) e", g=G),
                                         spread(gs[:].rearrange("p t g -> p (t g)").unsqueeze(2), (P, TILES * G, 8)),
                                         ALU.mult))
            for t in range(TILES):
                ins = nc.vector.max(best[:, t], choice[:, t])
            link(ins)
            for t in range(TILES):
                ins = nc.vector.match_replace(left[:, t], best[:, t], choice[:, t], -3e38)
            link(ins)
            link(nc.vector.tensor_scalar(left[:], left[:], -3e38, None, ALU.is_equal))
            link(nc.vector.tensor_tensor(score[:], score[:], left[:], ALU.mult))
            link(nc.vector.tensor_reduce(tot[:], score[:], AX.X, ALU.add))
            link(nc.vector.tensor_scalar(tot[:], tot[:], 1e-20, None, ALU.add))
            link(nc.vector.reciprocal(tot[:], tot[:]))
            link(nc.vector.tensor_tensor(score[:], score[:], spread(tot[:].unsqueeze(2), (P, TILES, E)), ALU.mult))
            nc.vector.tensor_scalar(score[:], score[:], 2.5, None, ALU.mult).then_inc(rw_ready, 1)
            dve.wait_ge(turned, 1)
            for h in range(2):
                nc.vector.tensor_copy(rwT[0:E, h * HALF:(h + 1) * HALF], net.bank(1 + h)[0:E, :]).then_inc(ones_set, 1)
            dve.wait_ge(ones_set, 3)


def route_top1(net, tag, rwT):
    nc, d = net.nc, net.dram
    E = 14
    with ExitStack() as mem, stage(nc, "w_in logits ex shifted chain rw_ready turned out_ready") as (
            block, w_in, logits, ex, shifted, chain, rw_ready, turned, out_ready):
        w = net.sb(tag + "_gw", [P, KC, E], ctx=mem)
        tri = net.sb(tag + "_tri", [P, E, E], ctx=mem)
        lg = net.sb(tag + "_lg", [P, TILES, E], ctx=mem)
        pr = net.sb(tag + "_pr", [P, TILES, E], ctx=mem)
        gt = net.sb(tag + "_gt", [P, TILES, E, E], ctx=mem)
        eq = net.sb(tag + "_eq", [P, TILES, E, E], ctx=mem)
        rank = net.sb(tag + "_rank", [P, TILES, E], ctx=mem)
        tot = net.sb(tag + "_tot", [P, TILES], ctx=mem)

        @block.sync
        def _(sp):
            sp.dma_start(w[:], d["router_w"].rearrange("(c p) n -> p c n", p=P)).then_inc(w_in, 16)
            sp.dma_start(tri[:], spread(d["tri14"].unsqueeze(0), (P, E, E))).then_inc(w_in, 16)

        @block.tensor
        def _(pe):
            pe.wait_ge(w_in, 32)
            for t in range(TILES):
                for k in range(KC):
                    last = nc.tensor.matmul(net.bank(0)[:, t * E:(t + 1) * E], net.xnT[:, k, t * P:(t + 1) * P], w[:, k],
                                            start=(k == 0), stop=(k == KC - 1))
            last.then_inc(logits, 1)
            pe.wait_ge(rw_ready, 1)
            for t in range(TILES):
                last = nc.tensor.transpose(net.bank(1 + t // 4)[0:E, (t % 4) * P:(t % 4 + 1) * P], pr[:, t],
                                           net.ident[:])
            last.then_inc(turned, 1)

        @block.scalar
        def _(act):
            act.wait_ge(shifted, 1)
            nc.scalar.activation(pr[:], pr[:], ACT.Exp).then_inc(ex, 1)

        @block.vector
        def _(dve):
            done = [0]

            def link(ins):
                done[0] += 1
                ins.then_inc(chain, 1)
                dve.wait_ge(chain, done[0])

            dve.wait_ge(w_in, 32)
            dve.wait_ge(logits, 1)
            link(nc.vector.tensor_copy(lg[:].rearrange("p t e -> p (t e)"), net.bank(0)[:, 0:TILES * E]))
            link(nc.vector.tensor_reduce(tot[:], lg[:], AX.X, ALU.max))
            nc.vector.tensor_tensor(pr[:], lg[:], spread(tot[:].unsqueeze(2), (P, TILES, E)),
                                    ALU.subtract).then_inc(shifted, 1)
            rank_below(nc, dve, link, gt[:], eq[:], lg, tri[:], rank[:].rearrange("p t g -> p (t g)"), E)
            link(nc.vector.tensor_scalar(rank[:], rank[:], 0.5, None, ALU.is_lt))
            dve.wait_ge(ex, 1)
            link(nc.vector.tensor_reduce(tot[:], pr[:], AX.X, ALU.add))
            link(nc.vector.reciprocal(tot[:], tot[:]))
            link(nc.vector.tensor_tensor(pr[:], pr[:], rank[:], ALU.mult))
            nc.vector.tensor_tensor(pr[:], pr[:], spread(tot[:].unsqueeze(2), (P, TILES, E)),
                                    ALU.mult).then_inc(rw_ready, 1)
            dve.wait_ge(turned, 1)
            for h in range(2):
                nc.vector.tensor_copy(rwT[0:E, h * HALF:(h + 1) * HALF], net.bank(1 + h)[0:E, :]).then_inc(out_ready, 1)
            dve.wait_ge(out_ready, 2)


def experts(net, tag, packed, tiles, rows, rwT, b2, gated):
    nc, d = net.nc, net.dram
    KINDS = 3 if gated else 2
    UNITS = 4
    WIDTH = d[packed].shape[2]
    o_u = 2 * P if gated else 0
    o_d = o_u + 2 * P
    o_s = o_d + D
    names = "w_in0 w_in1 b2_in ring_full act_done up_done h_ready down_done added"
    with ExitStack() as mem, stage(nc, names) as (
            block, w_in0, w_in1, b2_in, ring_full, act_done, up_done, h_ready, down_done, added):
        w_in = (w_in0, w_in1)
        w = net.sb(tag + "_w", [P, 2, WIDTH], ctx=mem)
        b2s = net.sb(tag + "_b2", [P, D], ctx=mem)
        g = net.sb(tag + "_g", [P, 2, HALF], ctx=mem)
        gu = net.sb(tag + "_gu", [P, 2, HALF], ctx=mem)
        h = net.sb(tag + "_h", [P, 2, HALF], ctx=mem)
        ring = [net.bank(j) for j in range(4)]
        acc = [net.ps[2 + t // 4][:, (t % 4) * D:(t % 4 + 1) * D] for t in range(TILES)]

        @block.sync
        def _(sp):
            sp.dma_start(b2s[0:rows, :], d[b2]).then_inc(b2_in, 16)
            for u in range(2):
                sp.dma_start(w[:, u], d[packed][u]).then_inc(w_in[u], 16)
            with sp.Fori(0, tiles // 2 - 1) as i:
                for u in range(2):
                    sp.wait_ge(down_done, 2 + 2 * (2 * i + u + 1))
                    sp.dma_start(w[:, u], d[packed][bass.ds(2 * i + 2 + u, 1)].rearrange("o p n -> p (o n)")).then_inc(w_in[u], 16)

        @block.tensor
        def _(pe):
            pe.wait_ge(b2_in, 16)
            for t in range(TILES):
                nc.tensor.matmul(acc[t], rwT[0:rows, t * P:(t + 1) * P], b2s[0:rows, :], start=(t % 2 == 0), stop=False,
                                 skip_group_check=True)

            def down(i, n):
                u, half = n // 2, n % 2
                pe.wait_ge(h_ready, 2 + UNITS * i + n + 1)
                for t in range(4):
                    last = nc.tensor.matmul(acc[4 * half + t], h[:, n % 2, t * P:(t + 1) * P], w[:, u, o_d:o_d + D],
                                            start=False, stop=False, skip_group_check=True)
                last.then_inc(down_done, 1)

            with pe.Fori(0, tiles // 2) as i:
                for n in range(UNITS):
                    u, half = n // 2, n % 2
                    if half == 0:
                        pe.wait_ge(w_in[u], 16 * i + 16)
                    tok = slice(half * HALF, (half + 1) * HALF)
                    for j in range(KINDS):
                        q = KINDS * n + j
                        unit = UNITS * i + n
                        if not gated:
                            pe.wait_ge((act_done, h_ready)[j], unit + 1)
                        elif j == 0:
                            pe.wait_ge(h_ready, unit + 1)
                        else:
                            pe.wait_ge((act_done, up_done)[j - 1], unit + 2)
                        if j < KINDS - 1:
                            for k in range(KC):
                                at = (o_u if j else 0) + k * P
                                last = nc.tensor.matmul(ring[q % 4], w[:, u, at:at + P], net.xnT[:, k, tok],
                                                        start=(k == 0), stop=(k == KC - 1))
                        else:
                            last = nc.tensor.matmul(ring[q % 4], w[0:rows, u, o_s:o_s + P], rwT[0:rows, tok],
                                                    start=True, stop=True)
                        last.then_inc(ring_full, 1)
                    if n:
                        down(i, n - 1)
                down(i, UNITS - 1)

        @block.vector
        def _(dve):
            dve.sem_inc(act_done, 2)
            dve.sem_inc(up_done, 2)
            dve.sem_inc(h_ready, 2)
            dve.sem_inc(down_done, 2)
            with dve.Fori(0, tiles // 2) as i:
                for n in range(UNITS):
                    src = g
                    dve.wait_ge(act_done, 2 + UNITS * i + n + 1)
                    if gated:
                        q = KINDS * n + 1
                        dve.wait_ge(ring_full, UNITS * KINDS * i + q + 1)
                        nc.vector.tensor_tensor(gu[:, n % 2], g[:, n % 2], ring[q % 4], ALU.mult).then_inc(up_done, 1)
                        dve.wait_ge(up_done, 2 + UNITS * i + n + 1)
                        src = gu
                    q = KINDS * n + KINDS - 1
                    dve.wait_ge(ring_full, UNITS * KINDS * i + q + 1)
                    dve.wait_ge(down_done, UNITS * i + n + 1)
                    nc.vector.tensor_tensor(h[:, n % 2], src[:, n % 2], ring[q % 4], ALU.mult).then_inc(h_ready, 1)
            dve.wait_ge(down_done, 2 + 2 * tiles)
            for t in range(TILES):
                nc.vector.tensor_tensor(net.x[:, t, :], net.x[:, t, :], acc[t], ALU.add).then_inc(added, 1)

        @block.scalar
        def _(act):
            with act.Fori(0, tiles // 2) as i:
                for n in range(UNITS):
                    q = KINDS * n
                    act.wait_ge(ring_full, UNITS * KINDS * i + q + 1)
                    act.wait_ge(h_ready, UNITS * i + n + 1)
                    if gated:
                        ins = nc.scalar.activation(g[:, n % 2], ring[q % 4], ACT.Silu)
                    else:
                        ins = nc.scalar.activation(g[:, n % 2], ring[q % 4], ACT.Gelu, bias=w[:, n // 2, o_s + P:o_s + P + 1])
                    ins.then_inc(act_done, 1)


def hidden_tiles(net, pe, made, taken, product):
    for n in range(16):
        if n >= 8:
            pe.wait_ge(taken, n - 7)
        product(n // 2, slice((n % 2) * HALF, (n % 2 + 1) * HALF), net.bank(n % 8)).then_inc(made, 1)


def ternary(net, tag, name, tiles, cols, out):
    nc, d = net.nc, net.dram
    MAGIC = 12582912.0
    with ExitStack() as mem, stage(nc, "w_in chain ready turned taken") as (block, w_in, chain, ready, turned, taken):
        w = net.sb(tag + "_raw", [P, tiles, cols], ctx=mem)
        q = net.sb(tag + "_q", [P, tiles, cols], ctx=mem)
        sc = net.sb(tag + "_sc", [P, tiles], ctx=mem)
        rs = net.sb(tag + "_rs", [P, tiles], ctx=mem)

        @block.sync
        def _(sp):
            sp.dma_start(w[:], d[name].rearrange("(t p) n -> p t n", p=P)).then_inc(w_in, 16)

        @block.vector
        def _(dve):
            done = [0]

            def link(ins):
                done[0] += 1
                ins.then_inc(chain, 1)
                dve.wait_ge(chain, done[0])

            dve.wait_ge(w_in, 16)
            link(nc.vector.tensor_reduce(sc[:], w[:], AX.X, ALU.add, apply_absolute_value=True))
            link(nc.vector.tensor_scalar(sc[:], sc[:], 1.0 / cols, 1e-5, ALU.mult, ALU.max))
            link(nc.vector.reciprocal(rs[:], sc[:]))
            for t in range(tiles):
                ins = nc.vector.tensor_scalar(q[:, t], w[:, t], rs[:, t:t + 1], 2.0, ALU.mult, ALU.min)
            link(ins)
            link(nc.vector.tensor_scalar(q[:], q[:], -2.0, MAGIC, ALU.max, ALU.add))
            link(nc.vector.tensor_scalar(q[:], q[:], -MAGIC, 1.0, ALU.add, ALU.min))
            link(nc.vector.scalar_tensor_tensor(q[:], q[:], -1.0, w[:], ALU.max, ALU.subtract))
            link(nc.vector.tensor_tensor(q[:], q[:], w[:], ALU.add))
            for t in range(tiles):
                nc.vector.tensor_scalar(q[:, t], q[:, t], sc[:, t:t + 1], None, ALU.mult).then_inc(ready, 1)

        @block.tensor
        def _(pe):
            for c in range(cols // P):
                for h in range(0, tiles, 4):
                    n = c * -(-tiles // 4) + h // 4
                    pe.wait_ge(ready, min(h + 4, tiles))
                    if n >= 8:
                        pe.wait_ge(taken, n - 7)
                    for t in range(h, min(h + 4, tiles)):
                        last = nc.tensor.transpose(net.bank(n % 8)[:, (t - h) * P:(t - h + 1) * P],
                                                   q[:, t, c * P:(c + 1) * P], net.ident[:])
                    last.then_inc(turned, 1)

        @block.scalar
        def _(act):
            for c in range(cols // P):
                for h in range(0, tiles, 4):
                    n = c * -(-tiles // 4) + h // 4
                    z = min(h + 4, tiles)
                    act.wait_ge(turned, n + 1)
                    nc.scalar.activation(out[:, c, h * P:z * P], net.bank(n % 8)[:, 0:(z - h) * P], ACT.Copy).then_inc(taken, 1)


def bit_hidden(net, tag, wfcT):
    nc, d = net.nc, net.dram
    R = 16
    with ExitStack() as mem, stage(nc, "w_in low low_taken made relu_done squared") as (
            block, w_in, low, low_taken, made, relu_done, squared):
        vT = net.sb(tag + "_v", [P, KC, R], ctx=mem)
        fbT = net.sb(tag + "_fb", [R, R], ctx=mem)
        uT = net.sb(tag + "_u", [R, 1024], ctx=mem)
        gate = net.sb(tag + "_gate", [R, 1], ctx=mem)
        t1 = net.sb(tag + "_t1", [R, TOK], ctx=mem)
        t2 = net.sb(tag + "_t2", [R, TOK], ctx=mem)
        r = net.sb(tag + "_r", [P, 2, HALF], ctx=mem)

        @block.sync
        def _(sp):
            sp.dma_start(vT[:], d["L1_ffn_vT"].rearrange("(c p) n -> p c n", p=P)).then_inc(w_in, 16)
            sp.dma_start(fbT[:], d["L1_ffn_fbT"]).then_inc(w_in, 16)
            sp.dma_start(uT[:], d["L1_ffn_uT"]).then_inc(w_in, 16)
            sp.dma_start(gate[:], spread(d["L1_ffn_gate"], (R, 1))).then_inc(w_in, 16)

        @block.tensor
        def _(pe):
            pe.wait_ge(w_in, 64)
            for h in range(2):
                for k in range(KC):
                    last = nc.tensor.matmul(net.bank(h)[0:R, :], vT[:, k], net.xnT[:, k, h * HALF:(h + 1) * HALF],
                                            start=(k == 0), stop=(k == KC - 1))
                last.then_inc(low, 1)
            for h in range(2):
                pe.wait_ge(low_taken, h + 1)
                nc.tensor.matmul(net.bank(2 + h)[0:R, :], fbT[:], t1[:, h * HALF:(h + 1) * HALF], start=True,
                                 stop=True).then_inc(low, 1)
            pe.wait_ge(low_taken, 4)

            def product(c, tok, bank):
                for k in range(KC):
                    nc.tensor.matmul(bank, wfcT[:, k, c * P:(c + 1) * P], net.xnT[:, k, tok], start=(k == 0), stop=False)
                return nc.tensor.matmul(bank, uT[:, c * P:(c + 1) * P], t2[:, tok], start=False, stop=True)
            hidden_tiles(net, pe, made, relu_done, product)

        @block.scalar
        def _(act):
            for n in range(16):
                act.wait_ge(made, n + 1)
                if n >= 2:
                    act.wait_ge(squared, n - 1)
                nc.scalar.activation(r[:, n % 2], net.bank(n % 8), ACT.Relu).then_inc(relu_done, 1)

        @block.vector
        def _(dve):
            for h in range(2):
                dve.wait_ge(low, h + 1)
                nc.vector.tensor_copy(t1[:, h * HALF:(h + 1) * HALF], net.bank(h)[0:R, :]).then_inc(low_taken, 1)
            dve.wait_ge(w_in, 64)
            for h in range(2):
                dve.wait_ge(low, h + 3)
                nc.vector.tensor_scalar(t2[:, h * HALF:(h + 1) * HALF], net.bank(2 + h)[0:R, :], gate[:, 0:1], None,
                                        ALU.mult).then_inc(low_taken, 1)
            for n in range(16):
                dve.wait_ge(relu_done, n + 1)
                nc.vector.tensor_tensor(net.actT[:, n // 2, (n % 2) * HALF:(n % 2 + 1) * HALF], r[:, n % 2], r[:, n % 2],
                                        ALU.mult).then_inc(squared, 1)


def scan_mixer(net, tag, y):
    nc, d = net.nc, net.dram
    names = "w_in made taken chain pchain u_ready p_ready out_ready turned y_taken"
    with ExitStack() as mem, stage(nc, names) as (
            block, w_in, made, taken, chain, pchain, u_ready, p_ready, out_ready, turned, y_taken):
        w = net.sb(tag + "_w", [P, KC, 6 * P], ctx=mem)
        bcols = net.sb(tag + "_b", [P, 6], ctx=mem)
        lb = net.sb(tag + "_lb", [P, 2], ctx=mem)
        olb = net.sb(tag + "_olb", [P, 2], ctx=mem)
        lam = net.sb(tag + "_lam", [P, 2, TOK], ctx=mem)
        oml = net.sb(tag + "_oml", [P, 2, TOK], ctx=mem)
        u = net.sb(tag + "_u", [P, 2, 2, TOK], ctx=mem)
        fwd = net.sb(tag + "_f", [P, 2, 2, TOK], ctx=mem)
        rev = net.sb(tag + "_r", [P, 2, 2, TOK], ctx=mem)
        tmp = net.sb(tag + "_t", [P, 2, 2, 2, S], ctx=mem)
        inp, og, fg = net.actT[:, 0:2], net.actT[:, 2:4], net.actT[:, 4:6]

        def at(buf, n):
            return buf[:, :, :, bass.ds(n * S, S)]

        def lam_at(n):
            return spread(lam[:, :, bass.ds(n * S, S)].unsqueeze(2), (P, 2, 2, S))

        @block.sync
        def _(sp):
            sp.dma_start(w[:], d["L2_attn_W_in"].rearrange("(c p) n -> p c n", p=P)).then_inc(w_in, 16)
            sp.dma_start(bcols[:], d["L2_attn_b_in"]).then_inc(w_in, 16)
            sp.dma_start(lb[:], d["L2_attn_lb"]).then_inc(w_in, 16)

        @block.tensor
        def _(pe):
            pe.wait_ge(w_in, 48)
            for n in range(12):
                if n >= 8:
                    pe.wait_ge(taken, n - 7)
                c, tok = n // 2, slice((n % 2) * HALF, (n % 2 + 1) * HALF)
                for k in range(KC):
                    last = nc.tensor.matmul(net.bank(n % 8), w[:, k, c * P:(c + 1) * P], net.xnT[:, k, tok],
                                            start=(k == 0), stop=(k == KC - 1))
                last.then_inc(made, 1)
            pe.wait_ge(out_ready, 2)
            pe.wait_ge(taken, 12)
            for t in range(TILES):
                for e in range(2):
                    last = nc.tensor.transpose(net.bank(t)[:, e * P:(e + 1) * P], oml[:, e, t * P:(t + 1) * P], net.ident[:])
                last.then_inc(turned, 1)

        @block.scalar
        def _(act):
            act.wait_ge(w_in, 48)
            for n in range(12):
                c, tok = n // 2, slice((n % 2) * HALF, (n % 2 + 1) * HALF)
                act.wait_ge(made, n + 1)
                nc.scalar.activation(net.actT[:, c, tok], net.bank(n % 8), ACT.Silu if c < 2 else ACT.Sigmoid,
                                     bias=bcols[:, c:c + 1]).then_inc(taken, 1)
            for t in range(TILES):
                act.wait_ge(turned, t + 1)
                nc.scalar.activation(y[:, t, :], net.bank(t)[:, 0:D], ACT.Copy).then_inc(y_taken, 1)

        @block.vector
        def _(dve):
            done = [0]

            def link(ins):
                done[0] += 1
                ins.then_inc(chain, 1)
                dve.wait_ge(chain, done[0])

            dve.wait_ge(w_in, 48)
            link(nc.vector.tensor_scalar(olb[:], lb[:], -1.0, 1.0, ALU.mult, ALU.add))
            dve.wait_ge(taken, 12)
            for e in range(2):
                ins = nc.vector.tensor_scalar(lam[:, e], fg[:, e], olb[:, e:e + 1], lb[:, e:e + 1], ALU.mult, ALU.add)
            link(ins)
            link(nc.vector.tensor_scalar(oml[:], lam[:], -1.0, 1.0, ALU.mult, ALU.add))
            for a in range(2):
                for e in range(2):
                    ins = nc.vector.tensor_tensor(u[:, a, e], oml[:, a], inp[:, e], ALU.mult)
            ins.then_inc(u_ready, 1)
            dve.wait_ge(u_ready, 1)
            link(nc.vector.tensor_copy(fwd[:, :, :, 0:S], u[:, :, :, 0:S]))
            base = done[0]
            with dve.Fori(1, B) as n:
                nc.vector.tensor_tensor(tmp[:, 0], lam_at(n), at(fwd, n - 1), ALU.mult).then_inc(chain, 1)
                dve.wait_ge(chain, base + 2 * n - 1)
                nc.vector.tensor_tensor(at(fwd, n), tmp[:, 0], at(u, n), ALU.add).then_inc(chain, 1)
                dve.wait_ge(chain, base + 2 * n)
            done[0] = base + 2 * (B - 1)
            dve.wait_ge(p_ready, 1)
            link(nc.vector.tensor_tensor(fwd[:], fwd[:], rev[:], ALU.add))
            for a in range(2):
                for e in range(2):
                    ins = nc.vector.tensor_tensor(u[:, a, e], fwd[:, a, e], og[:, a], ALU.mult)
            link(ins)
            for e in range(2):
                nc.vector.tensor_tensor(oml[:, e], u[:, 0, e], u[:, 1, e], ALU.add).then_inc(out_ready, 1)

        @block.gpsimd
        def _(pool):
            pool.wait_ge(u_ready, 1)
            nc.gpsimd.tensor_copy(rev[:, :, :, (B - 1) * S:], u[:, :, :, (B - 1) * S:]).then_inc(pchain, 1)
            pool.wait_ge(pchain, 1)
            with pool.Fori(0, B - 1) as i:
                n = B - 2 - i
                nc.gpsimd.tensor_tensor(tmp[:, 1], lam_at(n), at(rev, n + 1), ALU.mult).then_inc(pchain, 1)
                pool.wait_ge(pchain, 2 * i + 2)
                nc.gpsimd.tensor_tensor(at(rev, n), tmp[:, 1], at(u, n), ALU.add).then_inc(pchain, 1)
                pool.wait_ge(pchain, 2 * i + 3)
            pool.sem_inc(p_ready, 1)


def lora_hidden(net, tag, gm, e2):
    nc, d = net.nc, net.dram
    names = "w_in chain picked ev_made ev_taken e_ready c_made c_taken made taken g_made g_taken"
    R = 64
    with ExitStack() as mem, stage(nc, names) as (
            block, w_in, chain, picked, ev_made, ev_taken, e_ready, c_made, c_taken, made, taken, g_made, g_taken):
        w = net.sb(tag + "_w", [P, KC, 1024], ctx=mem)
        b1 = net.sb(tag + "_b1", [P, 8], ctx=mem)
        scale = net.sb(tag + "_scale", [R, 1], ctx=mem)
        own = net.sb(tag + "_own", [R, TOK], ctx=mem)
        m4 = net.sb(tag + "_m4", [R, 4], ctx=mem)
        pick = net.sb(tag + "_pick", [P, 4, KC, R], ctx=mem)
        ev = net.sb(tag + "_ev", [R, 2, D], ctx=mem)
        e1 = net.sb(tag + "_e1", [R, 4, D], ctx=mem)
        c1 = net.sb(tag + "_c1", [R, TOK], ctx=mem)
        FIRST = (1, 2, 9, 10)

        @block.sync
        def _(sp):
            sp.dma_start(w[:], d["L3_ffn_W1T"].rearrange("(c p) n -> p c n", p=P)).then_inc(w_in, 16)
            sp.dma_start(b1[:], d["L3_ffn_b1"]).then_inc(w_in, 16)
            sp.dma_start(scale[:], spread(d["L3_ffn_scale"], (R, 1))).then_inc(w_in, 16)
            sp.dma_start(own[:], d["own_batch"]).then_inc(w_in, 16)
            sp.dma_start(m4[:], d["m4"]).then_inc(w_in, 16)

        @block.tensor
        def _(pe):
            pe.wait_ge(picked, 8)
            for n in range(2):
                for c in range(KC):
                    last = nc.tensor.transpose(net.bank(n)[0:R, c * P:(c + 1) * P], pick[:, 2 * n, c], net.ident[:])
                last.then_inc(ev_made, 1)
            for h in range(2):
                for k in range(KC):
                    last = nc.tensor.matmul(net.bank(2 + h)[0:R, :], pick[:, 1, k], net.xnT[:, k, h * HALF:(h + 1) * HALF],
                                            start=(k == 0), stop=(k == KC - 1))
                last.then_inc(c_made, 1)
            pe.wait_ge(w_in, 80)
            pe.wait_ge(c_taken, 2)
            pe.wait_ge(e_ready, 8)

            def product(c, tok, bank):
                for k in range(KC):
                    nc.tensor.matmul(bank, w[:, k, c * P:(c + 1) * P], net.xnT[:, k, tok], start=(k == 0), stop=False)
                flat = e1[:].rearrange("p i d -> p (i d)")
                return nc.tensor.matmul(bank, flat[:, c * P:(c + 1) * P], c1[:, tok], start=False, stop=True)
            hidden_tiles(net, pe, made, taken, product)
            pe.wait_ge(taken, 16)
            for n in range(8):
                r, tok = n // 2, slice((n % 2) * HALF, (n % 2 + 1) * HALF)
                for c in range(KC):
                    last = nc.tensor.matmul(net.bank(n)[0:R, :], pick[:, 3, c], net.actT[:, 2 * r + c, tok],
                                            start=(c == 0), stop=(c == KC - 1))
                last.then_inc(g_made, 1)

        @block.scalar
        def _(act):
            act.wait_ge(w_in, 80)
            for n in range(16):
                act.wait_ge(made, n + 1)
                nc.scalar.activation(net.actT[:, n // 2, (n % 2) * HALF:(n % 2 + 1) * HALF], net.bank(n % 8), ACT.Gelu,
                                     bias=b1[:, n // 2:n // 2 + 1]).then_inc(taken, 1)

        @block.vector
        def _(dve):
            for n, first in enumerate(FIRST):
                for c in range(KC):
                    src = net.xnT[:, c].rearrange("p (b s) -> p b s", s=S)[:, :, first:first + 7:2]
                    nc.vector.tensor_copy(pick[:, n, c].rearrange("p (b i) -> p b i", i=4), src).then_inc(picked, 1)
            for n in range(2):
                dve.wait_ge(ev_made, n + 1)
                nc.vector.tensor_copy(ev[:, n], net.bank(n)[0:R, 0:D]).then_inc(ev_taken, 1)
            dve.wait_ge(w_in, 80)
            dve.wait_ge(ev_taken, 2)
            for i in range(4):
                nc.vector.tensor_scalar(e1[:, i], ev[:, 0], m4[:, i:i + 1], None, ALU.mult).then_inc(e_ready, 1)
                nc.vector.tensor_scalar(e2[:, :, i * S:(i + 1) * S], ev[:, 1].rearrange("p (j r) -> p r j", r=4),
                                        m4[:, i:i + 1], None, ALU.mult).then_inc(e_ready, 1)
            for h in range(2):
                dve.wait_ge(c_made, h + 1)
                tok = slice(h * HALF, (h + 1) * HALF)
                nc.vector.scalar_tensor_tensor(c1[:, tok], net.bank(2 + h)[0:R, :], scale[:, 0:1], own[:, tok], ALU.mult,
                                               ALU.mult).then_inc(c_taken, 1)
            for n in range(8):
                r, tok = n // 2, slice((n % 2) * HALF, (n % 2 + 1) * HALF)
                dve.wait_ge(g_made, n + 1)
                nc.vector.scalar_tensor_tensor(gm[:, r, tok], net.bank(n)[0:R, :], scale[:, 0:1], own[:, tok], ALU.mult,
                                               ALU.mult).then_inc(g_taken, 1)


def heads_reshaped(net, tag, scratch):
    nc, d = net.nc, net.dram
    with ExitStack() as mem, stage(nc, "loaded turned taken") as (block, loaded, turned, taken):
        a = net.sb(tag + "_a", [P, TILES, D], ctx=mem)

        @block.sync
        def _(sp):
            flat = scratch.rearrange("b h s f -> (b h s f)").rearrange("(t p n) -> p t n", p=P, n=D)
            sp.dma_start(a[:], flat).then_inc(loaded, 16)

        @block.tensor
        def _(pe):
            pe.wait_ge(loaded, 16)
            for t in range(TILES):
                for c in range(KC):
                    last = nc.tensor.transpose(net.bank(t)[:, c * P:(c + 1) * P], a[:, t, c * P:(c + 1) * P], net.ident[:])
                last.then_inc(turned, 1)

        @block.scalar
        def _(act):
            for t in range(TILES):
                act.wait_ge(turned, t + 1)
                nc.scalar.activation(net.actT[:, 0:KC, t * P:(t + 1) * P],
                                     net.bank(t)[:, 0:D].rearrange("p (c n) -> p c n", c=KC), ACT.Copy).then_inc(taken, 1)


def program(nc, dram, out, only=None):
    with ExitStack() as ctx:
        net = Net(nc, dram, ctx)
        scratch = nc.dram_tensor("heads_scratch", (B, HEADS, S, 16), F32, kind="Internal").ap()
        load_all(net)

        def xattn(layer, wo, bo, mask=None, scratch=None):
            pre = f"L{layer}_xattn_"
            norm(net, f"nx{layer}", net.x)
            cross_attention(net, f"x{layer}", pre + "Wq", pre + "bq", pre + "Wk", pre + "bk", pre + "Wv", pre + "bv",
                            mask, scratch)
            if scratch is not None:
                heads_reshaped(net, f"xr{layer}", scratch)
            project(net, f"px{layer}", pre + wo, pre + bo)

        xattn(0, "Wo", "bo")
        norm(net, "na0", net.x)
        self_attention(net, "a0", 32, 2, ["L0_q", "L0_qr", "L0_k", "L0_kr", "L0_v"], "alibi")
        project(net, "pa0", "L0_proj", "L0_proj_b")
        norm(net, "nf0", net.x)
        with ExitStack() as mem:
            rwT = net.sb("rw0", [65, TOK], ctx=mem)
            route_groups(net, "r0", rwT)
            experts(net, "e0", "L0_pack", L0_TILES, 65, rwT, "L0_b2", True)

        xattn(1, "Wo", "bo", "mask_f32")
        norm(net, "na1", net.x)
        self_attention(net, "a1", 128, 8, ["L1_q", "L1_qr", "L1_k", "L1_kr", "L1_v"], "band")
        project(net, "pa1", "L1_attn_Wo", None, chunks=8)
        norm(net, "nf1", net.x)
        with ExitStack() as mem:
            wfcT = net.sb("wfcT", [P, KC, 1024], ctx=mem)
            wprT = net.sb("wprT", [P, 8, D], ctx=mem)
            ternary(net, "tf", "L1_ffn_w_fc", 8, 256, wfcT)
            ternary(net, "tp", "L1_ffn_w_proj", 2, 1024, wprT)
            bit_hidden(net, "bh", wfcT)
            project(net, "pf1", None, None, chunks=8, w_sb=wprT)

        xattn(2, "Wh", "bh", scratch=scratch)
        norm(net, "na2", net.x)
        with ExitStack() as mem:
            y = net.sb("mix_y", [P, TILES, D], ctx=mem)
            scan_mixer(net, "sm", y)
            norm(net, "ny2", y, "L2_attn_gamma", "L2_attn_beta")
        project(net, "pa2", "L2_attn_W_out", "L2_attn_b_out", src=net.xnT)
        norm(net, "nf2", net.x)
        with ExitStack() as mem:
            rwT = net.sb("rw2", [14, TOK], ctx=mem)
            route_top1(net, "r2", rwT)
            experts(net, "e2", "L2_pack", L2_TILES, 14, rwT, "L2_ffn_b2", False)

        xattn(3, "Wo", "bo", "mask_int")
        norm(net, "na3", net.x)
        causal_attention(net, "a3")
        norm(net, "nf3", net.x)
        with ExitStack() as mem:
            gm = net.sb("gm", [64, 4, TOK], ctx=mem)
            e2 = net.sb("e2f", [64, 4, D], ctx=mem)
            lora_hidden(net, "lh", gm, e2)
            project(net, "pf3", "L3_ffn_W2T", "L3_ffn_b2", chunks=8, out=out,
                    extra=lambda t: [(gm[:, r, t * P:(t + 1) * P], e2[:, r, :]) for r in range(4)])


L0_ROWS = 64 * 176 + 352
L0_TILES = 2 * -(-L0_ROWS // (2 * P))
L2_TILES = 14 * 4


def _columns(v, chunks):
    return np.ascontiguousarray(v.reshape(chunks, P).T)


def _rope(head_dim, sections):
    inv = (1.0 / 10000.0 ** (np.arange(0, head_dim, 2, dtype=np.float32) / np.float32(head_dim))).astype(np.float32)
    ang = np.arange(S, dtype=np.float32)[:, None] * inv[None, :]
    j = np.arange(P) % head_dim
    f = ang.T[j % (head_dim // 2)]
    sign = np.where(j < head_dim // 2, -1.0, 1.0).astype(np.float32)[:, None]
    return np.stack([np.cos(f), np.sin(f) * sign], 1).astype(np.float32)


def _rotated(w, head_dim):
    shape = w.shape
    w = w.reshape(shape[0], -1, 2, head_dim // 2)
    return np.ascontiguousarray(w[:, :, ::-1, :].reshape(shape))


def arrange(a):
    f = np.float32
    o = {"x": np.ascontiguousarray(a["x"].reshape(TOK, D))}
    T = lambda m: np.ascontiguousarray(m.T)
    row = lambda v: np.ascontiguousarray(v.reshape(1, -1))
    o["ctxT"] = np.ascontiguousarray(a["ctx_1024"].transpose(0, 2, 1).reshape(B, KC, P, CTX))
    o["mask_f32"] = np.ascontiguousarray(a["mask_Bx1x1xS2_fk0"].reshape(B, CTX))
    o["mask_int"] = np.ascontiguousarray(a["mask_BxS2_ik0"])
    o["ident"] = np.eye(P, dtype=f)
    o["stack2"] = np.concatenate([np.eye(S, dtype=f)] * 2)
    p = np.arange(P)
    o["parity"] = np.stack([(p // 16 % 2 == 0) * 0.25, (p // 16 % 2 == 1) * 0.25, (p < 64) * 0.125, (p >= 64) * 0.125], 1).astype(f)
    for l, wo, bo in ((0, "Wo", "bo"), (1, "Wo", "bo"), (2, "Wh", "bh"), (3, "Wo", "bo")):
        pre = f"L{l}_xattn_"
        for w in ("Wq", "Wk", "Wv", wo):
            o[pre + w] = np.ascontiguousarray(a[pre + w]) if l == 1 else T(a[pre + w])
        for v in ("bq", "bk"):
            o[pre + v] = _columns(a[pre + v], KC)
        o[pre + "bv"], o[pre + bo] = row(a[pre + "bv"]), row(a[pre + bo])
    qkv = T(a["L0_attn_qkv_w"])
    o["L0_q"], o["L0_k"], o["L0_v"] = (np.ascontiguousarray(qkv[:, n * D:(n + 1) * D]) for n in range(3))
    o["L0_qr"], o["L0_kr"] = _rotated(o["L0_q"], 16), _rotated(o["L0_k"], 16)
    o["L0_proj"], o["L0_proj_b"] = T(a["L0_attn_proj_w"]), row(a["L0_attn_proj_b"])
    o["slopes"] = np.ascontiguousarray(a["L0_attn_slopes"].reshape(PAIRS, 2).T)
    pos = np.arange(S, dtype=f)
    diff = pos[None, :] - pos[:, None]
    o["a0_dist"] = np.concatenate([np.minimum(diff, 0.0) * 8.0] * 2).astype(f)
    o["a0_rope"] = _rope(16, 2)
    for n, w in (("q", "Wq"), ("k", "Wk"), ("v", "Wv")):
        o["L1_" + n] = np.ascontiguousarray(a["L1_attn_" + w])
    o["L1_qr"], o["L1_kr"] = _rotated(o["L1_q"], 64), _rotated(o["L1_k"], 64)
    o["L1_attn_Wo"] = np.ascontiguousarray(a["L1_attn_Wo"])
    o["a1_dist"] = np.concatenate([np.where(np.abs(diff) <= S // 4, 0.0, NEG)] * 2).astype(f)
    o["a1_rope"] = _rope(64, 2)
    o["gate_wT"], o["gate_bias"] = T(a["L0_ffn_gate_w"]), row(a["L0_ffn_gate_bias"])
    o["tri8"] = np.tril(np.ones((8, 8), f), -1)
    o["tri14"] = np.tril(np.ones((14, 14), f), -1)

    def pack(tiles, ups, down, expert_of, experts, b1):
        rows = tiles * P
        parts = []
        for m in ups:
            m = np.concatenate([m, np.zeros((rows - m.shape[0], D), f)])
            parts.append(m.reshape(tiles, P, KC, P).transpose(0, 3, 2, 1).reshape(tiles, P, KC * P))
        down = np.concatenate([down, np.zeros((rows - down.shape[0], D), f)])
        parts.append(down.reshape(tiles, P, D))
        sel = np.zeros((tiles, P, P), f)
        for r, e in enumerate(expert_of):
            sel[r // P, e, r % P] = 1.0
        parts.append(sel)
        if b1 is not None:
            parts.append(b1.reshape(tiles, P, 1))
        return np.ascontiguousarray(np.concatenate(parts, 2))

    Wg = np.concatenate([a["L0_ffn_Wg"].reshape(-1, D), a["L0_ffn_Sg"]])
    Wu = np.concatenate([a["L0_ffn_Wu"].reshape(-1, D), a["L0_ffn_Su"]])
    Wd = np.concatenate([a["L0_ffn_Wd"].transpose(0, 2, 1).reshape(-1, D), a["L0_ffn_Sd"].T])
    o["L0_pack"] = pack(L0_TILES, [Wg, Wu], Wd, list(np.repeat(np.arange(64), 176)) + [64] * 352, 65, None)
    o["L0_b2"] = np.zeros((65, D), f)
    w1 = a["L2_ffn_w1"].transpose(0, 2, 1).reshape(-1, D)
    o["L2_pack"] = pack(L2_TILES, [w1], a["L2_ffn_w2"].reshape(-1, D), list(np.repeat(np.arange(14), 512)), 14,
                        a["L2_ffn_b1"].reshape(-1))
    o["L2_ffn_b2"] = np.ascontiguousarray(a["L2_ffn_b2"])
    o["router_w"] = np.ascontiguousarray(a["L2_ffn_router_w"])
    o["L1_ffn_w_fc"], o["L1_ffn_w_proj"] = (np.ascontiguousarray(a["L1_ffn_" + n]) for n in ("w_fc", "w_proj"))
    o["L1_ffn_vT"], o["L1_ffn_fbT"], o["L1_ffn_uT"] = T(a["L1_ffn_v"]), T(a["L1_ffn_fast_b"]), T(a["L1_ffn_u"])
    o["L1_ffn_gate"] = a["L1_ffn_gate"].reshape(1, 1)
    split = lambda m: m.reshape(*m.shape[:-1], -1, P, 2)
    o["L2_attn_W_in"] = np.ascontiguousarray(np.moveaxis(split(a["L2_attn_W_in"]), -1, -2).reshape(D, 6 * P))
    o["L2_attn_b_in"] = np.ascontiguousarray(np.moveaxis(split(a["L2_attn_b_in"]), -1, -2).reshape(6, P).T)
    for n, k in (("lower_bound", "lb"), ("gamma", "gamma"), ("beta", "beta")):
        o["L2_attn_" + k] = np.ascontiguousarray(a["L2_attn_" + n].reshape(P, 2))
    o["L2_attn_W_out"] = np.ascontiguousarray(a["L2_attn_W_out"].reshape(P, 2, D).transpose(1, 0, 2).reshape(D, D))
    o["L2_attn_b_out"] = row(a["L2_attn_b_out"])
    for w in ("Wq", "Wk", "Wv"):
        o["L3_attn_" + w] = T(a["L3_attn_" + w])
    o["L3_attn_bq"], o["L3_attn_bk"] = _columns(a["L3_attn_bq"], KC), _columns(a["L3_attn_bk"], KC)
    o["L3_attn_bv"] = row(a["L3_attn_bv"])
    blk, q = p // S, p % S
    o["causal"] = np.where((blk[:, None] == blk[None, :]) & (q[None, :] <= q[:, None]), 0.0, NEG).astype(f)
    o["L3_ffn_W1T"], o["L3_ffn_W2T"] = T(a["L3_ffn_W1"]), T(a["L3_ffn_W2"])
    o["L3_ffn_b1"], o["L3_ffn_b2"] = _columns(a["L3_ffn_b1"], 8), row(a["L3_ffn_b2"])
    o["L3_ffn_scale"] = a["L3_ffn_scale"].reshape(1, 1)
    bi = np.arange(64)
    o["own_batch"] = (bi[:, None] // 4 == np.arange(TOK)[None, :] // S).astype(f)
    o["m4"] = (bi[:, None] % 4 == np.arange(4)[None, :]).astype(f)
    return o


def kernel(**inputs):
    import concourse.bacc as bacc
    from concourse.bass_utils import run_bass_kernel_spmd as run

    nc = bacc.Bacc("TRN2", target_bir_lowering=False, num_devices=1)
    arrays, dram = {}, {}
    for name, v in arrange({k: np.asarray(v) for k, v in inputs.items()}).items():
        arrays["in_" + name] = v
        dram[name] = nc.dram_tensor("in_" + name, v.shape, mybir.dt.from_np(v.dtype), kind="ExternalInput").ap()
    out = nc.dram_tensor("out_x", (TOK, D), F32, kind="ExternalOutput").ap()
    program(nc, dram, out)
    r = run(nc, [arrays], core_ids=[0])
    return r.results[0]["out_x"].reshape(B, S, D)
```

```python
from contextlib import ExitStack, contextmanager

import numpy as np
import concourse.bass as bass
from concourse import mybir

F32 = mybir.dt.float32
I32 = mybir.dt.int32
F32R = mybir.dt.float32r
ALU = mybir.AluOpType
ACT = mybir.ActivationFunctionType
AX = mybir.AxisListType

P = 128
B, S, D = 16, 64, 256
TOK = B * S
TILES = TOK // P
KC = D // P
HALF = 512
CTX = 1601
HEADS = 16
PAIRS = HEADS // 2
KEY_TILES = -(-CTX // P)
LAST_KEYS = CTX - (KEY_TILES - 1) * P
EPS = 1e-5
NEG = -1e30


@contextmanager
def stage(nc, names):
    sems = [nc.alloc_semaphore(f"{n}_{nc.next_id()}") for n in names.split()]
    with ExitStack() as mem:
        block = mem.enter_context(nc.Block())
        yield (block, *sems)
    nc.clear_and_free_semaphores(sems)
    nc.all_engine_barrier()


def spread(ap, shape):
    return ap.to_broadcast(list(shape))


class Net:

    def __init__(self, nc, dram, ctx):
        self.nc, self.dram = nc, dram
        self.ctx = ctx
        self.x = self.sb("x_tok", [P, TILES, D])
        self.xnT = self.sb("xnT", [P, KC, TOK])
        self.actT = self.sb("actT", [P, KC, TOK])
        self.ident = self.sb("ident", [P, P])
        self.stack2 = self.sb("stack2", [P, S])
        self.ones = self.sb("ones", [P, P])
        self.parity = self.sb("parity", [P, 14])
        self.eps = self.sb("eps", [P, 1])
        self.ps = [ctx.enter_context(nc.psum_tensor(f"bank{i}", [P, 1024], F32)) for i in range(4)]

    @contextmanager
    def eight_chunks(self, name):
        narrow = self.actT
        with self.nc.sbuf_tensor(name, [P, 8, TOK], F32) as self.actT:
            yield
        self.actT = narrow

    def sb(self, name, shape, dt=F32, ctx=None):
        return (ctx or self.ctx).enter_context(self.nc.sbuf_tensor(name, shape, dt))

    def bank(self, i):
        return self.ps[i // 2][:, (i % 2) * 512:(i % 2) * 512 + 512]


def load_all(net):
    nc, d = net.nc, net.dram
    with stage(nc, "loaded eps_set") as (block, loaded, eps_set):
        @block.sync
        def _(sp):
            sp.dma_start(net.x[:], d["x"].rearrange("(t p) n -> p t n", p=P)).then_inc(loaded, 16)
            sp.dma_start(net.ident[:], d["ident"]).then_inc(loaded, 16)
            sp.dma_start(net.stack2[:], d["stack2"]).then_inc(loaded, 16)
            sp.dma_start(net.parity[:], d["parity"]).then_inc(loaded, 16)
            sp.wait_ge(loaded, 64)

        @block.vector
        def _(dve):
            nc.vector.memset(net.eps[:], EPS).then_inc(eps_set, 1)
            nc.vector.memset(net.ones[:], 1.0).then_inc(eps_set, 1)
            dve.wait_ge(eps_set, 2)


def norm(net, tag, src, gamma=None, beta=None):
    nc, d = net.nc, net.dram
    with ExitStack() as mem, stage(nc, "chain stats_ready std_ready xn_ready turned taken cols") as (
            block, chain, stats_ready, std_ready, xn_ready, turned, taken, cols):
        stats = net.sb(tag + "_stats", [P, TILES, 6], ctx=mem)
        mv = net.sb(tag + "_mv", [P, TILES, 2], ctx=mem)
        std = net.sb(tag + "_std", [P, TILES], ctx=mem)
        rstd = net.sb(tag + "_rstd", [P, TILES], ctx=mem)
        xn = net.sb(tag + "_xn", [P, TILES, D], ctx=mem)
        gb = net.sb(tag + "_gb", [P, 2 * KC], ctx=mem)

        if gamma:
            @block.sync
            def _(sp):
                sp.dma_start(gb[:, 0:KC], d[gamma]).then_inc(cols, 16)
                sp.dma_start(gb[:, KC:2 * KC], d[beta]).then_inc(cols, 16)

        @block.vector
        def _(dve):
            for t in range(TILES):
                nc.vector.bn_stats(stats[:, t, :], src[:, t, :]).then_inc(chain, 1)
            for t in range(TILES):
                dve.wait_ge(chain, t + 1)
                nc.vector.bn_aggr(mv[:, t, :], stats[:, t, :]).then_inc(stats_ready, 1)
            dve.wait_ge(std_ready, 1)
            nc.vector.reciprocal(rstd[:], std[:]).then_inc(chain, 1)
            dve.wait_ge(chain, TILES + 1)
            for t in range(TILES):
                nc.vector.tensor_scalar(xn[:, t, :], src[:, t, :], mv[:, t, 0:1], rstd[:, t:t + 1],
                                        ALU.subtract, ALU.mult).then_inc(xn_ready, 1)

        @block.scalar
        def _(act):
            act.wait_ge(stats_ready, TILES)
            nc.scalar.activation(std[:], mv[:, :, 1], ACT.Sqrt, bias=net.eps[:, 0:1]).then_inc(std_ready, 1)
            if gamma:
                act.wait_ge(cols, 32)
            for t in range(TILES):
                act.wait_ge(turned, t + 1)
                for c in range(KC):
                    kw = dict(scale=gb[:, c:c + 1], bias=gb[:, KC + c:KC + c + 1]) if gamma else {}
                    fn = ACT.Identity if gamma else ACT.Copy
                    last = nc.scalar.activation(net.xnT[:, c, t * P:(t + 1) * P],
                                                net.bank(t % 8)[:, c * P:(c + 1) * P], fn, **kw)
                last.then_inc(taken, 1)

        @block.tensor
        def _(pe):
            for t in range(TILES):
                pe.wait_ge(xn_ready, t + 1)
                for c in range(KC):
                    last = nc.tensor.transpose(net.bank(t % 8)[:, c * P:(c + 1) * P],
                                               xn[:, t, c * P:(c + 1) * P], net.ident[:])
                last.then_inc(turned, 1)


def project(net, tag, w, bias, chunks=KC, extra=None, src=None, w_sb=None, out=None):
    nc, d = net.nc, net.dram
    src = src or net.actT
    with ExitStack() as mem, stage(nc, "w_in made added stored") as (block, w_in, made, added, stored):
        wsb = w_sb or net.sb(tag + "_w", [P, chunks, D], ctx=mem)
        brow = net.sb(tag + "_b", [1, D], ctx=mem)

        @block.sync
        def _(sp):
            if not w_sb:
                sp.dma_start(wsb[:], d[w].rearrange("(c p) n -> p c n", p=P)).then_inc(w_in, 16)
            if bias:
                sp.dma_start(brow[:], d[bias]).then_inc(w_in, 16)
            if out is not None:
                for t in range(TILES):
                    sp.wait_ge(added, t + 1)
                    sp.dma_start(out[t * P:(t + 1) * P, :], net.x[:, t, :]).then_inc(stored, 16)
                sp.wait_ge(stored, 16 * TILES)

        @block.tensor
        def _(pe):
            if bias or not w_sb:
                pe.wait_ge(w_in, 16 * (bool(bias) + (not w_sb)))
            for t in range(TILES):
                dst = net.bank(t % 8)[:, 0:D]
                if bias:
                    nc.tensor.matmul(dst, net.ones[0:1, :], brow[:], start=True, stop=False)
                for k, (a, b) in enumerate(extra(t) if extra else []):
                    nc.tensor.matmul(dst, a, b, start=(k == 0 and not bias), stop=False)
                for c in range(chunks):
                    last = nc.tensor.matmul(dst, src[:, c, t * P:(t + 1) * P], wsb[:, c, :],
                                            start=(c == 0 and not bias and not extra), stop=(c == chunks - 1))
                last.then_inc(made, 1)

        @block.vector
        def _(dve):
            for t in range(TILES):
                dve.wait_ge(made, t + 1)
                nc.vector.tensor_tensor(net.x[:, t, :], net.x[:, t, :], net.bank(t % 8)[:, 0:D],
                                        ALU.add).then_inc(added, 1)


def query_stacks(net, tag, wq, bq, mask, q_rows, m_rows):
    nc, d = net.nc, net.dram
    with ExitStack() as mem, stage(nc, "w_in m_in full q_full q_high q_low m_full m_high m_low stored") as (
            block, w_in, m_in, full, q_full, q_high, q_low, m_full, m_high, m_low, stored):
        w = net.sb(tag + "_wq", [P, KC, D], ctx=mem)
        col = net.sb(tag + "_bq", [P, KC], ctx=mem)
        q = net.sb(tag + "_qf", [P, KC, TOK], ctx=mem)
        parts = net.sb(tag + "_qhl", [P, 2, KC, TOK], F32R, ctx=mem)
        m = net.sb(tag + "_mf", [B, CTX], ctx=mem) if mask else None
        m_parts = net.sb(tag + "_mhl", [B, 2, CTX], F32R, ctx=mem) if mask else None

        @block.sync
        def _(sp):
            sp.dma_start(w[:], d[wq].rearrange("(c p) n -> p c n", p=P)).then_inc(w_in, 16)
            sp.dma_start(col[:], d[bq]).then_inc(w_in, 16)
            if mask:
                sp.dma_start(m[:].bitcast(I32) if mask == "mask_int" else m[:], d[mask]).then_inc(m_in, 16)
            stores = 0
            if mask:
                sp.wait_ge(m_high, 1)
                sp.wait_ge(m_low, 1)
                sp.dma_start(m_rows, m_parts[:].bitcast(F32)).then_inc(stored, 16)
                stores += 1
            for part in (0, 1, 2):
                sp.wait_ge(q_low if part == 2 else q_high, KC)
                for c in range(KC):
                    for j in range(4):
                        sp.dma_start(q_rows[32 * part:32 * part + 32, 4 * c + j, :],
                                     parts[32 * j:32 * j + 32, part // 2, c, :].bitcast(F32)).then_inc(stored, 16)
                        stores += 1
            sp.wait_ge(stored, 16 * stores)

        @block.tensor
        def _(pe):
            pe.wait_ge(w_in, 32)
            for c in range(KC):
                for h in range(2):
                    for k in range(KC):
                        last = nc.tensor.matmul(net.bank(2 * c + h), w[:, k, c * P:(c + 1) * P],
                                                net.xnT[:, k, h * HALF:(h + 1) * HALF], start=(k == 0), stop=(k == KC - 1))
                last.then_inc(full, 1)

        @block.vector
        def _(dve):
            if mask:
                dve.wait_ge(m_in, 16)
                if mask == "mask_f32":
                    nc.vector.tensor_scalar(m[:], m[:], -1e9, None, ALU.mult).then_inc(m_full, 1)
                else:
                    nc.vector.tensor_scalar(m[:], m[:].bitcast(I32), 0.0, -3e38, ALU.is_equal, ALU.mult).then_inc(m_full, 1)
                dve.wait_ge(m_high, 1)
                nc.vector.tensor_tensor(m_parts[:, 1], m[:], m_parts[:, 0], ALU.subtract).then_inc(m_low, 1)
            dve.wait_ge(w_in, 32)
            for c in range(KC):
                dve.wait_ge(full, c + 1)
                nc.vector.tensor_scalar(q[:, c], net.ps[c][:], col[:, c:c + 1], 0.25, ALU.add, ALU.mult).then_inc(q_full, 1)
            for c in range(KC):
                dve.wait_ge(q_high, c + 1)
                nc.vector.tensor_tensor(parts[:, 1, c], q[:, c], parts[:, 0, c], ALU.subtract).then_inc(q_low, 1)

        @block.scalar
        def _(act):
            if mask:
                act.wait_ge(m_full, 1)
                nc.scalar.activation(m_parts[:, 0], m[:], ACT.Copy).then_inc(m_high, 1)
            for c in range(KC):
                act.wait_ge(q_full, c + 1)
                nc.scalar.activation(parts[:, 0, c], q[:, c], ACT.Copy).then_inc(q_high, 1)


def cross_attention(net, tag, wk, bk, wv, bv, q_rows, m_rows):
    nc, d = net.nc, net.dram
    USES = 8 + 2 * PAIRS
    ROWS = 98 if m_rows is not None else 96
    STACKED = 16 * (12 + (m_rows is not None))
    SPLIT = 1024
    PART = [(0, SPLIT), (SPLIT, CTX)]
    EVEN = CTX + CTX % 2
    MID = SPLIT + (EVEN - SPLIT) // 4 * 2
    EDGE = HALF - (MID - SPLIT)
    SCORE_BLOCKS = [[(0, HALF, 0), (HALF, SPLIT, HALF)], [(SPLIT, MID, EDGE), (MID, EVEN, HALF)]]
    SCORE_AT = (0, EDGE)
    GROUPS = [(0, 4), (4, 8), (8, 12), (12, 13)]
    EARLY_INVERSE = (0,)
    EARLY_EXPS = (3,)
    RING = 4
    names = ("w_in bias_in ctx_in0 ctx_in1 q_in0 q_in1 stack_in0 stack_in1 slot_full slot_free0 slot_free1 turn_full "
             "turn_free0 turn_free1 ones_set q_ready negmax_ready exp_done rsum_ready prob_ready pv_done k_high k_low "
             "o_taken tail_ready")
    with ExitStack() as mem, stage(nc, names) as (
            block, w_in, bias_in, ctx_in0, ctx_in1, q_in0, q_in1, stack_in0, stack_in1, slot_full, slot_free0,
            slot_free1, turn_full, turn_free0, turn_free1, ones_set, q_ready, negmax_ready, exp_done, rsum_ready,
            prob_ready, pv_done, k_high, k_low, o_taken, tail_ready):
        ctx_in, q_in, stack_in = (ctx_in0, ctx_in1), (q_in0, q_in1), (stack_in0, stack_in1)
        slot_free = (slot_free0, slot_free1)
        turn_free = (turn_free0, turn_free1)
        wts = net.sb(tag + "_w", [P, 2, KC, D], ctx=mem)
        col = net.sb(tag + "_bk", [P, KC], ctx=mem)
        bvb = net.sb(tag + "_bv", [P, D], ctx=mem)
        ctxT = net.sb(tag + "_ctx", [P, 2, KC, CTX], ctx=mem)
        kh = net.sb(tag + "_kh", [P, CTX], F32R, ctx=mem)
        kl = net.sb(tag + "_kl", [P, CTX], F32R, ctx=mem)
        stack = net.sb(tag + "_ks", [P, PAIRS, EVEN], F32R, ctx=mem)
        v = net.sb(tag + "_v", [P, 2, KEY_TILES, D], ctx=mem)
        prob = net.sb(tag + "_p", [P, RING, CTX], ctx=mem)
        probT = net.sb(tag + "_pT", [P, 2, KEY_TILES, P], ctx=mem)
        qs = net.sb(tag + "_qs", [P, 2, PAIRS, S], F32R, ctx=mem)
        qb = net.sb(tag + "_q", [P, 2, PAIRS, 2, S], F32R, ctx=mem)
        part_max = net.sb(tag + "_mx", [P, RING, 2], ctx=mem)
        negmax = net.sb(tag + "_nm", [P, RING], ctx=mem)
        sums = net.sb(tag + "_sum", [P, RING], ctx=mem)
        rsum = net.sb(tag + "_rs", [P, 2], ctx=mem)
        half_o = net.sb(tag + "_o", [P, KC, S], ctx=mem)
        slots = net.ps[0:2]
        turns = (net.bank(4), net.bank(5))
        outs = (net.bank(6), net.bank(7))

        def o_psum(u):
            return outs[u][:, 0:2 * P].rearrange("p (c e s) -> p c e s", c=KC, e=2)

        def base(b):
            return 2 + USES * b

        def k_use(b, c):
            if c:
                return base(b)
            return 0 if isinstance(b, int) and b == 0 else base(b) - 6

        def v_use(b):
            return base(b) + 6

        def score_use(b, hp):
            last = isinstance(b, int) and b == B - 1
            return base(b) + 2 * hp + (2 if hp < 2 else 6 if hp < 6 or last else 8)


        def batches(eng, one):
            with eng.Fori(0, B // 2 - 1) as i:
                one(i, 0, False)
                one(i, 1, False)
            one(B // 2 - 1, 0, False)
            one(B // 2 - 1, 1, True)

        def following(i, u):
            return (i, 1) if u == 0 else (i + 1, 0)

        @block.sync
        def _(sp):
            for n, w in enumerate((wk, wv)):
                sp.dma_start(wts[:, n], d[w].rearrange("(c p) n -> p c n", p=P)).then_inc(w_in, 16)
            sp.dma_start(col[:], d[bk]).then_inc(bias_in, 16)
            sp.dma_start(bvb[:], spread(d[bv], (P, D))).then_inc(bias_in, 16)

            def load_context(b, u):
                sp.dma_start(ctxT[:, u], d["ctxT"][bass.ds(b, 1)].rearrange("o c p n -> p (o c) n")).then_inc(ctx_in[u], 16)

            def load_queries(b, u):
                sp.dma_start(qs[0:96, u].bitcast(F32), q_rows[:, :, bass.ds(b * S, S)]).then_inc(q_in[u], 16)

            def stack_keys(b, c):
                sp.wait_ge(k_low, 4 * b + 2 * c + 2)
                for part, src in enumerate((kh, kl, kh)):
                    for j in range(4):
                        sp.dma_start(stack[32 * part:32 * part + 32, 4 * c + j, 0:CTX].bitcast(F32),
                                     src[32 * j:32 * j + 32, :].bitcast(F32)).then_inc(stack_in[c], 16)
                if m_rows is not None:
                    rows = m_rows[bass.ds(b, 1)].rearrange("o r n -> r o n")
                    sp.dma_start(stack[96:98, 4 * c:4 * c + 4, 0:CTX].bitcast(F32), spread(rows, (2, 4, CTX))).then_inc(stack_in[c], 16)

            def one(i, u, last):
                b = 2 * i + u
                if not isinstance(b, int):
                    sp.wait_ge(slot_full, v_use(b) + 4)
                    load_context(b + 2, u)
                    load_queries(b + 2, u)
                if not last:
                    stack_keys(b + 1, 0)
                    stack_keys(b + 1, 1)

            for b in range(2):
                load_context(b, b)
                load_queries(b, b)
            stack_keys(0, 0)
            stack_keys(0, 1)
            batches(sp, one)

        @block.tensor
        def _(pe):
            pe.wait_ge(w_in, 32)
            pe.wait_ge(ones_set, (EVEN > CTX) + (m_rows is not None))

            def start_use(use, h):
                pe.wait_ge(slot_free[h], use // 2 + 1)
                return slots[h]

            def project_k(i, u, c):
                b = 2 * i + u
                if c == 0:
                    pe.wait_ge(ctx_in[u], i * 16 + 16)
                for h, (lo, hi) in enumerate(PART):
                    slot = start_use(k_use(b, c), h)
                    for a in range(lo, hi, HALF):
                        z = min(a + HALF, hi)
                        for k in range(KC):
                            last = nc.tensor.matmul(slot[:, a - lo:z - lo], wts[:, 0, k, c * P:(c + 1) * P],
                                                    ctxT[:, u, k, a:z], start=(k == 0), stop=(k == KC - 1))
                    last.then_inc(slot_full, 1)

            def project_v(i, u):
                b = 2 * i + u
                for g, (lo, hi) in enumerate(GROUPS):
                    slot = start_use(v_use(b) + g // 2 * 2, g % 2)
                    for t in range(lo, hi):
                        n = P if t < KEY_TILES - 1 else LAST_KEYS
                        for k in range(KC):
                            last = nc.tensor.matmul(slot[0:n, (t - lo) * D:(t - lo + 1) * D],
                                                    ctxT[:, u, k, t * P:t * P + n], wts[:, 1, k, :],
                                                    start=(k == 0), stop=(k == KC - 1))
                    last.then_inc(slot_full, 1)

            def scores(i, u, hp):
                b = 2 * i + u
                if hp == 0:
                    pe.wait_ge(q_ready, b * 2 + 2)
                if hp in (0, 4):
                    pe.wait_ge(stack_in[hp // 4], STACKED * (b + 1))
                for h, (lo, hi) in enumerate(PART):
                    slot = start_use(score_use(b, hp), h)
                    for a, z, at in SCORE_BLOCKS[h]:
                        last = nc.tensor.matmul(slot[:, at:at + z - a], qb[0:ROWS, u, hp], stack[0:ROWS, hp, a:z],
                                                start=True, stop=True)
                    last.then_inc(slot_full, 1)

            def turn(i, u, hp, groups):
                b = 2 * i + u
                pe.wait_ge(tail_ready if groups[0] else prob_ready, b * PAIRS + hp + 1)
                for g in groups:
                    lo, hi = GROUPS[g]
                    pe.wait_ge(turn_free[g % 2], b * 2 * PAIRS + 2 * hp + g // 2 + 1)
                    for t in range(lo, hi):
                        n = P if t < KEY_TILES - 1 else LAST_KEYS
                        last = nc.tensor.transpose(turns[g % 2][0:n, (t - lo) * P:(t - lo + 1) * P],
                                                   prob[:, hp % RING, t * P:t * P + n], net.ident[:])
                    last.then_inc(turn_full, 1)

            def attend(i, u, hp):
                b, c, j = 2 * i + u, hp // 4, hp % 4
                if hp == 0:
                    pe.wait_ge(o_taken, 2 * b + 2)
                for f in turn_free:
                    pe.wait_ge(f, b * 2 * PAIRS + 2 * hp + 3)
                if hp == 0:
                    for f in slot_free:
                        pe.wait_ge(f, v_use(b) // 2 + 3)
                for t in range(KEY_TILES):
                    n = P if t < KEY_TILES - 1 else LAST_KEYS
                    last = nc.tensor.matmul(outs[u][32 * j:32 * j + 32, c * P:(c + 1) * P],
                                            v[0:n, u, t, hp * 32:(hp + 1) * 32], probT[0:n, hp % 2, t, :],
                                            start=(t == 0), stop=(t == KEY_TILES - 1))
                last.then_inc(pv_done, 1)

            def one(i, u, last):
                nxt = following(i, u)
                for n in range(PAIRS):
                    turn(i, u, n, (0, 1))
                    if n < 6:
                        scores(i, u, n + 2)
                    elif not last:
                        if n == 6:
                            project_k(*nxt, 1)
                        scores(*nxt, n - 6)
                    if n == 3 and not last:
                        project_k(*nxt, 0)
                    turn(i, u, n, (2, 3))
                    if n:
                        attend(i, u, n - 1)
                if not last:
                    project_v(*nxt)
                attend(i, u, PAIRS - 1)

            project_k(0, 0, 0)
            project_k(0, 0, 1)
            scores(0, 0, 0)
            scores(0, 0, 1)
            project_v(0, 0)
            batches(pe, one)

        @block.vector
        def _(dve):
            dve.sem_inc(slot_free0, 1)
            dve.sem_inc(slot_free1, 1)
            dve.sem_inc(turn_free0, 1)
            dve.sem_inc(turn_free1, 1)
            dve.sem_inc(turn_full, 4 * RING)
            dve.sem_inc(pv_done, 2)
            dve.sem_inc(o_taken, 4)
            dve.wait_ge(bias_in, 32)

            def take_q(i, u):
                b = 2 * i + u
                dve.wait_ge(q_in[u], i * 16 + 16)
                for e in range(2):
                    nc.vector.tensor_scalar(qb[0:96, u, :, e, :], qs[0:96, u], net.parity[0:96, 12 + e:13 + e], None,
                                            ALU.mult).then_inc(q_ready, 1)

            def low_k(i, u, c):
                b = 2 * i + u
                for h, (lo, hi) in enumerate(PART):
                    dve.wait_ge(k_high, 4 * b + 2 * c + h + 1)
                    nc.vector.scalar_tensor_tensor(kl[:, lo:hi], slots[h][:, 0:hi - lo], col[:, c:c + 1], kh[:, lo:hi],
                                                   ALU.add, ALU.subtract).then_inc(slot_free[h], 1)
                    dve.wait_ge(slot_free[h], k_use(b, c) // 2 + 2)
                    dve.sem_inc(k_low, 1)

            def take_v(i, u):
                b = 2 * i + u
                for g, (lo, hi) in enumerate(GROUPS):
                    n = P if g < 3 else LAST_KEYS
                    dve.wait_ge(slot_full, v_use(b) + g + 1)
                    nc.vector.tensor_tensor(
                        v[0:n, u, lo:hi, :], slots[g % 2][0:n, 0:(hi - lo) * D].rearrange("p (t f) -> p t f", f=D),
                        spread(bvb[0:n, :].unsqueeze(1), (n, hi - lo, D)), ALU.add).then_inc(slot_free[g % 2], 1)

            def take_scores(i, u, hp):
                b, s = 2 * i + u, hp % RING
                dve.wait_ge(turn_full, b * 4 * PAIRS + 4 * hp + 4)
                for h, (lo, hi) in enumerate(PART):
                    dve.wait_ge(slot_full, score_use(b, hp) + h + 1)
                    nc.vector.tensor_scalar(prob[:, s, lo:hi], slots[h][:, SCORE_AT[h]:SCORE_AT[h] + hi - lo], 0.0, None,
                                            ALU.add, ALU.max, accum_out=part_max[:, s, h:h + 1]).then_inc(slot_free[h], 1)
                for f in slot_free:
                    dve.wait_ge(f, score_use(b, hp) // 2 + 2)
                nc.vector.tensor_reduce(negmax[:, s:s + 1], part_max[:, s, :], AX.X, ALU.max,
                                        negate=True).then_inc(negmax_ready, 1)

            def take_turn(i, u, hp):
                b = 2 * i + u
                dve.wait_ge(pv_done, b * PAIRS + hp + 1)
                for g in (0, 1):
                    lo, hi = GROUPS[g]
                    dve.wait_ge(turn_full, 4 * RING + b * 4 * PAIRS + 4 * hp + g + 1)
                    nc.vector.tensor_copy(probT[:, hp % 2, lo:hi, :].rearrange("p t n -> p (t n)"),
                                          turns[g % 2][:, 0:(hi - lo) * P]).then_inc(turn_free[g % 2], 1)

            def invert_sum(i, u, hp):
                dve.wait_ge(exp_done, (2 * i + u) * PAIRS + hp + 1)
                nc.vector.reciprocal(rsum[:, hp % 2:hp % 2 + 1], sums[:, hp % RING:hp % RING + 1]).then_inc(rsum_ready, 1)

            def take_output(i, u):
                b = 2 * i + u
                dve.wait_ge(pv_done, 2 + b * PAIRS + PAIRS)
                nc.vector.tensor_scalar(half_o[:], o_psum(u)[:, :, 0], net.parity[:, 12:13], None,
                                        ALU.mult).then_inc(o_taken, 1)
                dve.wait_ge(o_taken, 4 + 2 * b + 1)
                nc.vector.scalar_tensor_tensor(net.actT[:, 0:KC, bass.ds(b * S, S)], o_psum(u)[:, :, 1],
                                               net.parity[:, 13:14], half_o[:], ALU.mult, ALU.add).then_inc(o_taken, 1)

            def one(i, u, last):
                nxt = following(i, u)
                for n in range(PAIRS):
                    if n == 5 and not last:
                        take_q(*nxt)
                    early = n in EARLY_INVERSE
                    if not early:
                        take_turn(i, u, n)
                    if n < 7:
                        invert_sum(i, u, n + 1)
                    elif not last:
                        invert_sum(*nxt, 0)
                    if early:
                        take_turn(i, u, n)
                    if n < 6:
                        take_scores(i, u, n + 2)
                    elif not last:
                        if n == 6:
                            low_k(*nxt, 1)
                        take_scores(*nxt, n - 6)
                    if n == 3 and not last:
                        low_k(*nxt, 0)
                if not last:
                    take_v(*nxt)
                take_output(i, u)

            if EVEN > CTX:
                nc.vector.tensor_scalar(stack[:, :, CTX:EVEN], net.ones[:, 0:PAIRS].unsqueeze(2), 0.0, None,
                                        ALU.mult).then_inc(ones_set, 1)
            if m_rows is not None:
                nc.vector.tensor_copy(qb[96:98].rearrange("p u h e s -> p (u h) (e s)"),
                                      spread(net.ones[96:98, :].unsqueeze(1), (2, 2 * PAIRS, P))).then_inc(ones_set, 1)
            take_q(0, 0)
            low_k(0, 0, 0)
            low_k(0, 0, 1)
            take_scores(0, 0, 0)
            take_scores(0, 0, 1)
            invert_sum(0, 0, 0)
            take_v(0, 0)
            batches(dve, one)

        @block.gpsimd
        def _(pool):
            with pool.Fori(0, B) as b:
                for hp in range(PAIRS):
                    s = hp % RING
                    pool.wait_ge(rsum_ready, b * PAIRS + hp + 1)
                    nc.gpsimd.tensor_tensor(prob[:, s, SPLIT:CTX], prob[:, s, SPLIT:CTX],
                                            spread(rsum[:, hp % 2:hp % 2 + 1], (P, CTX - SPLIT)), ALU.mult).then_inc(tail_ready, 1)

        @block.scalar
        def _(act):
            act.wait_ge(bias_in, 32)

            def high_k(i, u, c):
                b = 2 * i + u
                if c:
                    act.wait_ge(stack_in[0], STACKED * (b + 1))
                elif not (isinstance(b, int) and b == 0):
                    act.wait_ge(stack_in[1], STACKED * b)
                for h, (lo, hi) in enumerate(PART):
                    act.wait_ge(slot_full, k_use(b, c) + h + 1)
                    nc.scalar.activation(kh[:, lo:hi], slots[h][:, 0:hi - lo], ACT.Identity,
                                         bias=col[:, c:c + 1]).then_inc(k_high, 1)

            def take_turn(i, u, hp):
                b = 2 * i + u
                act.wait_ge(pv_done, b * PAIRS + hp + 1)
                for g in (2, 3):
                    lo, hi = GROUPS[g]
                    n = P if g < 3 else LAST_KEYS
                    act.wait_ge(turn_full, 4 * RING + b * 4 * PAIRS + 4 * hp + g + 1)
                    nc.scalar.activation(probT[0:n, hp % 2, lo:hi, :].rearrange("p t n -> p (t n)"),
                                         turns[g % 2][0:n, 0:(hi - lo) * P], ACT.Copy).then_inc(turn_free[g % 2], 1)

            def exps(i, u, hp):
                s = hp % RING
                act.wait_ge(negmax_ready, (2 * i + u) * PAIRS + hp + 1)
                nc.scalar.activation(prob[:, s, :], prob[:, s, :], ACT.Exp, bias=negmax[:, s:s + 1],
                                     accum_out=sums[:, s:s + 1]).then_inc(exp_done, 1)

            def normalise(i, u, hp):
                act.wait_ge(rsum_ready, (2 * i + u) * PAIRS + hp + 1)
                nc.scalar.activation(prob[:, hp % RING, 0:SPLIT], prob[:, hp % RING, 0:SPLIT], ACT.Copy,
                                     scale=rsum[:, hp % 2:hp % 2 + 1]).then_inc(prob_ready, 1)

            def one(i, u, last):
                nxt = following(i, u)
                for n in range(PAIRS):
                    if n < 7 or not last:
                        normalise(*((i, u, n + 1) if n < 7 else (*nxt, 0)))
                    if n in EARLY_EXPS:
                        exps(i, u, n + 2)
                    if n in (3, 6) and not last:
                        high_k(*nxt, n // 6)
                    take_turn(i, u, n)
                    if n not in EARLY_EXPS and (n < 6 or not last):
                        exps(*((i, u, n + 2) if n < 6 else (*nxt, n - 6)))

            high_k(0, 0, 0)
            high_k(0, 0, 1)
            exps(0, 0, 0)
            normalise(0, 0, 0)
            exps(0, 0, 1)
            batches(act, one)


def self_attention(net, tag, width, chunks, wts, extra_bias):
    with ExitStack() as mem:
        F = chunks * P
        qT = net.sb(tag + "_qT", [P, chunks, TOK], ctx=mem)
        kT = net.sb(tag + "_kT", [P, chunks, TOK], ctx=mem)
        rotary(net, tag, chunks, wts, (qT, kT))
        attend_batches(net, tag, width, chunks, wts[4], extra_bias, qT, kT)


def rotary(net, tag, chunks, wts, outs):
    nc, d = net.nc, net.dram
    UNITS = [(t, c, h) for t in range(2) for c in range(chunks) for h in range(2)]
    with ExitStack() as mem, stage(nc, "wq_in wk_in tab_in full taken rotated") as (
            block, wq_in, wk_in, tab_in, full, taken, rotated):
        w = net.sb(tag + "_w", [P, 4, KC, chunks * P], ctx=mem)
        tabs = net.sb(tag + "_rope", [P, 2, S], ctx=mem)
        part = net.sb(tag + "_part", [P, 2, 2, HALF], ctx=mem)

        @block.sync
        def _(sp):
            for n in range(4):
                sp.dma_start(w[:, n], d[wts[n]].rearrange("(c p) n -> p c n", p=P)).then_inc((wq_in, wk_in)[n // 2], 16)
            sp.dma_start(tabs[:], d[tag + "_rope"]).then_inc(tab_in, 16)

        @block.tensor
        def _(pe):
            for n, (t, c, h) in enumerate(UNITS):
                if c == h == 0:
                    pe.wait_ge((wq_in, wk_in)[t], 32)
                if n >= 4:
                    pe.wait_ge(taken, 2 * (n - 3))
                for r in range(2):
                    for k in range(KC):
                        last = nc.tensor.matmul(net.bank(2 * (n % 4) + r), w[:, 2 * t + r, k, c * P:(c + 1) * P],
                                                net.xnT[:, k, h * HALF:(h + 1) * HALF], start=(k == 0), stop=(k == KC - 1))
                last.then_inc(full, 1)

        @block.vector
        def _(dve):
            dve.wait_ge(tab_in, 16)
            for n, (t, c, h) in enumerate(UNITS):
                dve.wait_ge(full, n + 1)
                if n >= 2:
                    dve.wait_ge(rotated, n - 1)
                for r in range(2):
                    nc.vector.tensor_tensor(part[:, n % 2, r].rearrange("p (b s) -> p b s", s=S),
                                            net.bank(2 * (n % 4) + r).rearrange("p (b s) -> p b s", s=S),
                                            spread(tabs[:, r:r + 1], (P, B // 2, S)), ALU.mult).then_inc(taken, 1)

        @block.gpsimd
        def _(pool):
            for n, (t, c, h) in enumerate(UNITS):
                pool.wait_ge(taken, 2 * n + 2)
                nc.gpsimd.tensor_tensor(outs[t][:, c, h * HALF:(h + 1) * HALF], part[:, n % 2, 0], part[:, n % 2, 1],
                                        ALU.add).then_inc(rotated, 1)


def attend_batches(net, tag, width, chunks, wv, extra_bias, qT, kT):
    nc, d = net.nc, net.dram
    F = chunks * P
    N = chunks * S
    names = ("w_in tab_in xb_ready kb_ready q_ready s_full biased maxed soft p_ready turned pt_ready v_full v_ready "
             "o_full o_ready added inverted summed act_done zeroed bias_ready")
    with ExitStack() as mem, stage(nc, names) as (
            block, w_in, tab_in, xb_ready, kb_ready, q_ready, s_full, biased, maxed, soft, p_ready, turned, pt_ready,
            v_full, v_ready, o_full, o_ready, added, inverted, summed, act_done, zeroed, bias_ready):
        w = net.sb(tag + "_wv", [P, KC, F], ctx=mem)
        xb = net.sb(tag + "_xb", [P, 2, KC, 2, S], ctx=mem)
        qb = net.sb(tag + "_qb", [P, 2, chunks, 2, S], ctx=mem)
        kb = net.sb(tag + "_kb", [P, 2, chunks, S], ctx=mem)
        v2 = net.sb(tag + "_v", [P, 2, F], ctx=mem)
        bias = net.sb(tag + "_bias", [P, PAIRS, S], ctx=mem)
        slopes = net.sb(tag + "_slopes", [P, PAIRS], ctx=mem)
        dist = net.sb(tag + "_dist", [P, S], ctx=mem)
        sc = net.sb(tag + "_s", [P, 2, PAIRS, S], ctx=mem)
        mx = net.sb(tag + "_mx", [P, PAIRS], ctx=mem)
        sums = net.sb(tag + "_sum", [P, PAIRS], ctx=mem)
        rs = net.sb(tag + "_rs", [P, PAIRS], ctx=mem)
        pT = net.sb(tag + "_pT", [P, PAIRS // 2, P], ctx=mem)
        o_bd = net.sb(tag + "_o", [P, PAIRS, 2, width // 2], ctx=mem)
        t_ps = net.bank(7)
        if width == P:
            o_ps, v_ps, a_ps, s_ps = net.ps[0][:], net.ps[2][:], net.bank(3)[:, 0:N], net.bank(6)
        else:
            o_ps, v_ps, a_ps, s_ps = net.ps[2][:], net.bank(6)[:, 0:F], net.bank(5)[:, F:F + N], None

        def inside(b):
            return not isinstance(b, int) or 0 <= b < B

        def steps(eng, step):
            step(0, 0)
            with eng.Fori(0, (B - 4) // 2) as i:
                for u in range(2):
                    step(2 * i + 1 + u, (1 + u) % 2)
            for b in range(B - 3, B):
                step(b, b % 2)

        @block.sync
        def _(sp):
            sp.dma_start(w[:], d[wv].rearrange("(c p) n -> p c n", p=P)).then_inc(w_in, 16)
            sp.dma_start(dist[:], d[tag + "_dist"]).then_inc(tab_in, 16)
            if extra_bias == "alibi":
                for e in range(2):
                    sp.dma_start(slopes[e * S:(e + 1) * S, :], spread(d["slopes"][e:e + 1], (S, PAIRS))).then_inc(tab_in, 16)

        @block.gpsimd
        def _(pool):
            nc.gpsimd.memset(o_bd[:], 0.0).then_inc(zeroed, 1)
            with pool.Fori(0, B // 2) as i:
                for u in range(2):
                    b = 2 * i + u
                    pool.wait_ge(s_full, 1 + b)
                    nc.gpsimd.tensor_copy(kb[:, u], kT[:, :, bass.ds(b * S, S)]).then_inc(kb_ready, 1)
                    pool.wait_ge(v_full, 1 + b)
                    for c in range(2):
                        nc.gpsimd.tensor_copy(xb[:, u, :, c, :], net.xnT[:, :, bass.ds(b * S, S)]).then_inc(xb_ready, 1)

        @block.tensor
        def _(pe):
            def scores(b, u):
                pe.wait_ge(q_ready, 2 * b + 2)
                pe.wait_ge(kb_ready, b + 1)
                pe.wait_ge(biased, 2 * b + 2)
                for hp in range(PAIRS):
                    c, r = hp * width // P, hp * width % P
                    dst = s_ps[:, hp * S:(hp + 1) * S] if width == P else net.bank(r // width)[:, c * S:(c + 1) * S]
                    last = nc.tensor.matmul(dst, qb[r:r + width, u, c], kb[r:r + width, u, c], start=True, stop=True)
                last.then_inc(s_full, 1)

            def values(b, u):
                pe.wait_ge(xb_ready, 2 * b + 2)
                pe.wait_ge(v_ready, b + 1)
                for h in range(0, F, HALF):
                    z = min(h + HALF, F)
                    for k in range(KC):
                        last = nc.tensor.matmul(v_ps[:, h:z], xb[:, u, k], w[:, k, h:z], start=(k == 0), stop=(k == KC - 1))
                last.then_inc(v_full, 1)

            def add_up(b):
                pe.wait_ge(o_ready, 2 * b + 4)
                pe.wait_ge(act_done, b + 1)
                flat = o_bd[:].rearrange("p h e f -> p (h e f)")
                for c in range(chunks):
                    last = nc.tensor.matmul(a_ps[:, c * S:(c + 1) * S], flat[:, c * P:(c + 1) * P], net.stack2[:],
                                            start=True, stop=True)
                last.then_inc(summed, 1)

            def step(b, u):
                pe.wait_ge(p_ready, b + 1)
                pe.wait_ge(pt_ready, b + 1)
                for j in range(PAIRS // 2):
                    last = nc.tensor.transpose(t_ps[:, j * P:(j + 1) * P],
                                               sc[:, u, 2 * j:2 * j + 2].rearrange("p h s -> p (h s)"), net.ident[:])
                last.then_inc(turned, 1)
                if inside(b - 1):
                    add_up(b - 1)
                if inside(b + 1):
                    scores(b + 1, 1 - u)
                    values(b + 1, 1 - u)
                pe.wait_ge(pt_ready, b + 2)
                pe.wait_ge(v_ready, b + 2)
                pe.wait_ge(o_ready, 2 * b + 2)
                pe.wait_ge(act_done, b + 1)
                for hp in range(PAIRS):
                    r = S * (hp % 2)
                    at = (hp % 2) * 512 + (hp // 2) * width
                    last = nc.tensor.matmul(o_ps[:, at:at + width], pT[r:r + S, hp // 2],
                                            v2[r:r + S, u, hp * width:(hp + 1) * width], start=True, stop=True)
                last.then_inc(o_full, 1)

            pe.wait_ge(w_in, 16)
            scores(0, 0)
            values(0, 0)
            steps(pe, step)
            add_up(B - 1)

        @block.vector
        def _(dve):
            for sem, count in ((act_done, 1), (pt_ready, 1), (v_ready, 1), (s_full, 2), (v_full, 2), (o_full, 2),
                               (turned, 2), (biased, 2), (o_ready, 2)):
                dve.sem_inc(sem, count)
            dve.wait_ge(tab_in, 48 if extra_bias == "alibi" else 16)
            for hp in range(PAIRS):
                if extra_bias == "alibi":
                    nc.vector.tensor_scalar(bias[:, hp], dist[:], slopes[:, hp:hp + 1], None, ALU.mult).then_inc(bias_ready, 1)
                else:
                    nc.vector.tensor_copy(bias[:, hp], dist[:]).then_inc(bias_ready, 1)

            def shift_scores(b, u):
                dve.wait_ge(turned, b + 1)
                dve.wait_ge(s_full, b + 3)
                if width == P:
                    nc.vector.tensor_tensor(sc[:, u], s_ps.rearrange("p (h s) -> p h s", s=S), bias[:],
                                            ALU.add).then_inc(biased, 2)
                else:
                    for t in range(2):
                        s4 = net.ps[t][:].rearrange("p (j n) -> p j n", j=2)[:, :, 0:chunks * S]
                        sel = [z.rearrange("p (c t j) s -> p t j c s", c=chunks, t=2)[:, t] for z in (sc[:, u], bias[:])]
                        nc.vector.tensor_tensor(sel[0], s4.rearrange("p j (c s) -> p j c s", s=S), sel[1],
                                                ALU.add).then_inc(biased, 1)
                dve.wait_ge(biased, 2 * b + 4)
                nc.vector.tensor_reduce(mx[:], sc[:, u], AX.X, ALU.max).then_inc(maxed, 1)
                dve.wait_ge(maxed, b + 1)
                nc.vector.tensor_tensor(sc[:, u], sc[:, u], spread(mx[:].unsqueeze(2), (P, PAIRS, S)),
                                        ALU.subtract).then_inc(soft, 1)

            def step(b, u):
                dve.wait_ge(turned, b + 3)
                nc.vector.tensor_copy(pT[:].rearrange("p j n -> p (j n)"), t_ps).then_inc(pt_ready, 1)
                dve.wait_ge(p_ready, b + 1)
                nc.vector.tensor_reduce(sums[:], sc[:, u], AX.X, ALU.add).then_inc(added, 1)
                dve.wait_ge(added, b + 1)
                nc.vector.reciprocal(rs[:], sums[:]).then_inc(inverted, 1)
                if inside(b + 1):
                    shift_scores(b + 1, 1 - u)
                dve.wait_ge(inverted, b + 1)
                dve.wait_ge(o_full, b + 3)
                o5 = o_ps.rearrange("p (b n) -> p b n", b=2)[:, :, 0:4 * width]\
                    .rearrange("p b (j e f) -> p b j e f", j=4, e=2)
                bd = o_bd[:].rearrange("p (j b) e f -> p b j e f", b=2)
                r5 = rs[:].rearrange("p (j b) -> p b j", b=2)
                for e in range(2):
                    r = slice(e * S, (e + 1) * S)
                    nc.vector.tensor_tensor(bd[r, :, :, e, :], o5[r, :, :, e, :],
                                            spread(r5[r].unsqueeze(3), (S, 2, 4, width // 2)), ALU.mult).then_inc(o_ready, 1)

            dve.wait_ge(zeroed, 1)
            dve.wait_ge(bias_ready, PAIRS)
            shift_scores(0, 0)
            steps(dve, step)

        @block.scalar
        def _(act):
            def queries(b, u):
                act.wait_ge(s_full, b + 1)
                for e in range(2):
                    at = 2 * (width // P) + e
                    nc.scalar.activation(qb[:, u, :, e, :], qT[:, :, bass.ds(b * S, S)], ACT.Copy,
                                         scale=net.parity[:, at:at + 1]).then_inc(q_ready, 1)

            def values(b, u):
                act.wait_ge(o_full, b + 1)
                act.wait_ge(v_full, b + 3)
                nc.scalar.activation(v2[:, u], v_ps[:, 0:F], ACT.Copy).then_inc(v_ready, 1)

            def exps(b, u):
                act.wait_ge(soft, b + 1)
                nc.scalar.activation(sc[:, u], sc[:, u], ACT.Exp).then_inc(p_ready, 1)

            def output(b):
                act.wait_ge(summed, b + 1)
                nc.scalar.activation(net.actT[:, 0:chunks, bass.ds(b * S, S)],
                                     a_ps.rearrange("p (c s) -> p c s", s=S), ACT.Copy).then_inc(act_done, 1)

            def step(b, u):
                if inside(b - 1):
                    output(b - 1)
                if inside(b + 1):
                    exps(b + 1, 1 - u)
                    values(b + 1, 1 - u)
                if inside(b + 2):
                    queries(b + 2, u)

            queries(0, 0)
            queries(1, 1)
            exps(0, 0)
            values(0, 0)
            steps(act, step)
            output(B - 1)
            act.wait_ge(act_done, B + 1)


def causal_attention(net, tag):
    nc, d = net.nc, net.dram
    names = "w_in xb_ready qk_full qk_ready v_full v_ready s_full chain p_ready turned pt_ready o_full added"
    with ExitStack() as mem, stage(nc, names) as (
            block, w_in, xb_ready, qk_full, qk_ready, v_full, v_ready, s_full, chain, p_ready, turned, pt_ready,
            o_full, added):
        w = net.sb(tag + "_w", [P, 3, KC, D], ctx=mem)
        cols = net.sb(tag + "_cols", [P, 2, KC], ctx=mem)
        bvb = net.sb(tag + "_bv", [P, D], ctx=mem)
        mask = net.sb(tag + "_mask", [P, P], ctx=mem)
        xb = net.sb(tag + "_xb", [P, KC, P], ctx=mem)
        qk = net.sb(tag + "_qk", [P, 2, KC, P], ctx=mem)
        v = net.sb(tag + "_v", [P, D], ctx=mem)
        sc = net.sb(tag + "_s", [P, P], ctx=mem)
        negmax = net.sb(tag + "_nm", [P, 1], ctx=mem)
        total = net.sb(tag + "_sum", [P, 2], ctx=mem)
        pT = net.sb(tag + "_pT", [P, P], ctx=mem)

        @block.sync
        def _(sp):
            for n, name in enumerate(("L3_attn_Wq", "L3_attn_Wk", "L3_attn_Wv")):
                sp.dma_start(w[:, n], d[name].rearrange("(c p) n -> p c n", p=P)).then_inc(w_in, 16)
            sp.dma_start(cols[:, 0], d["L3_attn_bq"]).then_inc(w_in, 16)
            sp.dma_start(cols[:, 1], d["L3_attn_bk"]).then_inc(w_in, 16)
            sp.dma_start(bvb[:], spread(d["L3_attn_bv"], (P, D))).then_inc(w_in, 16)
            sp.dma_start(mask[:], d["causal"]).then_inc(w_in, 16)

        @block.gpsimd
        def _(pool):
            with pool.Fori(0, TILES) as t:
                pool.wait_ge(v_full, t + 1)
                nc.gpsimd.tensor_copy(xb[:], net.xnT[:, :, bass.ds(t * P, P)]).then_inc(xb_ready, 1)

        @block.tensor
        def _(pe):
            pe.wait_ge(w_in, 112)
            with pe.Fori(0, TILES) as t:
                pe.wait_ge(xb_ready, t + 1)
                pe.wait_ge(added, t + 1)
                for n in range(2):
                    for c in range(KC):
                        for k in range(KC):
                            last = nc.tensor.matmul(net.bank(n)[:, c * P:(c + 1) * P], w[:, n, k, c * P:(c + 1) * P],
                                                    xb[:, k], start=(k == 0), stop=(k == KC - 1))
                    last.then_inc(qk_full, 1)
                for k in range(KC):
                    last = nc.tensor.matmul(net.bank(2)[:, 0:D], xb[:, k], w[:, 2, k], start=(k == 0), stop=(k == KC - 1))
                last.then_inc(v_full, 1)
                pe.wait_ge(qk_ready, 4 * t + 4)
                for k in range(KC):
                    last = nc.tensor.matmul(net.bank(3)[:, 0:P], qk[:, 0, k], qk[:, 1, k], start=(k == 0), stop=(k == KC - 1))
                last.then_inc(s_full, 1)
                pe.wait_ge(p_ready, t + 1)
                nc.tensor.transpose(net.bank(4)[:, 0:P], sc[:], net.ident[:]).then_inc(turned, 1)
                pe.wait_ge(pt_ready, t + 1)
                pe.wait_ge(v_ready, t + 1)
                nc.tensor.matmul(net.bank(5)[:, 0:D], pT[:], v[:], start=True, stop=True).then_inc(o_full, 1)

        @block.vector
        def _(dve):
            dve.sem_inc(added, 1)
            dve.sem_inc(v_full, 1)
            dve.wait_ge(w_in, 112)
            with dve.Fori(0, TILES) as t:
                dve.wait_ge(v_full, t + 2)
                nc.vector.tensor_tensor(v[:], net.bank(2)[:, 0:D], bvb[:], ALU.add).then_inc(v_ready, 1)
                dve.wait_ge(s_full, t + 1)
                nc.vector.scalar_tensor_tensor(sc[:], net.bank(3)[:, 0:P], float(D) ** -0.5, mask[:], ALU.mult,
                                               ALU.add).then_inc(chain, 1)
                dve.wait_ge(chain, 3 * t + 1)
                nc.vector.tensor_reduce(negmax[:], sc[:], AX.X, ALU.max, negate=True).then_inc(chain, 1)
                dve.wait_ge(p_ready, t + 1)
                nc.vector.reciprocal(total[:, 1:2], total[:, 0:1]).then_inc(chain, 1)
                dve.wait_ge(turned, t + 1)
                nc.vector.tensor_copy(pT[:], net.bank(4)[:, 0:P]).then_inc(pt_ready, 1)
                dve.wait_ge(o_full, t + 1)
                dve.wait_ge(chain, 3 * t + 3)
                xt = net.x[:, bass.ds(t, 1), :].rearrange("p o n -> p (o n)")
                nc.vector.scalar_tensor_tensor(xt, net.bank(5)[:, 0:D], total[:, 1:2], xt, ALU.mult,
                                               ALU.add).then_inc(added, 1)

        @block.scalar
        def _(act):
            act.wait_ge(w_in, 112)
            with act.Fori(0, TILES) as t:
                for n in range(2):
                    act.wait_ge(qk_full, 2 * t + n + 1)
                    for c in range(KC):
                        nc.scalar.activation(qk[:, n, c], net.bank(n)[:, c * P:(c + 1) * P], ACT.Identity,
                                             bias=cols[:, n, c:c + 1]).then_inc(qk_ready, 1)
                act.wait_ge(chain, 3 * t + 2)
                nc.scalar.activation(sc[:], sc[:], ACT.Exp, bias=negmax[:, 0:1],
                                     accum_out=total[:, 0:1]).then_inc(p_ready, 1)


def rank_below(nc, dve, link, gt, eq, vals, tri, rank, n):
    shape = (P, TILES * n * n)
    for t in range(TILES):
        a = spread(vals[:, t, :].unsqueeze(1), (P, n, n))
        b = spread(vals[:, t, :].unsqueeze(2), (P, n, n))
        nc.vector.tensor_tensor(gt[:, t], a, b, ALU.is_gt)
        link(nc.vector.tensor_tensor(eq[:, t], a, b, ALU.is_equal))
    for t in range(TILES):
        link(nc.vector.tensor_tensor(eq[:, t], eq[:, t], tri, ALU.mult))
    link(nc.vector.tensor_tensor(gt.rearrange("p t i j -> p (t i j)"), gt.rearrange("p t i j -> p (t i j)"),
                                 eq.rearrange("p t i j -> p (t i j)"), ALU.add))
    link(nc.vector.tensor_reduce(rank, gt.rearrange("p t i j -> p (t i) j"), AX.X, ALU.add))


def route_groups(net, tag, rwT):
    nc, d = net.nc, net.dram
    E, G, K = 64, 8, 8
    with ExitStack() as mem, stage(nc, "w_in logits sig chain rw_ready turned ones_set") as (
            block, w_in, logits, sig, chain, rw_ready, turned, ones_set):
        w = net.sb(tag + "_gw", [P, KC, E], ctx=mem)
        gb = net.sb(tag + "_gb", [P, E], ctx=mem)
        tri = net.sb(tag + "_tri", [P, G, G], ctx=mem)
        score = net.sb(tag + "_score", [P, TILES, E], ctx=mem)
        choice = net.sb(tag + "_choice", [P, TILES, E], ctx=mem)
        top = net.sb(tag + "_top", [P, TILES, G, 8], ctx=mem)
        gs = net.sb(tag + "_gs", [P, TILES, G], ctx=mem)
        gt = net.sb(tag + "_gt", [P, TILES, G, G], ctx=mem)
        eq = net.sb(tag + "_eq", [P, TILES, G, G], ctx=mem)
        rank = net.sb(tag + "_rank", [P, TILES, G], ctx=mem)
        best = net.sb(tag + "_best", [P, TILES, K], ctx=mem)
        left = net.sb(tag + "_left", [P, TILES, E], ctx=mem)
        tot = net.sb(tag + "_tot", [P, TILES], ctx=mem)

        @block.sync
        def _(sp):
            sp.dma_start(w[:], d["gate_wT"].rearrange("(c p) n -> p c n", p=P)).then_inc(w_in, 16)
            sp.dma_start(gb[:], spread(d["gate_bias"], (P, E))).then_inc(w_in, 16)
            sp.dma_start(tri[:], spread(d["tri8"].unsqueeze(0), (P, G, G))).then_inc(w_in, 16)

        @block.tensor
        def _(pe):
            pe.wait_ge(w_in, 48)
            for t in range(TILES):
                for k in range(KC):
                    last = nc.tensor.matmul(net.bank(0)[:, t * E:(t + 1) * E], net.xnT[:, k, t * P:(t + 1) * P], w[:, k],
                                            start=(k == 0), stop=(k == KC - 1))
            last.then_inc(logits, 1)
            pe.wait_ge(rw_ready, 1)
            for t in range(TILES):
                last = nc.tensor.transpose(net.bank(1 + t // 4)[0:E, (t % 4) * P:(t % 4 + 1) * P], score[:, t],
                                           net.ident[:])
            last.then_inc(turned, 1)

        @block.scalar
        def _(act):
            act.wait_ge(logits, 1)
            nc.scalar.activation(score[:].rearrange("p t e -> p (t e)"), net.bank(0), ACT.Sigmoid).then_inc(sig, 1)

        @block.vector
        def _(dve):
            done = [0]

            def link(ins):
                done[0] += 1
                ins.then_inc(chain, 1)
                dve.wait_ge(chain, done[0])

            nc.vector.memset(rwT[:], 0.0).then_inc(ones_set, 1)
            dve.wait_ge(ones_set, 1)
            nc.vector.memset(rwT[E:E + 1, :], 1.0).then_inc(ones_set, 1)
            dve.wait_ge(w_in, 48)
            dve.wait_ge(sig, 1)
            link(nc.vector.tensor_tensor(choice[:], score[:], spread(gb[:].unsqueeze(1), (P, TILES, E)), ALU.add))
            for t in range(TILES):
                for g in range(G):
                    ins = nc.vector.max(top[:, t, g], choice[:, t, g * 8:(g + 1) * 8])
            link(ins)
            link(nc.vector.tensor_tensor(gs[:], top[:, :, :, 0], top[:, :, :, 1], ALU.add))
            rank_below(nc, dve, link, gt[:], eq[:], gs, tri[:], rank[:].rearrange("p t g -> p (t g)"), G)
            link(nc.vector.tensor_scalar(gs[:], rank[:], 4.0, None, ALU.is_lt))
            link(nc.vector.tensor_tensor(choice[:].rearrange("p t (g e) -> p (t g) e", g=G),
                                         choice[:].rearrange("p t (g e) -> p (t g) e", g=G),
                                         spread(gs[:].rearrange("p t g -> p (t g)").unsqueeze(2), (P, TILES * G, 8)),
                                         ALU.mult))
            for t in range(TILES):
                ins = nc.vector.max(best[:, t], choice[:, t])
            link(ins)
            for t in range(TILES):
                ins = nc.vector.match_replace(left[:, t], best[:, t], choice[:, t], -3e38)
            link(ins)
            link(nc.vector.tensor_scalar(left[:], left[:], -3e38, None, ALU.is_equal))
            link(nc.vector.tensor_tensor(score[:], score[:], left[:], ALU.mult))
            link(nc.vector.tensor_reduce(tot[:], score[:], AX.X, ALU.add))
            link(nc.vector.tensor_scalar(tot[:], tot[:], 1e-20, None, ALU.add))
            link(nc.vector.reciprocal(tot[:], tot[:]))
            link(nc.vector.tensor_tensor(score[:], score[:], spread(tot[:].unsqueeze(2), (P, TILES, E)), ALU.mult))
            nc.vector.tensor_scalar(score[:], score[:], 2.5, None, ALU.mult).then_inc(rw_ready, 1)
            dve.wait_ge(turned, 1)
            for h in range(2):
                nc.vector.tensor_copy(rwT[0:E, h * HALF:(h + 1) * HALF], net.bank(1 + h)[0:E, :]).then_inc(ones_set, 1)
            dve.wait_ge(ones_set, 4)


def route_top1(net, tag, rwT):
    nc, d = net.nc, net.dram
    E = 14
    with ExitStack() as mem, stage(nc, "w_in logits ex shifted chain rw_ready turned out_ready") as (
            block, w_in, logits, ex, shifted, chain, rw_ready, turned, out_ready):
        w = net.sb(tag + "_gw", [P, KC, E], ctx=mem)
        tri = net.sb(tag + "_tri", [P, E, E], ctx=mem)
        lg = net.sb(tag + "_lg", [P, TILES, E], ctx=mem)
        pr = net.sb(tag + "_pr", [P, TILES, E], ctx=mem)
        gt = net.sb(tag + "_gt", [P, TILES, E, E], ctx=mem)
        eq = net.sb(tag + "_eq", [P, TILES, E, E], ctx=mem)
        rank = net.sb(tag + "_rank", [P, TILES, E], ctx=mem)
        tot = net.sb(tag + "_tot", [P, TILES], ctx=mem)

        @block.sync
        def _(sp):
            sp.dma_start(w[:], d["router_w"].rearrange("(c p) n -> p c n", p=P)).then_inc(w_in, 16)
            sp.dma_start(tri[:], spread(d["tri14"].unsqueeze(0), (P, E, E))).then_inc(w_in, 16)

        @block.tensor
        def _(pe):
            pe.wait_ge(w_in, 32)
            for t in range(TILES):
                for k in range(KC):
                    last = nc.tensor.matmul(net.bank(0)[:, t * E:(t + 1) * E], net.xnT[:, k, t * P:(t + 1) * P], w[:, k],
                                            start=(k == 0), stop=(k == KC - 1))
            last.then_inc(logits, 1)
            pe.wait_ge(rw_ready, 1)
            for t in range(TILES):
                last = nc.tensor.transpose(net.bank(1 + t // 4)[0:E, (t % 4) * P:(t % 4 + 1) * P], pr[:, t],
                                           net.ident[:])
            last.then_inc(turned, 1)

        @block.scalar
        def _(act):
            act.wait_ge(shifted, 1)
            nc.scalar.activation(pr[:], pr[:], ACT.Exp).then_inc(ex, 1)

        @block.vector
        def _(dve):
            done = [0]

            def link(ins):
                done[0] += 1
                ins.then_inc(chain, 1)
                dve.wait_ge(chain, done[0])

            link(nc.vector.memset(rwT[:], 0.0))
            dve.wait_ge(w_in, 32)
            dve.wait_ge(logits, 1)
            link(nc.vector.tensor_copy(lg[:].rearrange("p t e -> p (t e)"), net.bank(0)[:, 0:TILES * E]))
            link(nc.vector.tensor_reduce(tot[:], lg[:], AX.X, ALU.max))
            nc.vector.tensor_tensor(pr[:], lg[:], spread(tot[:].unsqueeze(2), (P, TILES, E)),
                                    ALU.subtract).then_inc(shifted, 1)
            rank_below(nc, dve, link, gt[:], eq[:], lg, tri[:], rank[:].rearrange("p t g -> p (t g)"), E)
            link(nc.vector.tensor_scalar(rank[:], rank[:], 0.5, None, ALU.is_lt))
            dve.wait_ge(ex, 1)
            link(nc.vector.tensor_reduce(tot[:], pr[:], AX.X, ALU.add))
            link(nc.vector.reciprocal(tot[:], tot[:]))
            link(nc.vector.tensor_tensor(pr[:], pr[:], rank[:], ALU.mult))
            nc.vector.tensor_tensor(pr[:], pr[:], spread(tot[:].unsqueeze(2), (P, TILES, E)),
                                    ALU.mult).then_inc(rw_ready, 1)
            dve.wait_ge(turned, 1)
            for h in range(2):
                nc.vector.tensor_copy(rwT[0:E, h * HALF:(h + 1) * HALF], net.bank(1 + h)[0:E, :]).then_inc(out_ready, 1)
            dve.wait_ge(out_ready, 2)


def experts(net, tag, packed, tiles, rows, rwT, b2, gated):
    nc, d = net.nc, net.dram
    KINDS = 3 if gated else 2
    UNITS = 4
    WIDTH = d[packed].shape[2]
    o_u = 2 * P if gated else 0
    o_d = o_u + 2 * P
    o_s = o_d + D
    names = ("w_in0 w_in1 b2_in x_hi x_lo w_hi w_lo ring_full act_done up_done h_ready h_hi h_lo down_done out_ready "
             "turned added")
    with ExitStack() as mem, stage(nc, names) as (
            block, w_in0, w_in1, b2_in, x_hi, x_lo, w_hi, w_lo, ring_full, act_done, up_done, h_ready, h_hi, h_lo,
            down_done, out_ready, turned, added):
        w_in = (w_in0, w_in1)
        w = net.sb(tag + "_w", [P, 2, WIDTH], ctx=mem)
        wh = net.sb(tag + "_wh", [P, 2, o_s + P], F32R, ctx=mem)
        wl = net.sb(tag + "_wl", [P, 2, o_s], F32R, ctx=mem)
        xh = net.sb(tag + "_xh", [P, KC, TOK], F32R, ctx=mem)
        xl = net.sb(tag + "_xl", [P, KC, TOK], F32R, ctx=mem)
        rh = net.sb(tag + "_rh", [P, TOK], F32R, ctx=mem)
        rl = net.sb(tag + "_rl", [P, TOK], F32R, ctx=mem)
        b2s = net.sb(tag + "_b2", [P, D], ctx=mem)
        g = net.sb(tag + "_g", [P, 2, HALF], ctx=mem)
        gu = net.sb(tag + "_gu", [P, 2, HALF], ctx=mem)
        h = net.sb(tag + "_h", [P, 2, HALF], ctx=mem)
        hh = net.sb(tag + "_hh", [P, 2, HALF], F32R, ctx=mem)
        hl = net.sb(tag + "_hl", [P, 2, HALF], F32R, ctx=mem)
        out_sb = net.sb(tag + "_out", [P, KC, TOK], ctx=mem)
        ring = [net.bank(j) for j in range(4)]
        acc = [[net.bank(4 + 2 * c + half) for half in range(2)] for c in range(KC)]

        def pairs(eng, one):
            one(0, True, False)
            with eng.Fori(1, tiles // 2 - 1) as i:
                one(i, False, False)
            one(tiles // 2 - 1, False, True)

        @block.sync
        def _(sp):
            for u in range(2):
                sp.dma_start(w[:, u], d[packed][u]).then_inc(w_in[u], 16)
            sp.dma_start(b2s[0:rows, :], d[b2]).then_inc(b2_in, 16)
            with sp.Fori(0, tiles // 2 - 1) as i:
                for u in range(2):
                    tile = 2 * i + u
                    sp.wait_ge(w_lo, tile + 1)
                    sp.wait_ge(act_done, 2 * tile + 4)
                    sp.dma_start(w[:, u], d[packed][bass.ds(tile + 2, 1)].rearrange("o p n -> p (o n)")).then_inc(w_in[u], 16)

        @block.tensor
        def _(pe):
            def split_product(out, u, at, right, start, stop):
                for n, (a, b) in enumerate(((wh, 0), (wl, 0), (wh, 1))):
                    last = nc.tensor.matmul(out, a[:, u, at:at + P], right[b], start=start and n == 0,
                                            stop=stop and n == 2, skip_group_check=not start and not stop)
                return last

            def down(i, n):
                u, half = n // 2 % 2, n % 2
                pe.wait_ge(h_lo, UNITS * i + n + 3)
                for c in range(KC):
                    last = split_product(acc[c][half], u, o_d + c * P, (hh[:, n % 2], hl[:, n % 2]), False, False)
                last.then_inc(down_done, 1)

            def one(i, first, last_pair):
                for n in range(UNITS):
                    u, half = n // 2, n % 2
                    if half == 0:
                        pe.wait_ge(w_lo, 2 * i + u + 1)
                    tok = slice(half * HALF, (half + 1) * HALF)
                    for j in range(KINDS):
                        q = KINDS * n + j
                        unit = UNITS * i + n
                        if not gated:
                            pe.wait_ge((act_done, h_ready)[j], unit + 1)
                        elif j == 0:
                            pe.wait_ge(h_ready, unit + 1)
                        else:
                            pe.wait_ge((act_done, up_done)[j - 1], unit + 2)
                        if j < KINDS - 1:
                            for k in range(KC):
                                last = split_product(ring[q % 4], u, (o_u if j else 0) + k * P,
                                                     (xh[:, k, tok], xl[:, k, tok]), k == 0, k == KC - 1)
                        else:
                            for m, r in enumerate((rh, rl)):
                                last = nc.tensor.matmul(ring[q % 4], wh[0:rows, u, o_s:o_s + P], r[0:rows, tok],
                                                        start=(m == 0), stop=(m == 1))
                        last.then_inc(ring_full, 1)
                    if n or not first:
                        down(i, n - 1)
                if last_pair:
                    down(i, UNITS - 1)

            pe.wait_ge(b2_in, 16)
            for c in range(KC):
                for half in range(2):
                    nc.tensor.matmul(acc[c][half], b2s[0:rows, c * P:(c + 1) * P], rwT[0:rows, half * HALF:(half + 1) * HALF],
                                     start=True, stop=False, skip_group_check=True)
            pe.wait_ge(x_lo, 2)
            pairs(pe, one)
            pe.wait_ge(out_ready, 4)
            for t in range(TILES):
                for c in range(KC):
                    last = nc.tensor.transpose(net.ps[t // 4][:, (t % 4) * D + c * P:(t % 4) * D + (c + 1) * P],
                                               out_sb[:, c, t * P:(t + 1) * P], net.ident[:])
                if t % 4 == 3:
                    last.then_inc(turned, 1)

        @block.vector
        def _(dve):
            for sem in (act_done, up_done, h_ready, h_lo, down_done):
                dve.sem_inc(sem, 2)

            def split_low(tile, u):
                dve.wait_ge(w_hi, tile + 1)
                nc.vector.tensor_tensor(wl[:, u], w[:, u, 0:o_s], wh[:, u, 0:o_s], ALU.subtract).then_inc(w_lo, 1)

            def one(i, first, last_pair):
                for n in range(UNITS):
                    unit = UNITS * i + n
                    src = g
                    dve.wait_ge(act_done, unit + 3)
                    if gated:
                        q = KINDS * n + 1
                        dve.wait_ge(ring_full, UNITS * KINDS * i + q + 1)
                        nc.vector.tensor_tensor(gu[:, n % 2], g[:, n % 2], ring[q % 4], ALU.mult).then_inc(up_done, 1)
                        dve.wait_ge(up_done, unit + 3)
                        src = gu
                    q = KINDS * n + KINDS - 1
                    dve.wait_ge(ring_full, UNITS * KINDS * i + q + 1)
                    nc.vector.tensor_tensor(h[:, n % 2], src[:, n % 2], ring[q % 4], ALU.mult).then_inc(h_ready, 1)
                    dve.wait_ge(h_hi, unit + 1)
                    nc.vector.tensor_tensor(hl[:, n % 2], h[:, n % 2], hh[:, n % 2], ALU.subtract).then_inc(h_lo, 1)
                    if n % 2 == 0 and not (last_pair and n == 2):
                        split_low(2 * i + n // 2 + 1, 1 - n // 2)

            dve.wait_ge(x_hi, 2)
            nc.vector.tensor_tensor(xl[:], net.xnT[:], xh[:], ALU.subtract).then_inc(x_lo, 1)
            nc.vector.tensor_tensor(rl[:], rwT[:], rh[:], ALU.subtract).then_inc(x_lo, 1)
            split_low(0, 0)
            pairs(dve, one)
            dve.wait_ge(down_done, 2 + 2 * tiles)
            nc.vector.tensor_copy(out_sb[:, 1, 0:HALF], acc[1][0]).then_inc(out_ready, 1)
            nc.vector.tensor_copy(out_sb[:, 1, HALF:TOK], acc[1][1]).then_inc(out_ready, 1)
            for part in range(2):
                dve.wait_ge(turned, part + 1)
                nc.vector.tensor_tensor(net.x[:, 4 * part:4 * part + 4, :], net.x[:, 4 * part:4 * part + 4, :],
                                        net.ps[part][:].rearrange("p (t f) -> p t f", f=D), ALU.add).then_inc(added, 1)
            dve.wait_ge(added, 2)

        @block.scalar
        def _(act):
            def split_high(tile, u, wait):
                act.wait_ge(w_in[u], wait)
                nc.scalar.activation(wh[:, u], w[:, u, 0:o_s + P], ACT.Copy).then_inc(w_hi, 1)

            def one(i, first, last_pair):
                for n in range(UNITS):
                    q = KINDS * n
                    unit = UNITS * i + n
                    act.wait_ge(ring_full, UNITS * KINDS * i + q + 1)
                    act.wait_ge(h_ready, unit + 1)
                    if gated:
                        ins = nc.scalar.activation(g[:, n % 2], ring[q % 4], ACT.Silu)
                    else:
                        ins = nc.scalar.activation(g[:, n % 2], ring[q % 4], ACT.Gelu, bias=w[:, n // 2, o_s + P:o_s + P + 1])
                    ins.then_inc(act_done, 1)
                    act.wait_ge(h_ready, unit + 3)
                    act.wait_ge(down_done, unit + 1)
                    nc.scalar.activation(hh[:, n % 2], h[:, n % 2], ACT.Copy).then_inc(h_hi, 1)
                    if n % 2 == 0 and not (last_pair and n == 2):
                        act.wait_ge(down_done, unit + 2)
                        split_high(2 * i + n // 2 + 1, 1 - n // 2, 16 * i + 16 * (1 + n // 2))

            nc.scalar.activation(xh[:], net.xnT[:], ACT.Copy).then_inc(x_hi, 1)
            nc.scalar.activation(rh[:], rwT[:], ACT.Copy).then_inc(x_hi, 1)
            split_high(0, 0, 16)
            pairs(act, one)
            act.wait_ge(down_done, 2 + 2 * tiles)
            for half in range(2):
                nc.scalar.activation(out_sb[:, 0, half * HALF:(half + 1) * HALF], acc[0][half], ACT.Copy).then_inc(out_ready, 1)


def hidden_tiles(net, pe, made, taken, product):
    for n in range(16):
        if n >= 8:
            pe.wait_ge(taken, n - 7)
        product(n // 2, slice((n % 2) * HALF, (n % 2 + 1) * HALF), net.bank(n % 8)).then_inc(made, 1)


def ternary(net, tag, name, tiles, cols, out):
    nc, d = net.nc, net.dram
    MAGIC = 12582912.0
    with ExitStack() as mem, stage(nc, "w_in chain ready turned taken") as (block, w_in, chain, ready, turned, taken):
        w = net.sb(tag + "_raw", [P, tiles, cols], ctx=mem)
        q = net.sb(tag + "_q", [P, tiles, cols], ctx=mem)
        sc = net.sb(tag + "_sc", [P, tiles], ctx=mem)
        rs = net.sb(tag + "_rs", [P, tiles], ctx=mem)

        @block.sync
        def _(sp):
            sp.dma_start(w[:], d[name].rearrange("(t p) n -> p t n", p=P)).then_inc(w_in, 16)

        @block.vector
        def _(dve):
            done = [0]

            def link(ins):
                done[0] += 1
                ins.then_inc(chain, 1)
                dve.wait_ge(chain, done[0])

            dve.wait_ge(w_in, 16)
            link(nc.vector.tensor_reduce(sc[:], w[:], AX.X, ALU.add, apply_absolute_value=True))
            link(nc.vector.tensor_scalar(sc[:], sc[:], 1.0 / cols, 1e-5, ALU.mult, ALU.max))
            link(nc.vector.reciprocal(rs[:], sc[:]))
            for t in range(tiles):
                ins = nc.vector.tensor_scalar(q[:, t], w[:, t], rs[:, t:t + 1], 2.0, ALU.mult, ALU.min)
            link(ins)
            link(nc.vector.tensor_scalar(q[:], q[:], -2.0, MAGIC, ALU.max, ALU.add))
            link(nc.vector.tensor_scalar(q[:], q[:], -MAGIC, 1.0, ALU.add, ALU.min))
            link(nc.vector.scalar_tensor_tensor(q[:], q[:], -1.0, w[:], ALU.max, ALU.subtract))
            link(nc.vector.tensor_tensor(q[:], q[:], w[:], ALU.add))
            for t in range(tiles):
                nc.vector.tensor_scalar(q[:, t], q[:, t], sc[:, t:t + 1], None, ALU.mult).then_inc(ready, 1)

        @block.tensor
        def _(pe):
            for c in range(cols // P):
                for h in range(0, tiles, 4):
                    n = c * -(-tiles // 4) + h // 4
                    pe.wait_ge(ready, min(h + 4, tiles))
                    if n >= 8:
                        pe.wait_ge(taken, n - 7)
                    for t in range(h, min(h + 4, tiles)):
                        last = nc.tensor.transpose(net.bank(n % 8)[:, (t - h) * P:(t - h + 1) * P],
                                                   q[:, t, c * P:(c + 1) * P], net.ident[:])
                    last.then_inc(turned, 1)

        @block.scalar
        def _(act):
            for c in range(cols // P):
                for h in range(0, tiles, 4):
                    n = c * -(-tiles // 4) + h // 4
                    z = min(h + 4, tiles)
                    act.wait_ge(turned, n + 1)
                    nc.scalar.activation(out[:, c, h * P:z * P], net.bank(n % 8)[:, 0:(z - h) * P], ACT.Copy).then_inc(taken, 1)


def bit_hidden(net, tag, wfcT):
    nc, d = net.nc, net.dram
    R = 16
    with ExitStack() as mem, stage(nc, "w_in low low_taken made relu_done squared") as (
            block, w_in, low, low_taken, made, relu_done, squared):
        vT = net.sb(tag + "_v", [P, KC, R], ctx=mem)
        fbT = net.sb(tag + "_fb", [R, R], ctx=mem)
        uT = net.sb(tag + "_u", [R, 1024], ctx=mem)
        gate = net.sb(tag + "_gate", [R, 1], ctx=mem)
        t1 = net.sb(tag + "_t1", [R, TOK], ctx=mem)
        t2 = net.sb(tag + "_t2", [R, TOK], ctx=mem)
        r = net.sb(tag + "_r", [P, 2, HALF], ctx=mem)

        @block.sync
        def _(sp):
            sp.dma_start(vT[:], d["L1_ffn_vT"].rearrange("(c p) n -> p c n", p=P)).then_inc(w_in, 16)
            sp.dma_start(fbT[:], d["L1_ffn_fbT"]).then_inc(w_in, 16)
            sp.dma_start(uT[:], d["L1_ffn_uT"]).then_inc(w_in, 16)
            sp.dma_start(gate[:], spread(d["L1_ffn_gate"], (R, 1))).then_inc(w_in, 16)

        @block.tensor
        def _(pe):
            pe.wait_ge(w_in, 64)
            for h in range(2):
                for k in range(KC):
                    last = nc.tensor.matmul(net.bank(h)[0:R, :], vT[:, k], net.xnT[:, k, h * HALF:(h + 1) * HALF],
                                            start=(k == 0), stop=(k == KC - 1))
                last.then_inc(low, 1)
            for h in range(2):
                pe.wait_ge(low_taken, h + 1)
                nc.tensor.matmul(net.bank(2 + h)[0:R, :], fbT[:], t1[:, h * HALF:(h + 1) * HALF], start=True,
                                 stop=True).then_inc(low, 1)
            pe.wait_ge(low_taken, 4)

            def product(c, tok, bank):
                for k in range(KC):
                    nc.tensor.matmul(bank, wfcT[:, k, c * P:(c + 1) * P], net.xnT[:, k, tok], start=(k == 0), stop=False)
                return nc.tensor.matmul(bank, uT[:, c * P:(c + 1) * P], t2[:, tok], start=False, stop=True)
            hidden_tiles(net, pe, made, relu_done, product)

        @block.scalar
        def _(act):
            for n in range(16):
                act.wait_ge(made, n + 1)
                if n >= 2:
                    act.wait_ge(squared, n - 1)
                nc.scalar.activation(r[:, n % 2], net.bank(n % 8), ACT.Relu).then_inc(relu_done, 1)

        @block.vector
        def _(dve):
            for h in range(2):
                dve.wait_ge(low, h + 1)
                nc.vector.tensor_copy(t1[:, h * HALF:(h + 1) * HALF], net.bank(h)[0:R, :]).then_inc(low_taken, 1)
            dve.wait_ge(w_in, 64)
            for h in range(2):
                dve.wait_ge(low, h + 3)
                nc.vector.tensor_scalar(t2[:, h * HALF:(h + 1) * HALF], net.bank(2 + h)[0:R, :], gate[:, 0:1], None,
                                        ALU.mult).then_inc(low_taken, 1)
            for n in range(16):
                dve.wait_ge(relu_done, n + 1)
                nc.vector.tensor_tensor(net.actT[:, n // 2, (n % 2) * HALF:(n % 2 + 1) * HALF], r[:, n % 2], r[:, n % 2],
                                        ALU.mult).then_inc(squared, 1)


def scan_mixer(net, tag, y):
    nc, d = net.nc, net.dram
    names = "w_in made taken chain pchain u_ready p_ready out_ready turned y_taken"
    with ExitStack() as mem, stage(nc, names) as (
            block, w_in, made, taken, chain, pchain, u_ready, p_ready, out_ready, turned, y_taken):
        w = net.sb(tag + "_w", [P, KC, 6 * P], ctx=mem)
        bcols = net.sb(tag + "_b", [P, 6], ctx=mem)
        lb = net.sb(tag + "_lb", [P, 2], ctx=mem)
        olb = net.sb(tag + "_olb", [P, 2], ctx=mem)
        lam = net.sb(tag + "_lam", [P, 2, TOK], ctx=mem)
        oml = net.sb(tag + "_oml", [P, 2, TOK], ctx=mem)
        u = net.sb(tag + "_u", [P, 2, 2, TOK], ctx=mem)
        fwd = net.sb(tag + "_f", [P, 2, 2, TOK], ctx=mem)
        rev = net.sb(tag + "_r", [P, 2, 2, TOK], ctx=mem)
        tmp = net.sb(tag + "_t", [P, 2, 2, 2, S], ctx=mem)
        inp, og, fg = net.actT[:, 0:2], net.actT[:, 2:4], net.actT[:, 4:6]

        def at(buf, n):
            return buf[:, :, :, bass.ds(n * S, S)]

        def lam_at(n):
            return spread(lam[:, :, bass.ds(n * S, S)].unsqueeze(2), (P, 2, 2, S))

        @block.sync
        def _(sp):
            sp.dma_start(w[:], d["L2_attn_W_in"].rearrange("(c p) n -> p c n", p=P)).then_inc(w_in, 16)
            sp.dma_start(bcols[:], d["L2_attn_b_in"]).then_inc(w_in, 16)
            sp.dma_start(lb[:], d["L2_attn_lb"]).then_inc(w_in, 16)

        @block.tensor
        def _(pe):
            pe.wait_ge(w_in, 48)
            for n in range(12):
                if n >= 8:
                    pe.wait_ge(taken, n - 7)
                c, tok = n // 2, slice((n % 2) * HALF, (n % 2 + 1) * HALF)
                for k in range(KC):
                    last = nc.tensor.matmul(net.bank(n % 8), w[:, k, c * P:(c + 1) * P], net.xnT[:, k, tok],
                                            start=(k == 0), stop=(k == KC - 1))
                last.then_inc(made, 1)
            pe.wait_ge(out_ready, 2)
            pe.wait_ge(taken, 12)
            for t in range(TILES):
                for e in range(2):
                    last = nc.tensor.transpose(net.bank(t)[:, e * P:(e + 1) * P], oml[:, e, t * P:(t + 1) * P], net.ident[:])
                last.then_inc(turned, 1)

        @block.scalar
        def _(act):
            act.wait_ge(w_in, 48)
            for n in range(12):
                c, tok = n // 2, slice((n % 2) * HALF, (n % 2 + 1) * HALF)
                act.wait_ge(made, n + 1)
                nc.scalar.activation(net.actT[:, c, tok], net.bank(n % 8), ACT.Silu if c < 2 else ACT.Sigmoid,
                                     bias=bcols[:, c:c + 1]).then_inc(taken, 1)
            for t in range(TILES):
                act.wait_ge(turned, t + 1)
                nc.scalar.activation(y[:, t, :], net.bank(t)[:, 0:D], ACT.Copy).then_inc(y_taken, 1)

        @block.vector
        def _(dve):
            done = [0]

            def link(ins):
                done[0] += 1
                ins.then_inc(chain, 1)
                dve.wait_ge(chain, done[0])

            dve.wait_ge(w_in, 48)
            link(nc.vector.tensor_scalar(olb[:], lb[:], -1.0, 1.0, ALU.mult, ALU.add))
            dve.wait_ge(taken, 12)
            for e in range(2):
                ins = nc.vector.tensor_scalar(lam[:, e], fg[:, e], olb[:, e:e + 1], lb[:, e:e + 1], ALU.mult, ALU.add)
            link(ins)
            link(nc.vector.tensor_scalar(oml[:], lam[:], -1.0, 1.0, ALU.mult, ALU.add))
            for a in range(2):
                for e in range(2):
                    ins = nc.vector.tensor_tensor(u[:, a, e], oml[:, a], inp[:, e], ALU.mult)
            ins.then_inc(u_ready, 1)
            dve.wait_ge(u_ready, 1)
            link(nc.vector.tensor_copy(fwd[:, :, :, 0:S], u[:, :, :, 0:S]))
            base = done[0]
            with dve.Fori(1, B) as n:
                nc.vector.tensor_tensor(tmp[:, 0], lam_at(n), at(fwd, n - 1), ALU.mult).then_inc(chain, 1)
                dve.wait_ge(chain, base + 2 * n - 1)
                nc.vector.tensor_tensor(at(fwd, n), tmp[:, 0], at(u, n), ALU.add).then_inc(chain, 1)
                dve.wait_ge(chain, base + 2 * n)
            done[0] = base + 2 * (B - 1)
            dve.wait_ge(p_ready, 1)
            link(nc.vector.tensor_tensor(fwd[:], fwd[:], rev[:], ALU.add))
            for a in range(2):
                for e in range(2):
                    ins = nc.vector.tensor_tensor(u[:, a, e], fwd[:, a, e], og[:, a], ALU.mult)
            link(ins)
            for e in range(2):
                nc.vector.tensor_tensor(oml[:, e], u[:, 0, e], u[:, 1, e], ALU.add).then_inc(out_ready, 1)

        @block.gpsimd
        def _(pool):
            pool.wait_ge(u_ready, 1)
            nc.gpsimd.tensor_copy(rev[:, :, :, (B - 1) * S:], u[:, :, :, (B - 1) * S:]).then_inc(pchain, 1)
            pool.wait_ge(pchain, 1)
            with pool.Fori(0, B - 1) as i:
                n = B - 2 - i
                nc.gpsimd.tensor_tensor(tmp[:, 1], lam_at(n), at(rev, n + 1), ALU.mult).then_inc(pchain, 1)
                pool.wait_ge(pchain, 2 * i + 2)
                nc.gpsimd.tensor_tensor(at(rev, n), tmp[:, 1], at(u, n), ALU.add).then_inc(pchain, 1)
                pool.wait_ge(pchain, 2 * i + 3)
            pool.sem_inc(p_ready, 1)


def lora_hidden(net, tag, gm, e2):
    nc, d = net.nc, net.dram
    names = "w_in chain picked ev_made ev_taken e_ready c_made c_taken made taken g_made g_taken"
    R = 64
    with ExitStack() as mem, stage(nc, names) as (
            block, w_in, chain, picked, ev_made, ev_taken, e_ready, c_made, c_taken, made, taken, g_made, g_taken):
        w = net.sb(tag + "_w", [P, KC, 1024], ctx=mem)
        b1 = net.sb(tag + "_b1", [P, 8], ctx=mem)
        scale = net.sb(tag + "_scale", [R, 1], ctx=mem)
        own = net.sb(tag + "_own", [R, TOK], ctx=mem)
        m4 = net.sb(tag + "_m4", [R, 4], ctx=mem)
        pick = net.sb(tag + "_pick", [P, 4, KC, R], ctx=mem)
        ev = net.sb(tag + "_ev", [R, 2, D], ctx=mem)
        e1 = net.sb(tag + "_e1", [R, 4, D], ctx=mem)
        c1 = net.sb(tag + "_c1", [R, TOK], ctx=mem)
        FIRST = (1, 2, 9, 10)

        @block.sync
        def _(sp):
            sp.dma_start(w[:], d["L3_ffn_W1T"].rearrange("(c p) n -> p c n", p=P)).then_inc(w_in, 16)
            sp.dma_start(b1[:], d["L3_ffn_b1"]).then_inc(w_in, 16)
            sp.dma_start(scale[:], spread(d["L3_ffn_scale"], (R, 1))).then_inc(w_in, 16)
            sp.dma_start(own[:], d["own_batch"]).then_inc(w_in, 16)
            sp.dma_start(m4[:], d["m4"]).then_inc(w_in, 16)

        @block.tensor
        def _(pe):
            pe.wait_ge(picked, 8)
            for n in range(2):
                for c in range(KC):
                    last = nc.tensor.transpose(net.bank(n)[0:R, c * P:(c + 1) * P], pick[:, 2 * n, c], net.ident[:])
                last.then_inc(ev_made, 1)
            for h in range(2):
                for k in range(KC):
                    last = nc.tensor.matmul(net.bank(2 + h)[0:R, :], pick[:, 1, k], net.xnT[:, k, h * HALF:(h + 1) * HALF],
                                            start=(k == 0), stop=(k == KC - 1))
                last.then_inc(c_made, 1)
            pe.wait_ge(w_in, 80)
            pe.wait_ge(c_taken, 2)
            pe.wait_ge(e_ready, 8)

            def product(c, tok, bank):
                for k in range(KC):
                    nc.tensor.matmul(bank, w[:, k, c * P:(c + 1) * P], net.xnT[:, k, tok], start=(k == 0), stop=False)
                flat = e1[:].rearrange("p i d -> p (i d)")
                return nc.tensor.matmul(bank, flat[:, c * P:(c + 1) * P], c1[:, tok], start=False, stop=True)
            hidden_tiles(net, pe, made, taken, product)
            pe.wait_ge(taken, 16)
            for n in range(8):
                r, tok = n // 2, slice((n % 2) * HALF, (n % 2 + 1) * HALF)
                for c in range(KC):
                    last = nc.tensor.matmul(net.bank(n)[0:R, :], pick[:, 3, c], net.actT[:, 2 * r + c, tok],
                                            start=(c == 0), stop=(c == KC - 1))
                last.then_inc(g_made, 1)

        @block.scalar
        def _(act):
            act.wait_ge(w_in, 80)
            for n in range(16):
                act.wait_ge(made, n + 1)
                nc.scalar.activation(net.actT[:, n // 2, (n % 2) * HALF:(n % 2 + 1) * HALF], net.bank(n % 8), ACT.Gelu,
                                     bias=b1[:, n // 2:n // 2 + 1]).then_inc(taken, 1)

        @block.vector
        def _(dve):
            for n, first in enumerate(FIRST):
                for c in range(KC):
                    src = net.xnT[:, c].rearrange("p (b s) -> p b s", s=S)[:, :, first:first + 7:2]
                    nc.vector.tensor_copy(pick[:, n, c].rearrange("p (b i) -> p b i", i=4), src).then_inc(picked, 1)
            for n in range(2):
                dve.wait_ge(ev_made, n + 1)
                nc.vector.tensor_copy(ev[:, n], net.bank(n)[0:R, 0:D]).then_inc(ev_taken, 1)
            dve.wait_ge(w_in, 80)
            dve.wait_ge(ev_taken, 2)
            for i in range(4):
                nc.vector.tensor_scalar(e1[:, i], ev[:, 0], m4[:, i:i + 1], None, ALU.mult).then_inc(e_ready, 1)
                nc.vector.tensor_scalar(e2[:, :, i * S:(i + 1) * S], ev[:, 1].rearrange("p (j r) -> p r j", r=4),
                                        m4[:, i:i + 1], None, ALU.mult).then_inc(e_ready, 1)
            for h in range(2):
                dve.wait_ge(c_made, h + 1)
                tok = slice(h * HALF, (h + 1) * HALF)
                nc.vector.scalar_tensor_tensor(c1[:, tok], net.bank(2 + h)[0:R, :], scale[:, 0:1], own[:, tok], ALU.mult,
                                               ALU.mult).then_inc(c_taken, 1)
            for n in range(8):
                r, tok = n // 2, slice((n % 2) * HALF, (n % 2 + 1) * HALF)
                dve.wait_ge(g_made, n + 1)
                nc.vector.scalar_tensor_tensor(gm[:, r, tok], net.bank(n)[0:R, :], scale[:, 0:1], own[:, tok], ALU.mult,
                                               ALU.mult).then_inc(g_taken, 1)


def heads_reshaped(net, tag, scratch):
    nc, d = net.nc, net.dram
    names = "turned taken stored loaded turned_back taken_back"
    with ExitStack() as mem, stage(nc, names) as (block, turned, taken, stored, loaded, turned_back, taken_back):
        a = net.sb(tag + "_a", [P, TILES, D], ctx=mem)
        r = net.sb(tag + "_r", [P, TILES, D], ctx=mem)

        @block.sync
        def _(sp):
            for t in range(TILES):
                sp.wait_ge(taken, t + 1)
                for e in range(2):
                    sp.dma_start(scratch[2 * t + e].rearrange("h s f -> s h f"),
                                 a[e * S:(e + 1) * S, t, :].rearrange("p (h f) -> p h f", f=16)).then_inc(stored, 16)
            sp.wait_ge(stored, 32 * TILES)
            flat = scratch.rearrange("b h s f -> (b h s f)").rearrange("(t p n) -> p t n", p=P, n=D)
            sp.dma_start(r[:], flat).then_inc(loaded, 16)

        @block.tensor
        def _(pe):
            for t in range(TILES):
                for c in range(KC):
                    last = nc.tensor.transpose(net.bank(t)[:, c * P:(c + 1) * P], net.actT[:, c, t * P:(t + 1) * P],
                                               net.ident[:])
                last.then_inc(turned, 1)
            pe.wait_ge(loaded, 16)
            pe.wait_ge(taken, TILES)
            for t in range(TILES):
                for c in range(KC):
                    last = nc.tensor.transpose(net.bank(t)[:, c * P:(c + 1) * P], r[:, t, c * P:(c + 1) * P], net.ident[:])
                last.then_inc(turned_back, 1)

        @block.scalar
        def _(act):
            for t in range(TILES):
                act.wait_ge(turned, t + 1)
                nc.scalar.activation(a[:, t, :], net.bank(t)[:, 0:D], ACT.Copy).then_inc(taken, 1)
            for t in range(TILES):
                act.wait_ge(turned_back, t + 1)
                nc.scalar.activation(net.actT[:, 0:KC, t * P:(t + 1) * P],
                                     net.bank(t)[:, 0:D].rearrange("p (c n) -> p c n", c=KC), ACT.Copy).then_inc(taken_back, 1)


def program(nc, dram, out, only=None):
    with ExitStack() as ctx:
        net = Net(nc, dram, ctx)
        scratch = nc.dram_tensor("heads_scratch", (B, HEADS, S, 16), F32, kind="Internal").ap()
        q_rows = nc.dram_tensor("query_rows", (96, PAIRS, TOK), F32, kind="Internal").ap()
        m_rows = nc.dram_tensor("mask_rows", (B, 2, CTX), F32, kind="Internal").ap()
        load_all(net)

        def xattn(layer, wo, bo, mask=None, scratch=None):
            pre = f"L{layer}_xattn_"
            norm(net, f"nx{layer}", net.x)
            query_stacks(net, f"q{layer}", pre + "Wq", pre + "bq", mask, q_rows, m_rows)
            cross_attention(net, f"x{layer}", pre + "Wk", pre + "bk", pre + "Wv", pre + "bv", q_rows,
                            m_rows if mask else None)
            if scratch is not None:
                heads_reshaped(net, f"xr{layer}", scratch)
            project(net, f"px{layer}", pre + wo, pre + bo)

        xattn(0, "Wo", "bo")
        norm(net, "na0", net.x)
        self_attention(net, "a0", 32, 2, ["L0_q", "L0_qr", "L0_k", "L0_kr", "L0_v"], "alibi")
        project(net, "pa0", "L0_proj", "L0_proj_b")
        norm(net, "nf0", net.x)
        with ExitStack() as mem:
            rwT = net.sb("rw0", [P, TOK], ctx=mem)
            route_groups(net, "r0", rwT)
            experts(net, "e0", "L0_pack", L0_TILES, P, rwT, "L0_b2", True)

        xattn(1, "Wo", "bo", "mask_f32")
        norm(net, "na1", net.x)
        with net.eight_chunks("act_a1"):
            self_attention(net, "a1", 128, 8, ["L1_q", "L1_qr", "L1_k", "L1_kr", "L1_v"], "band")
            project(net, "pa1", "L1_attn_Wo", None, chunks=8)
        norm(net, "nf1", net.x)
        with net.eight_chunks("act_f1"), ExitStack() as mem:
            wfcT = net.sb("wfcT", [P, KC, 1024], ctx=mem)
            wprT = net.sb("wprT", [P, 8, D], ctx=mem)
            ternary(net, "tf", "L1_ffn_w_fc", 8, 256, wfcT)
            ternary(net, "tp", "L1_ffn_w_proj", 2, 1024, wprT)
            bit_hidden(net, "bh", wfcT)
            project(net, "pf1", None, None, chunks=8, w_sb=wprT)

        xattn(2, "Wh", "bh", scratch=scratch)
        norm(net, "na2", net.x)
        with net.eight_chunks("act_mix"), ExitStack() as mem:
            y = net.sb("mix_y", [P, TILES, D], ctx=mem)
            scan_mixer(net, "sm", y)
            norm(net, "ny2", y, "L2_attn_gamma", "L2_attn_beta")
        project(net, "pa2", "L2_attn_W_out", "L2_attn_b_out", src=net.xnT)
        norm(net, "nf2", net.x)
        with ExitStack() as mem:
            rwT = net.sb("rw2", [P, TOK], ctx=mem)
            route_top1(net, "r2", rwT)
            experts(net, "e2", "L2_pack", L2_TILES, P, rwT, "L2_ffn_b2", False)

        xattn(3, "Wo", "bo", "mask_int")
        norm(net, "na3", net.x)
        causal_attention(net, "a3")
        norm(net, "nf3", net.x)
        with net.eight_chunks("act_f3"), ExitStack() as mem:
            gm = net.sb("gm", [64, 4, TOK], ctx=mem)
            e2 = net.sb("e2f", [64, 4, D], ctx=mem)
            lora_hidden(net, "lh", gm, e2)
            project(net, "pf3", "L3_ffn_W2T", "L3_ffn_b2", chunks=8, out=out,
                    extra=lambda t: [(gm[:, r, t * P:(t + 1) * P], e2[:, r, :]) for r in range(4)])


L0_ROWS = 64 * 176 + 352
L0_TILES = 2 * -(-L0_ROWS // (2 * P))
L2_TILES = 14 * 4


def _columns(v, chunks):
    return np.ascontiguousarray(v.reshape(chunks, P).T)


def _rope(head_dim, sections):
    inv = (1.0 / 10000.0 ** (np.arange(0, head_dim, 2, dtype=np.float32) / np.float32(head_dim))).astype(np.float32)
    ang = np.arange(S, dtype=np.float32)[:, None] * inv[None, :]
    j = np.arange(P) % head_dim
    f = ang.T[j % (head_dim // 2)]
    sign = np.where(j < head_dim // 2, -1.0, 1.0).astype(np.float32)[:, None]
    return np.stack([np.cos(f), np.sin(f) * sign], 1).astype(np.float32)


def _rotated(w, head_dim):
    shape = w.shape
    w = w.reshape(shape[0], -1, 2, head_dim // 2)
    return np.ascontiguousarray(w[:, :, ::-1, :].reshape(shape))


def arrange(a):
    f = np.float32
    o = {"x": np.ascontiguousarray(a["x"].reshape(TOK, D))}
    T = lambda m: np.ascontiguousarray(m.T)
    row = lambda v: np.ascontiguousarray(v.reshape(1, -1))
    o["ctxT"] = np.ascontiguousarray(a["ctx_1024"].transpose(0, 2, 1).reshape(B, KC, P, CTX))
    o["mask_f32"] = np.ascontiguousarray(a["mask_Bx1x1xS2_fk0"].reshape(B, CTX))
    o["mask_int"] = np.ascontiguousarray(a["mask_BxS2_ik0"])
    o["ident"] = np.eye(P, dtype=f)
    o["stack2"] = np.concatenate([np.eye(S, dtype=f)] * 2)
    p = np.arange(P)
    o["parity"] = np.stack([(p // 16 % 2 == 0) * 0.25, (p // 16 % 2 == 1) * 0.25, (p < 64) * 0.125, (p >= 64) * 0.125]
                           + [(p // 16 == m) * 0.25 for m in range(8)]
                           + [p // 16 % 2 == 0, p // 16 % 2 == 1], 1).astype(f)
    for l, wo, bo in ((0, "Wo", "bo"), (1, "Wo", "bo"), (2, "Wh", "bh"), (3, "Wo", "bo")):
        pre = f"L{l}_xattn_"
        for w in ("Wq", "Wk", "Wv", wo):
            o[pre + w] = np.ascontiguousarray(a[pre + w]) if l == 1 else T(a[pre + w])
        for v in ("bq", "bk"):
            o[pre + v] = _columns(a[pre + v], KC)
        o[pre + "bv"], o[pre + bo] = row(a[pre + "bv"]), row(a[pre + bo])
    qkv = T(a["L0_attn_qkv_w"])
    o["L0_q"], o["L0_k"], o["L0_v"] = (np.ascontiguousarray(qkv[:, n * D:(n + 1) * D]) for n in range(3))
    o["L0_qr"], o["L0_kr"] = _rotated(o["L0_q"], 16), _rotated(o["L0_k"], 16)
    o["L0_proj"], o["L0_proj_b"] = T(a["L0_attn_proj_w"]), row(a["L0_attn_proj_b"])
    o["slopes"] = np.ascontiguousarray(a["L0_attn_slopes"].reshape(PAIRS, 2).T)
    pos = np.arange(S, dtype=f)
    diff = pos[None, :] - pos[:, None]
    o["a0_dist"] = np.concatenate([np.minimum(diff, 0.0) * 8.0] * 2).astype(f)
    o["a0_rope"] = _rope(16, 2)
    for n, w in (("q", "Wq"), ("k", "Wk"), ("v", "Wv")):
        o["L1_" + n] = np.ascontiguousarray(a["L1_attn_" + w])
    o["L1_qr"], o["L1_kr"] = _rotated(o["L1_q"], 64), _rotated(o["L1_k"], 64)
    o["L1_attn_Wo"] = np.ascontiguousarray(a["L1_attn_Wo"])
    o["a1_dist"] = np.concatenate([np.where(np.abs(diff) <= S // 4, 0.0, NEG)] * 2).astype(f)
    o["a1_rope"] = _rope(64, 2)
    o["gate_wT"], o["gate_bias"] = T(a["L0_ffn_gate_w"]), row(a["L0_ffn_gate_bias"])
    o["tri8"] = np.tril(np.ones((8, 8), f), -1)
    o["tri14"] = np.tril(np.ones((14, 14), f), -1)

    def pack(tiles, ups, down, expert_of, experts, b1):
        rows = tiles * P
        parts = []
        for m in ups:
            m = np.concatenate([m, np.zeros((rows - m.shape[0], D), f)])
            parts.append(m.reshape(tiles, P, KC, P).transpose(0, 3, 2, 1).reshape(tiles, P, KC * P))
        down = np.concatenate([down, np.zeros((rows - down.shape[0], D), f)])
        parts.append(down.reshape(tiles, P, D))
        sel = np.zeros((tiles, P, P), f)
        for r, e in enumerate(expert_of):
            sel[r // P, e, r % P] = 1.0
        parts.append(sel)
        if b1 is not None:
            parts.append(b1.reshape(tiles, P, 1))
        return np.ascontiguousarray(np.concatenate(parts, 2))

    Wg = np.concatenate([a["L0_ffn_Wg"].reshape(-1, D), a["L0_ffn_Sg"]])
    Wu = np.concatenate([a["L0_ffn_Wu"].reshape(-1, D), a["L0_ffn_Su"]])
    Wd = np.concatenate([a["L0_ffn_Wd"].transpose(0, 2, 1).reshape(-1, D), a["L0_ffn_Sd"].T])
    o["L0_pack"] = pack(L0_TILES, [Wg, Wu], Wd, list(np.repeat(np.arange(64), 176)) + [64] * 352, 65, None)
    o["L0_b2"] = np.zeros((P, D), f)
    w1 = a["L2_ffn_w1"].transpose(0, 2, 1).reshape(-1, D)
    o["L2_pack"] = pack(L2_TILES, [w1], a["L2_ffn_w2"].reshape(-1, D), list(np.repeat(np.arange(14), 512)), 14,
                        a["L2_ffn_b1"].reshape(-1))
    o["L2_ffn_b2"] = np.concatenate([a["L2_ffn_b2"], np.zeros((P - 14, D), f)])
    o["router_w"] = np.ascontiguousarray(a["L2_ffn_router_w"])
    o["L1_ffn_w_fc"], o["L1_ffn_w_proj"] = (np.ascontiguousarray(a["L1_ffn_" + n]) for n in ("w_fc", "w_proj"))
    o["L1_ffn_vT"], o["L1_ffn_fbT"], o["L1_ffn_uT"] = T(a["L1_ffn_v"]), T(a["L1_ffn_fast_b"]), T(a["L1_ffn_u"])
    o["L1_ffn_gate"] = a["L1_ffn_gate"].reshape(1, 1)
    split = lambda m: m.reshape(*m.shape[:-1], -1, P, 2)
    o["L2_attn_W_in"] = np.ascontiguousarray(np.moveaxis(split(a["L2_attn_W_in"]), -1, -2).reshape(D, 6 * P))
    o["L2_attn_b_in"] = np.ascontiguousarray(np.moveaxis(split(a["L2_attn_b_in"]), -1, -2).reshape(6, P).T)
    for n, k in (("lower_bound", "lb"), ("gamma", "gamma"), ("beta", "beta")):
        o["L2_attn_" + k] = np.ascontiguousarray(a["L2_attn_" + n].reshape(P, 2))
    o["L2_attn_W_out"] = np.ascontiguousarray(a["L2_attn_W_out"].reshape(P, 2, D).transpose(1, 0, 2).reshape(D, D))
    o["L2_attn_b_out"] = row(a["L2_attn_b_out"])
    for w in ("Wq", "Wk", "Wv"):
        o["L3_attn_" + w] = T(a["L3_attn_" + w])
    o["L3_attn_bq"], o["L3_attn_bk"] = _columns(a["L3_attn_bq"], KC), _columns(a["L3_attn_bk"], KC)
    o["L3_attn_bv"] = row(a["L3_attn_bv"])
    blk, q = p // S, p % S
    o["causal"] = np.where((blk[:, None] == blk[None, :]) & (q[None, :] <= q[:, None]), 0.0, NEG).astype(f)
    o["L3_ffn_W1T"], o["L3_ffn_W2T"] = T(a["L3_ffn_W1"]), T(a["L3_ffn_W2"])
    o["L3_ffn_b1"], o["L3_ffn_b2"] = _columns(a["L3_ffn_b1"], 8), row(a["L3_ffn_b2"])
    o["L3_ffn_scale"] = a["L3_ffn_scale"].reshape(1, 1)
    bi = np.arange(64)
    o["own_batch"] = (bi[:, None] // 4 == np.arange(TOK)[None, :] // S).astype(f)
    o["m4"] = (bi[:, None] % 4 == np.arange(4)[None, :]).astype(f)
    return o


def kernel(**inputs):
    import concourse.bacc as bacc
    from concourse.bass_utils import run_bass_kernel_spmd as run

    nc = bacc.Bacc("TRN2", target_bir_lowering=False, num_devices=1)
    arrays, dram = {}, {}
    for name, v in arrange({k: np.asarray(v) for k, v in inputs.items()}).items():
        arrays["in_" + name] = v
        dram[name] = nc.dram_tensor("in_" + name, v.shape, mybir.dt.from_np(v.dtype), kind="ExternalInput").ap()
    out = nc.dram_tensor("out_x", (TOK, D), F32, kind="ExternalOutput").ap()
    program(nc, dram, out)
    r = run(nc, [arrays], core_ids=[0])
    return r.results[0]["out_x"].reshape(B, S, D)
```
